# Optimizing a Trainium2 kernel written in Bass

```python
import numpy as np
import jax
import jax.numpy as jnp

def _softmax(x, axis=-1):
    return jax.nn.softmax(x, axis=axis)

def _gelu(x):
    return jax.nn.gelu(x, approximate=True)

def _silu(x):
    return jax.nn.silu(x)

def _sigmoid(x):
    return jax.nn.sigmoid(x)

def _layernorm(x, axis=-1, eps=1e-05):
    m = jnp.mean(x, axis=axis, keepdims=True)
    v = jnp.var(x, axis=axis, keepdims=True)
    return (x - m) / jnp.sqrt(v + eps)

def _scatter_add(tgt, idx, src, axis=0):
    return tgt.at[idx].add(src)

def _segment_sum(src, seg, n):
    return jax.ops.segment_sum(src, seg, n)
kernel_name = 'mk_xattn_ffn_d4_seqx_r8_fb5c23'

def setup_inputs(seed: int=0):
    np.random.seed(seed)
    _w = jnp.asarray

    def _rec_inputs():
        import jax
        import jax.numpy as jnp
        _rk = jax.random.key(seed)
        x = -0.0003929 + 0.9999 * jax.random.normal(jax.random.fold_in(_rk, 1), (128, 64, 128), jnp.float32)
        _lenS = 64 - jax.random.randint(jax.random.fold_in(_rk, 7), (128,), 0, max(1, 64 // 4) + 1, jnp.int32)
        _lenS2 = 64 - jax.random.randint(jax.random.fold_in(_rk, 8), (128,), 0, max(1, 64 // 4) + 1, jnp.int32)
        _ctx_1024P = jax.random.normal(jax.random.fold_in(_rk, 11), (128, 16, 128), jnp.float32)
        _ctx_1024c = jax.random.dirichlet(jax.random.fold_in(_rk, 511), 0.3 * jnp.ones((16,), jnp.float32), (128, 64))
        _ctx_1024t = jnp.einsum('bsk,bkd->bsd', _ctx_1024c, _ctx_1024P)
        _ctx_1024t = _ctx_1024t * jax.lax.rsqrt(jnp.mean(jnp.square(_ctx_1024t)) + 1e-12) * 0.953939
        ctx_1024 = 2.81802e-05 + 1.00001 * (_ctx_1024t + 0.3 * jax.random.normal(jax.random.fold_in(_rk, 611), (128, 64, 128), jnp.float32))
        itok_SxS2_0_2016 = jax.random.randint(jax.random.fold_in(_rk, 12), (64, 64), 0, 2017, jnp.int32)
        _validS = jnp.arange(64)[None, :] < _lenS[:, None]
        _validS2 = jnp.arange(64)[None, :] < _lenS2[:, None]
        _causal = jnp.tril(jnp.ones((64, 64), dtype=bool))
        mask_BxS2_ff1 = jnp.where(jnp.ones((128, 64), dtype=bool), 1.0, 0.0).astype(jnp.float32)
        mask_Bx1x1xS2_if1 = jnp.where(jnp.ones((128, 1, 1, 64), dtype=bool), 1, 0).astype(jnp.int32)
        return (x, ctx_1024, itok_SxS2_0_2016, mask_BxS2_ff1, mask_Bx1x1xS2_if1)
    x, ctx_1024, itok_SxS2_0_2016, mask_BxS2_ff1, mask_Bx1x1xS2_if1 = _rec_inputs()

    def _L0_xattn_setup():
        import jax, jax.numpy as jnp
        import numpy as np
        B, S, DIM, NH = (32, 64, 128, 8)
        DH = DIM // NH
        EPS = 1e-06
        LN_EPS = 1e-05

        def _make_hops(n):
            hops = np.zeros((n, n), dtype=np.int64)
            cur = 1
            for i in range(n):
                for j in range(i + 1, n):
                    hops[i, j] = cur
                    hops[j, i] = cur
                    cur += 1
            return (hops, cur)

        def _mlstm_forward(q, k, v, igate_w, igate_b, fgate_w, fgate_b, rpe, ln_w, ln_b, hops):
            Bq, Sq, _ = q.shape
            pos_emb = rpe[hops]
            gate_in = jnp.concatenate([q, k, v], axis=-1)
            ig = gate_in @ igate_w.T + igate_b
            fg = gate_in @ fgate_w.T + fgate_b
            ig = jnp.transpose(ig, (0, 2, 1))
            fg = jnp.transpose(fg, (0, 2, 1))
            qh = q.reshape(Bq, Sq, NH, DH).transpose(0, 2, 1, 3)
            kh = k.reshape(Bq, Sq, NH, DH).transpose(0, 2, 1, 3)
            vh = v.reshape(Bq, Sq, NH, DH).transpose(0, 2, 1, 3)
            log_f = jax.nn.log_sigmoid(fg)
            csum = jnp.cumsum(log_f, axis=-1)
            csum = jnp.concatenate([jnp.zeros((Bq, NH, 1), csum.dtype), csum], axis=-1)
            lfm = csum[:, :, :, None] - csum[:, :, None, :]
            ltr = jnp.tril(jnp.ones((Sq, Sq), dtype=bool))
            log_fg_matrix = jnp.where(ltr, lfm[:, :, 1:, 1:], -jnp.inf)
            log_D = log_fg_matrix + ig[:, :, None, :]
            max_log_D = jnp.max(log_D, axis=-1, keepdims=True)
            D = jnp.exp(log_D - max_log_D)
            k_scaled = kh / np.sqrt(DH).astype(np.float32)
            pe = pos_emb.reshape(Sq, Sq, NH, DH)
            k_hop = jnp.einsum('bhvc,vmhc->bhvm', qh, pe)
            qk = jnp.einsum('bhsd,bhtd->bhst', qh, k_scaled)
            C = (qk + k_hop) * D
            normalizer = jnp.maximum(jnp.abs(jnp.sum(C, axis=-1, keepdims=True)), jnp.exp(-max_log_D))
            Cn = C / (normalizer + EPS)
            h = Cn @ vh
            mu = jnp.mean(h, axis=-1, keepdims=True)
            var = jnp.mean(jnp.square(h - mu), axis=-1, keepdims=True)
            hn = (h - mu) / jnp.sqrt(var + LN_EPS)
            w = (1.0 + ln_w).reshape(NH, DH)
            b = ln_b.reshape(NH, DH)
            hn = hn * w[None, :, None, :] + b[None, :, None, :]
            return hn.transpose(0, 2, 1, 3).reshape(Bq, Sq, DIM)
        key = jax.random.key(seed)
        ks = jax.random.split(key, 8)
        hops_np, curnum = _make_hops(S)
        return {'q': jax.random.normal(ks[0], (B, S, DIM), dtype=jnp.float32), 'k': jax.random.normal(ks[1], (B, S, DIM), dtype=jnp.float32), 'v': jax.random.normal(ks[2], (B, S, DIM), dtype=jnp.float32), 'igate_w': jax.random.normal(ks[3], (NH, 3 * DIM), dtype=jnp.float32) * 0.02, 'igate_b': jax.random.normal(ks[4], (NH,), dtype=jnp.float32) * 0.1, 'fgate_w': jax.random.normal(ks[5], (NH, 3 * DIM), dtype=jnp.float32) * 0.02, 'fgate_b': jnp.linspace(3.0, 6.0, NH, dtype=jnp.float32), 'rpe': jax.random.normal(ks[6], (curnum, DIM), dtype=jnp.float32) * 0.02, 'ln_w': jax.random.normal(ks[7], (DIM,), dtype=jnp.float32) * 0.1, 'ln_b': jnp.zeros((DIM,), dtype=jnp.float32), 'hops': jnp.asarray(hops_np)}
    _L0_xattn_all = _L0_xattn_setup()
    _L0_xattn_in = {k: v for k, v in _L0_xattn_all.items() if k in ('igate_w', 'igate_b', 'fgate_w', 'fgate_b', 'rpe', 'ln_w', 'ln_b')}
    del _L0_xattn_all

    def _L0_ffn_setup():
        import jax, jax.numpy as jnp
        import numpy as np
        from jax import lax
        T, B, I, M, O = (32, 64, 128, 128, 128)

        def _xavier(key, shape):
            fan_out, fan_in = shape
            limit = float(np.sqrt(6.0 / (fan_in + fan_out)))
            return jax.random.uniform(key, shape, jnp.float32, -limit, limit)
        key = jax.random.key(seed)
        ks = jax.random.split(key, 9)
        x = jax.random.normal(ks[0], (T, B, I), jnp.float32)
        return {'x': x, 'wf': _xavier(ks[1], (M, I)), 'uf': _xavier(ks[2], (M, M)), 'bf': jnp.zeros((M,), jnp.float32), 'wi': _xavier(ks[3], (M, I)), 'ui': _xavier(ks[4], (M, M)), 'bi': jnp.zeros((M,), jnp.float32), 'wc': _xavier(ks[5], (M, I)), 'uc': _xavier(ks[6], (M, M)), 'bc': jnp.zeros((M,), jnp.float32), 'wo': _xavier(ks[7], (O, I)), 'uo': _xavier(ks[8], (O, M)), 'bo': jnp.zeros((O,), jnp.float32), 'in_c': jnp.zeros((M,), jnp.float32)}
    _L0_ffn_all = _L0_ffn_setup()
    _L0_ffn_in = {k: v for k, v in _L0_ffn_all.items() if k in ('wf', 'uf', 'bf', 'wi', 'ui', 'bi', 'wc', 'uc', 'bc', 'wo', 'uo', 'bo', 'in_c')}
    del _L0_ffn_all

    def _L1_xattn_setup():
        import jax, jax.numpy as jnp
        import numpy as np
        B, Q, K, D = (4, 1500, 1500, 128)
        H, HD = (16, 64)
        key = jax.random.key(seed)
        ks = jax.random.split(key, 10)
        s = 0.02
        return {'inputs_q': jax.random.normal(ks[0], (B, Q, D), jnp.float32), 'inputs_kv': jax.random.normal(ks[1], (B, K, D), jnp.float32), 'Wq': jax.random.normal(ks[2], (D, H, HD), jnp.float32) * s, 'bq': jnp.zeros((H, HD), jnp.float32), 'Wk': jax.random.normal(ks[3], (D, H, HD), jnp.float32) * s, 'bk': jnp.zeros((H, HD), jnp.float32), 'Wv': jax.random.normal(ks[4], (D, H, HD), jnp.float32) * s, 'bv': jnp.zeros((H, HD), jnp.float32), 'Wo': jax.random.normal(ks[5], (H, HD, D), jnp.float32) * s, 'bo': jnp.zeros((D,), jnp.float32)}
    _L1_xattn_all = _L1_xattn_setup()
    _L1_xattn_in = {k: v for k, v in _L1_xattn_all.items() if k in ('Wq', 'bq', 'Wk', 'bk', 'Wv', 'bv', 'Wo', 'bo')}
    del _L1_xattn_all

    def _L1_ffn_setup():
        import jax, jax.numpy as jnp
        import numpy as np
        B, T, D, E, TOP_K = (4, 512, 128, 8, 2)
        CAPACITY_FACTOR = 1.5
        key = jax.random.key(seed)
        k1, k2, k3 = jax.random.split(key, 3)
        x = jax.random.normal(k1, (B, T, D), dtype=jnp.float32)
        Wr = jax.random.normal(k2, (E, D), dtype=jnp.float32) * 0.02
        We = jax.random.normal(k3, (E, D, D), dtype=jnp.float32) * 0.02
        return {'x': x, 'Wr': Wr, 'We': We}
    _L1_ffn_all = _L1_ffn_setup()
    _L1_ffn_in = {k: v for k, v in _L1_ffn_all.items() if k in ('Wr', 'We')}
    del _L1_ffn_all

    def _L2_xattn_setup():
        import jax, jax.numpy as jnp
        import numpy as np
        D_MODEL = 128
        HEADS = 16
        DEPTH = D_MODEL // HEADS
        B, S = (4, 512)
        EPS_K = 1e-06
        EPS_LN = 1e-06

        def _layernorm(x, g, b):
            m = jnp.mean(x, axis=-1, keepdims=True)
            var = jnp.var(x, axis=-1, keepdims=True)
            return (x - m) * jax.lax.rsqrt(var + EPS_LN) * g + b

        def _split_heads(x):
            bsz, sl, _ = x.shape
            return x.reshape(bsz, sl, HEADS, DEPTH).transpose(0, 2, 1, 3)
        key = jax.random.key(seed)
        ks = jax.random.split(key, 8)
        lecun = 1.0 / np.sqrt(D_MODEL)
        glorot = np.sqrt(2.0 / (D_MODEL + D_MODEL))
        return {'q': jax.random.normal(ks[0], (B, S, D_MODEL), jnp.float32), 'k': jax.random.normal(ks[1], (B, S, D_MODEL), jnp.float32), 'v': jax.random.normal(ks[2], (B, S, D_MODEL), jnp.float32), 'mask': jnp.ones((B, S), jnp.float32), 'wq': jax.random.normal(ks[3], (D_MODEL, D_MODEL), jnp.float32) * lecun, 'wk': jax.random.normal(ks[4], (D_MODEL, D_MODEL), jnp.float32) * lecun, 'wv': jax.random.normal(ks[5], (D_MODEL, D_MODEL), jnp.float32) * lecun, 'ln_gamma': jnp.ones((D_MODEL,), jnp.float32), 'ln_beta': jnp.zeros((D_MODEL,), jnp.float32), 'dense_w': jax.random.normal(ks[6], (D_MODEL, D_MODEL), jnp.float32) * glorot, 'dense_b': jnp.zeros((D_MODEL,), jnp.float32)}
    _L2_xattn_all = _L2_xattn_setup()
    _L2_xattn_in = {k: v for k, v in _L2_xattn_all.items() if k in ('wq', 'wk', 'wv', 'ln_gamma', 'ln_beta', 'dense_w', 'dense_b')}
    del _L2_xattn_all

    def _L2_ffn_setup():
        import jax, jax.numpy as jnp
        import numpy as np
        H = 128
        I = 512
        E = 4
        LN_EPS = 1e-12

        def _layer_norm(x, gamma, beta, eps=LN_EPS):
            mu = jnp.mean(x, axis=-1, keepdims=True)
            var = jnp.mean(jnp.square(x - mu), axis=-1, keepdims=True)
            return (x - mu) * jax.lax.rsqrt(var + eps) * gamma + beta
        key = jax.random.key(seed)
        ks = jax.random.split(key, 8)
        B, S = (4, 64)
        scale = 0.02
        return {'hidden_states': jax.random.normal(ks[0], (B, S, H), jnp.float32), 'W_router': jax.random.normal(ks[1], (H, E), jnp.float32) * scale, 'W1': jax.random.normal(ks[2], (E, H, I), jnp.float32) * scale, 'b1': jax.random.normal(ks[3], (E, I), jnp.float32) * scale, 'Wo': jax.random.normal(ks[4], (I, H), jnp.float32) * scale, 'bo': jax.random.normal(ks[5], (H,), jnp.float32) * scale, 'ln_gamma': jnp.ones((H,), jnp.float32), 'ln_beta': jnp.zeros((H,), jnp.float32)}
    _L2_ffn_all = _L2_ffn_setup()
    _L2_ffn_in = {k: v for k, v in _L2_ffn_all.items() if k in ('W_router', 'W1', 'b1', 'Wo', 'bo', 'ln_gamma', 'ln_beta')}
    del _L2_ffn_all

    def _L3_xattn_setup():
        import jax, jax.numpy as jnp
        import numpy as np
        D_MODEL = 128
        H = 16
        D_K = D_MODEL // H
        key = jax.random.key(seed)
        ks = jax.random.split(key, 8)
        B, S = (2, 256)
        scale = 1.0 / np.sqrt(D_MODEL)
        return {'query': jax.random.normal(ks[0], (B, S, D_MODEL), dtype=jnp.float32), 'key': jax.random.normal(ks[1], (B, S, D_MODEL), dtype=jnp.float32), 'value': jax.random.normal(ks[2], (B, S, D_MODEL), dtype=jnp.float32), 'mask': jnp.ones((B, 1, 1, S), dtype=jnp.int32), 'Wq': jax.random.normal(ks[3], (D_MODEL, D_MODEL), dtype=jnp.float32) * scale, 'Wk': jax.random.normal(ks[4], (D_MODEL, D_MODEL), dtype=jnp.float32) * scale, 'Wv': jax.random.normal(ks[5], (D_MODEL, D_MODEL), dtype=jnp.float32) * scale, 'Wo': jax.random.normal(ks[6], (D_MODEL, D_MODEL), dtype=jnp.float32) * scale}
    _L3_xattn_all = _L3_xattn_setup()
    _L3_xattn_in = {k: v for k, v in _L3_xattn_all.items() if k in ('Wq', 'Wk', 'Wv', 'Wo')}
    del _L3_xattn_all

    def _L3_ffn_setup():
        import jax, jax.numpy as jnp
        import numpy as np
        E = 8
        K = 2
        D = 128
        key = jax.random.key(seed)
        k0, k1, k2, k3 = jax.random.split(key, 4)
        x = jax.random.normal(k0, (2, 256, D), dtype=jnp.float32)
        gate_w = jax.random.normal(k1, (D, E), dtype=jnp.float32) * 0.02
        fc_w = jax.random.normal(k2, (E, D, 4 * D), dtype=jnp.float32) * 0.02
        proj_w = jax.random.normal(k3, (E, 4 * D, D), dtype=jnp.float32) * 0.02
        return {'x': x, 'gate_w': gate_w, 'fc_w': fc_w, 'proj_w': proj_w}
    _L3_ffn_all = _L3_ffn_setup()
    _L3_ffn_in = {k: v for k, v in _L3_ffn_all.items() if k in ('gate_w', 'fc_w', 'proj_w')}
    del _L3_ffn_all
    return {'x': x, 'ctx_1024': ctx_1024, 'itok_SxS2_0_2016': itok_SxS2_0_2016, 'mask_BxS2_ff1': mask_BxS2_ff1, 'mask_Bx1x1xS2_if1': mask_Bx1x1xS2_if1, 'L0_xattn_igate_w': _L0_xattn_in['igate_w'], 'L0_xattn_igate_b': _L0_xattn_in['igate_b'], 'L0_xattn_fgate_w': _L0_xattn_in['fgate_w'], 'L0_xattn_fgate_b': _L0_xattn_in['fgate_b'], 'L0_xattn_rpe': _L0_xattn_in['rpe'], 'L0_xattn_ln_w': _L0_xattn_in['ln_w'], 'L0_xattn_ln_b': _L0_xattn_in['ln_b'], 'L0_ffn_wf': _L0_ffn_in['wf'], 'L0_ffn_uf': _L0_ffn_in['uf'], 'L0_ffn_bf': _L0_ffn_in['bf'], 'L0_ffn_wi': _L0_ffn_in['wi'], 'L0_ffn_ui': _L0_ffn_in['ui'], 'L0_ffn_bi': _L0_ffn_in['bi'], 'L0_ffn_wc': _L0_ffn_in['wc'], 'L0_ffn_uc': _L0_ffn_in['uc'], 'L0_ffn_bc': _L0_ffn_in['bc'], 'L0_ffn_wo': _L0_ffn_in['wo'], 'L0_ffn_uo': _L0_ffn_in['uo'], 'L0_ffn_bo': _L0_ffn_in['bo'], 'L0_ffn_in_c': _L0_ffn_in['in_c'], 'L1_xattn_Wq': _L1_xattn_in['Wq'], 'L1_xattn_bq': _L1_xattn_in['bq'], 'L1_xattn_Wk': _L1_xattn_in['Wk'], 'L1_xattn_bk': _L1_xattn_in['bk'], 'L1_xattn_Wv': _L1_xattn_in['Wv'], 'L1_xattn_bv': _L1_xattn_in['bv'], 'L1_xattn_Wo': _L1_xattn_in['Wo'], 'L1_xattn_bo': _L1_xattn_in['bo'], 'L1_ffn_Wr': _L1_ffn_in['Wr'], 'L1_ffn_We': _L1_ffn_in['We'], 'L2_xattn_wq': _L2_xattn_in['wq'], 'L2_xattn_wk': _L2_xattn_in['wk'], 'L2_xattn_wv': _L2_xattn_in['wv'], 'L2_xattn_ln_gamma': _L2_xattn_in['ln_gamma'], 'L2_xattn_ln_beta': _L2_xattn_in['ln_beta'], 'L2_xattn_dense_w': _L2_xattn_in['dense_w'], 'L2_xattn_dense_b': _L2_xattn_in['dense_b'], 'L2_ffn_W_router': _L2_ffn_in['W_router'], 'L2_ffn_W1': _L2_ffn_in['W1'], 'L2_ffn_b1': _L2_ffn_in['b1'], 'L2_ffn_Wo': _L2_ffn_in['Wo'], 'L2_ffn_bo': _L2_ffn_in['bo'], 'L2_ffn_ln_gamma': _L2_ffn_in['ln_gamma'], 'L2_ffn_ln_beta': _L2_ffn_in['ln_beta'], 'L3_xattn_Wq': _L3_xattn_in['Wq'], 'L3_xattn_Wk': _L3_xattn_in['Wk'], 'L3_xattn_Wv': _L3_xattn_in['Wv'], 'L3_xattn_Wo': _L3_xattn_in['Wo'], 'L3_ffn_gate_w': _L3_ffn_in['gate_w'], 'L3_ffn_fc_w': _L3_ffn_in['fc_w'], 'L3_ffn_proj_w': _L3_ffn_in['proj_w']}

def reference(x, ctx_1024, itok_SxS2_0_2016, mask_BxS2_ff1, mask_Bx1x1xS2_if1, L0_xattn_igate_w, L0_xattn_igate_b, L0_xattn_fgate_w, L0_xattn_fgate_b, L0_xattn_rpe, L0_xattn_ln_w, L0_xattn_ln_b, L0_ffn_wf, L0_ffn_uf, L0_ffn_bf, L0_ffn_wi, L0_ffn_ui, L0_ffn_bi, L0_ffn_wc, L0_ffn_uc, L0_ffn_bc, L0_ffn_wo, L0_ffn_uo, L0_ffn_bo, L0_ffn_in_c, L1_xattn_Wq, L1_xattn_bq, L1_xattn_Wk, L1_xattn_bk, L1_xattn_Wv, L1_xattn_bv, L1_xattn_Wo, L1_xattn_bo, L1_ffn_Wr, L1_ffn_We, L2_xattn_wq, L2_xattn_wk, L2_xattn_wv, L2_xattn_ln_gamma, L2_xattn_ln_beta, L2_xattn_dense_w, L2_xattn_dense_b, L2_ffn_W_router, L2_ffn_W1, L2_ffn_b1, L2_ffn_Wo, L2_ffn_bo, L2_ffn_ln_gamma, L2_ffn_ln_beta, L3_xattn_Wq, L3_xattn_Wk, L3_xattn_Wv, L3_xattn_Wo, L3_ffn_gate_w, L3_ffn_fc_w, L3_ffn_proj_w):
    import jax
    import jax.numpy as jnp

    def _L0_xattn_ref(q, k, v, igate_w, igate_b, fgate_w, fgate_b, rpe, ln_w, ln_b, hops):
        import jax, jax.numpy as jnp
        import numpy as np
        B, S, DIM, NH = (32, 64, 128, 8)
        DH = DIM // NH
        EPS = 1e-06
        LN_EPS = 1e-05

        def _make_hops(n):
            hops = np.zeros((n, n), dtype=np.int64)
            cur = 1
            for i in range(n):
                for j in range(i + 1, n):
                    hops[i, j] = cur
                    hops[j, i] = cur
                    cur += 1
            return (hops, cur)

        def _mlstm_forward(q, k, v, igate_w, igate_b, fgate_w, fgate_b, rpe, ln_w, ln_b, hops):
            Bq, Sq, _ = q.shape
            pos_emb = rpe[hops]
            gate_in = jnp.concatenate([q, k, v], axis=-1)
            ig = gate_in @ igate_w.T + igate_b
            fg = gate_in @ fgate_w.T + fgate_b
            ig = jnp.transpose(ig, (0, 2, 1))
            fg = jnp.transpose(fg, (0, 2, 1))
            qh = q.reshape(Bq, Sq, NH, DH).transpose(0, 2, 1, 3)
            kh = k.reshape(Bq, Sq, NH, DH).transpose(0, 2, 1, 3)
            vh = v.reshape(Bq, Sq, NH, DH).transpose(0, 2, 1, 3)
            log_f = jax.nn.log_sigmoid(fg)
            csum = jnp.cumsum(log_f, axis=-1)
            csum = jnp.concatenate([jnp.zeros((Bq, NH, 1), csum.dtype), csum], axis=-1)
            lfm = csum[:, :, :, None] - csum[:, :, None, :]
            ltr = jnp.tril(jnp.ones((Sq, Sq), dtype=bool))
            log_fg_matrix = jnp.where(ltr, lfm[:, :, 1:, 1:], -jnp.inf)
            log_D = log_fg_matrix + ig[:, :, None, :]
            max_log_D = jnp.max(log_D, axis=-1, keepdims=True)
            D = jnp.exp(log_D - max_log_D)
            k_scaled = kh / np.sqrt(DH).astype(np.float32)
            pe = pos_emb.reshape(Sq, Sq, NH, DH)
            k_hop = jnp.einsum('bhvc,vmhc->bhvm', qh, pe)
            qk = jnp.einsum('bhsd,bhtd->bhst', qh, k_scaled)
            C = (qk + k_hop) * D
            normalizer = jnp.maximum(jnp.abs(jnp.sum(C, axis=-1, keepdims=True)), jnp.exp(-max_log_D))
            Cn = C / (normalizer + EPS)
            h = Cn @ vh
            mu = jnp.mean(h, axis=-1, keepdims=True)
            var = jnp.mean(jnp.square(h - mu), axis=-1, keepdims=True)
            hn = (h - mu) / jnp.sqrt(var + LN_EPS)
            w = (1.0 + ln_w).reshape(NH, DH)
            b = ln_b.reshape(NH, DH)
            hn = hn * w[None, :, None, :] + b[None, :, None, :]
            return hn.transpose(0, 2, 1, 3).reshape(Bq, Sq, DIM)
        return _mlstm_forward(q, k, v, igate_w, igate_b, fgate_w, fgate_b, rpe, ln_w, ln_b, hops)

    def _L0_ffn_ref(x, wf, uf, bf, wi, ui, bi, wc, uc, bc, wo, uo, bo, in_c):
        import jax, jax.numpy as jnp
        import numpy as np
        from jax import lax
        T, B, I, M, O = (32, 64, 128, 128, 128)

        def _xavier(key, shape):
            fan_out, fan_in = shape
            limit = float(np.sqrt(6.0 / (fan_in + fan_out)))
            return jax.random.uniform(key, shape, jnp.float32, -limit, limit)
        batch = x.shape[1]
        c0 = jnp.broadcast_to(in_c, (batch, in_c.shape[0]))

        def step(c, xt):
            ft = jax.nn.sigmoid(xt @ wf.T + c @ uf.T + bf)
            it = jax.nn.sigmoid(xt @ wi.T + c @ ui.T + bi)
            gt = jnp.tanh(xt @ wc.T + c @ uc.T + bc)
            c = ft * c + it * gt
            return (c, None)
        c_final, _ = lax.scan(step, c0, x)
        h = jnp.tanh(jnp.einsum('tbi,oi->tbo', x, wo) + c_final @ uo.T + bo)
        return h

    def _L1_xattn_ref(inputs_q, inputs_kv, Wq, bq, Wk, bk, Wv, bv, Wo, bo):
        import jax, jax.numpy as jnp
        import numpy as np
        B, Q, K, D = (4, 1500, 1500, 128)
        H, HD = (16, 64)
        q = jnp.einsum('bqm,mhd->bqhd', inputs_q, Wq) + bq
        k = jnp.einsum('bkm,mhd->bkhd', inputs_kv, Wk) + bk
        v = jnp.einsum('bkm,mhd->bkhd', inputs_kv, Wv) + bv
        q = q / jnp.sqrt(jnp.asarray(HD, q.dtype))
        attn = jnp.einsum('bqhd,bkhd->bhqk', q, k)
        attn = jax.nn.softmax(attn, axis=-1)
        out = jnp.einsum('bhqk,bkhd->bqhd', attn, v)
        return jnp.einsum('bqhd,hdm->bqm', out, Wo) + bo

    def _L1_ffn_ref(x, Wr, We):
        import jax, jax.numpy as jnp
        import numpy as np
        B, T, D, E, TOP_K = (4, 512, 128, 8, 2)
        CAPACITY_FACTOR = 1.5
        Bb, Tt, Dd = x.shape
        Ee = Wr.shape[0]
        K = TOP_K
        C = int(Tt * K / Ee * CAPACITY_FACTOR) + 1
        logits = jnp.einsum('btd,ed->bte', x, Wr)
        top_vals, top_idx = jax.lax.top_k(logits, K)
        w = jax.nn.softmax(top_vals, axis=-1)
        flat_e = top_idx.reshape(Bb, Tt * K)
        oh = jax.nn.one_hot(flat_e, Ee, dtype=jnp.int32)
        pos_all = jnp.cumsum(oh, axis=1) - oh
        pos = jnp.take_along_axis(pos_all, flat_e[..., None], axis=-1)[..., 0]
        keep = pos < C
        b_idx = jnp.arange(Bb, dtype=jnp.int32)[:, None]
        dst = (b_idx * Ee + flat_e) * C + pos
        dst = jnp.where(keep, dst, Bb * Ee * C).reshape(-1)
        x_rep = jnp.repeat(x, K, axis=1).reshape(-1, Dd)
        buf = jnp.zeros((Bb * Ee * C, Dd), dtype=x.dtype).at[dst].add(x_rep, mode='drop')
        expert_in = buf.reshape(Bb, Ee, C, Dd)
        expert_out = jnp.einsum('becd,edf->becf', expert_in, We)
        gathered = jnp.take(expert_out.reshape(Bb * Ee * C, Dd), dst, axis=0, mode='fill', fill_value=0.0)
        gathered = gathered.reshape(Bb, Tt, K, Dd)
        out = jnp.einsum('btk,btkd->btd', w, gathered)
        return out

    def _L2_xattn_ref(q, k, v, mask, wq, wk, wv, ln_gamma, ln_beta, dense_w, dense_b):
        import jax, jax.numpy as jnp
        import numpy as np
        D_MODEL = 128
        HEADS = 16
        DEPTH = D_MODEL // HEADS
        B, S = (4, 512)
        EPS_K = 1e-06
        EPS_LN = 1e-06

        def _layernorm(x, g, b):
            m = jnp.mean(x, axis=-1, keepdims=True)
            var = jnp.var(x, axis=-1, keepdims=True)
            return (x - m) * jax.lax.rsqrt(var + EPS_LN) * g + b

        def _split_heads(x):
            bsz, sl, _ = x.shape
            return x.reshape(bsz, sl, HEADS, DEPTH).transpose(0, 2, 1, 3)
        bsz = q.shape[0]
        em = mask[:, None, :, None]
        qh = _split_heads(_layernorm(q @ wq, ln_gamma, ln_beta))
        kh = _split_heads(_layernorm(k @ wk, ln_gamma, ln_beta))
        vh = _split_heads(_layernorm(v @ wv, ln_gamma, ln_beta))
        q_prime = jax.nn.relu(qh) + EPS_K
        k_prime = (jax.nn.relu(kh) + EPS_K) * em
        vh = vh * em
        kv = jnp.einsum('bhnd,bhne->bhde', k_prime, vh)
        z = 1.0 / (jnp.einsum('bhnd,bhd->bhn', q_prime, k_prime.sum(axis=-2)) + EPS_K)
        att = jnp.einsum('bhnd,bhde,bhn->bhne', q_prime, kv, z)
        att = att.reshape(bsz, -1, D_MODEL)
        out = att @ dense_w + dense_b
        return _layernorm(out, ln_gamma, ln_beta)

    def _L2_ffn_ref(hidden_states, W_router, W1, b1, Wo, bo, ln_gamma, ln_beta):
        import jax, jax.numpy as jnp
        import numpy as np
        H = 128
        I = 512
        E = 4
        LN_EPS = 1e-12

        def _layer_norm(x, gamma, beta, eps=LN_EPS):
            mu = jnp.mean(x, axis=-1, keepdims=True)
            var = jnp.mean(jnp.square(x - mu), axis=-1, keepdims=True)
            return (x - mu) * jax.lax.rsqrt(var + eps) * gamma + beta
        B, S, _ = hidden_states.shape
        x = hidden_states.reshape(-1, H)
        logits = x @ W_router
        expert_idx = jnp.argmax(logits, axis=-1)
        h = jnp.einsum('th,ehi->tei', x, W1) + b1
        h = jax.nn.gelu(h, approximate=False)
        onehot = jax.nn.one_hot(expert_idx, E, dtype=x.dtype)
        intermediate = jnp.einsum('te,tei->ti', onehot, h)
        y = intermediate @ Wo + bo + x
        y = _layer_norm(y, ln_gamma, ln_beta)
        return y.reshape(B, S, H)

    def _L3_xattn_ref(query, key, value, mask, Wq, Wk, Wv, Wo):
        import jax, jax.numpy as jnp
        import numpy as np
        D_MODEL = 128
        H = 16
        D_K = D_MODEL // H
        B, S, _ = query.shape
        q = (query @ Wq.T).reshape(B, S, H, D_K)
        k = (key @ Wk.T).reshape(B, S, H, D_K)
        v = (value @ Wv.T).reshape(B, S, H, D_K)
        scores = jnp.einsum('bqhd,bkhd->bhqk', q, k) / jnp.sqrt(jnp.float32(D_K))
        out = jnp.einsum('bhqk,bkhd->bqhd', scores, v).reshape(B, S, D_MODEL)
        return out @ Wo.T

    def _L3_ffn_ref(x, gate_w, fc_w, proj_w):
        import jax, jax.numpy as jnp
        import numpy as np
        E = 8
        K = 2
        D = 128
        orig_shape = x.shape
        d = orig_shape[-1]
        xt = x.reshape(-1, d)
        gates = jax.nn.softmax(xt @ gate_w, axis=-1)
        top_v, top_i = jax.lax.top_k(gates, K)
        top_v = top_v / jnp.sum(top_v, axis=-1, keepdims=True)
        h = jnp.einsum('nd,edf->enf', xt, fc_w)
        h = jax.nn.gelu(h, approximate=False)
        eo = jnp.einsum('enf,efd->end', h, proj_w)
        eo_nt = jnp.swapaxes(eo, 0, 1)
        sel = jnp.take_along_axis(eo_nt, top_i[:, :, None], axis=1)
        out = jnp.sum(sel * top_v[:, :, None], axis=1)
        return out.reshape(orig_shape)
    x = x + _L0_xattn_ref(_layernorm(x, axis=-1), ctx_1024, ctx_1024, L0_xattn_igate_w, L0_xattn_igate_b, L0_xattn_fgate_w, L0_xattn_fgate_b, L0_xattn_rpe, L0_xattn_ln_w, L0_xattn_ln_b, itok_SxS2_0_2016)
    x = x + _L0_ffn_ref(_layernorm(x, axis=-1), L0_ffn_wf, L0_ffn_uf, L0_ffn_bf, L0_ffn_wi, L0_ffn_ui, L0_ffn_bi, L0_ffn_wc, L0_ffn_uc, L0_ffn_bc, L0_ffn_wo, L0_ffn_uo, L0_ffn_bo, L0_ffn_in_c)
    x = x + _L1_xattn_ref(_layernorm(x, axis=-1), ctx_1024, L1_xattn_Wq, L1_xattn_bq, L1_xattn_Wk, L1_xattn_bk, L1_xattn_Wv, L1_xattn_bv, L1_xattn_Wo, L1_xattn_bo)
    x = x + _L1_ffn_ref(_layernorm(x, axis=-1), L1_ffn_Wr, L1_ffn_We)
    x = x + _L2_xattn_ref(_layernorm(x, axis=-1), ctx_1024, ctx_1024, mask_BxS2_ff1, L2_xattn_wq, L2_xattn_wk, L2_xattn_wv, L2_xattn_ln_gamma, L2_xattn_ln_beta, L2_xattn_dense_w, L2_xattn_dense_b)
    x = x + _L2_ffn_ref(_layernorm(x, axis=-1), L2_ffn_W_router, L2_ffn_W1, L2_ffn_b1, L2_ffn_Wo, L2_ffn_bo, L2_ffn_ln_gamma, L2_ffn_ln_beta)
    x = x + _L3_xattn_ref(_layernorm(x, axis=-1), ctx_1024, ctx_1024, mask_Bx1x1xS2_if1, L3_xattn_Wq, L3_xattn_Wk, L3_xattn_Wv, L3_xattn_Wo)
    x = x + _L3_ffn_ref(_layernorm(x, axis=-1), L3_ffn_gate_w, L3_ffn_fc_w, L3_ffn_proj_w)
    return x

_drawn_inputs = setup_inputs


def setup_inputs(seed=0):
    import zlib

    import numpy as np

    out = dict(_drawn_inputs(seed))
    spreads = {'L0_xattn_ln_b': (0.0, 0.1),
     'L0_ffn_bf': (0.0, 0.697),
     'L0_ffn_bi': (0.0, 0.733),
     'L0_ffn_bc': (0.0, 0.1),
     'L0_ffn_bo': (0.0, 0.1),
     'L0_ffn_in_c': (0.0, 2.0),
     'L1_xattn_bq': (0.0, 0.8),
     'L1_xattn_bk': (0.0, 2.0),
     'L1_xattn_bv': (0.0, 0.1),
     'L1_xattn_bo': (0.0, 0.1),
     'L2_xattn_ln_gamma': (1.0, 0.2),
     'L2_xattn_ln_beta': (0.0, 0.1),
     'L2_xattn_dense_b': (0.0, 0.1),
     'L2_ffn_ln_gamma': (1.0, 0.2),
     'L2_ffn_ln_beta': (0.0, 0.283)}
    factors = {'L0_xattn_igate_b': 64.0,
     'L0_xattn_fgate_w': 5.114,
     'L1_xattn_Wq': 8.0,
     'L1_xattn_Wk': 8.0,
     'L2_ffn_W_router': 3.787,
     'L2_ffn_W1': 3.222,
     'L2_ffn_b1': 8.0,
     'L2_ffn_Wo': 3.182,
     'L2_ffn_bo': 7.039,
     'L3_ffn_gate_w': 8.0,
     'L3_ffn_fc_w': 8.0,
     'L3_ffn_proj_w': 8.0}
    for name, (base, spread) in spreads.items():
        noise = np.random.default_rng([zlib.crc32(name.encode()), seed]).standard_normal(out[name].shape)
        drawn = base * np.exp(spread * noise) if base else spread * noise
        out[name] = jnp.asarray(drawn.astype(out[name].dtype))
    for name, factor in factors.items():
        out[name] = (out[name] * factor).astype(out[name].dtype)
    return out
```

```python
from contextlib import ExitStack

import concourse.bass as bass
from concourse import mybir

F32 = mybir.dt.float32
BF16 = mybir.dt.bfloat16
I32 = mybir.dt.int32
ALU = mybir.AluOpType
ACT = mybir.ActivationFunctionType
AX_X = mybir.AxisListType.X
ds = bass.ds

P = 128
B, S, D = 128, 64, 128
TOK = B * S
NT = TOK // P
NG = NT // 4
GW = 4 * P
LN_EPS = 1e-5

H0, C0 = 8, 16
H1, C1 = 16, 64
HP1 = H1 // 2
E1, CAP = 8, 25
H2, C2 = 16, 8
E2, I2 = 4, 512
E3, I3 = 8, 512
NEG = -1e30


def tile_of(t, i):
    return t[:, ds(i, 1), :].rearrange("p a w -> p (a w)")


def tiles_of(t, i, n):
    return t[:, ds(i, n), :]


def skewed(eng, units, front, back):
    front(0, 0, 0)
    with eng.Fori(0, units // 2 - 1) as j:
        front(2 * j + 1, 1, j)
        back(2 * j, 0, j)
        front(2 * j + 2, 0, j + 1)
        back(2 * j + 1, 1, j)
    last = units // 2 - 1
    front(units - 1, 1, last)
    back(units - 2, 0, last)
    back(units - 1, 1, last)


def two_slots(eng, units, body):
    with eng.Fori(0, units // 2) as j:
        body(2 * j, 0, j)
        body(2 * j + 1, 1, j)


def three_steps(eng, units, first, second, third):
    first(0, 0, 0)
    with eng.Fori(0, units // 2 - 1) as j:
        second(2 * j, 0, j)
        first(2 * j + 1, 1, j)
        third(2 * j, 0, j)
        second(2 * j + 1, 1, j)
        first(2 * j + 2, 0, j + 1)
        third(2 * j + 1, 1, j)
    last = units // 2 - 1
    second(units - 2, 0, last)
    first(units - 1, 1, last)
    third(units - 2, 0, last)
    second(units - 1, 1, last)
    third(units - 1, 1, last)


class Chain:

    def __init__(self, eng, sem, base=0):
        self.eng, self.sem, self.base, self.n = eng, sem, base, 0

    def __call__(self, ins):
        self.n += 1
        ins.then_inc(self.sem, 1)
        self.eng.wait_ge(self.sem, self.base + self.n)


def free_at(u):
    return u + 1


def done_at(u, n=2):
    return u + 1 + n


def bcast_mid(ap, n):
    return ap.rearrange("p (a w) -> p a w", a=1).broadcast_to([ap.shape[0], n, ap.shape[1]])


def bcast_in(ap, n):
    return ap.rearrange("p (w a) -> p w a", a=1).broadcast_to([ap.shape[0], ap.shape[1], n])


class Stage:

    def __init__(self, nc, name):
        self.nc, self.name, self.ctx, self.sems = nc, name, ExitStack(), []

    def __enter__(self):
        self.ctx.__enter__()
        return self

    def __exit__(self, *e):
        if not e[0]:
            self.nc.clear_and_free_semaphores(self.sems)
            self.nc.all_engine_barrier()
        return self.ctx.__exit__(*e)

    def sb(self, name, shape, dt=F32):
        return self.ctx.enter_context(self.nc.sbuf_tensor(f"{self.name}_{name}", shape, dt))

    def ps(self, name, shape, dt=F32):
        return self.ctx.enter_context(self.nc.psum_tensor(f"{self.name}_{name}", shape, dt))

    def sem(self, name):
        self.sems.append(self.nc.alloc_semaphore(name=f"{self.name}_{name}"))
        return self.sems[-1]


class Resident:
    pass


def stage_setup(nc, R, A):
    with Stage(nc, "setup") as st:
        loaded, made, zeroed = st.sem("loaded"), st.sem("made"), st.sem("zeroed")
        with nc.Block() as block:
            @block.sync
            def _(sp):
                sp.dma_start(R.X[:], A["x"].rearrange("(i p) d -> p i d", p=P)).then_inc(loaded, 16)
                sp.wait_ge(loaded, 16)

            @block.vector
            def _(dve):
                for t in (R.ident, R.same2, R.tri_incl, R.tri_strict, R.delta, R.bd16, R.bd8,
                          R.vmask, R.causal, R.ident_bf):
                    dve.memset(t[:], 0.0).then_inc(zeroed, 1)
                dve.memset(R.ones[:], 1.0)
                dve.wait_ge(zeroed, 10)
                for h in range(2):
                    rows = slice(64 * h, 64 * h + 64)
                    for t in (R.same2, R.tri_incl, R.tri_strict):
                        dve.memset(t[rows, 64 * h:64 * h + 64], 1.0).then_inc(zeroed, 1)
                    dve.memset(R.vmask[rows, :, h, :], 1.0).then_inc(zeroed, 1)
                dve.memset(R.bd16[:], 1.0).then_inc(zeroed, 1)
                dve.memset(R.bd8[:], 1.0).then_inc(zeroed, 1)

            @block.gpsimd
            def _(gp):
                gp.wait_ge(zeroed, 20)
                link = Chain(gp, made)
                for t in (R.ident, R.ident_bf):
                    link(gp.affine_select(out=t[:], in_=t[:], compare_op=ALU.not_equal, fill=1.0, base=0,
                                     pattern=[[-1, 128]], channel_multiplier=1))
                link(gp.affine_select(out=R.tri_incl[:], in_=R.tri_incl[:], compare_op=ALU.is_ge, fill=0.0,
                                 base=0, pattern=[[1, 128]], channel_multiplier=-1))
                link(gp.affine_select(out=R.tri_strict[:], in_=R.tri_strict[:], compare_op=ALU.is_gt, fill=0.0,
                                 base=0, pattern=[[1, 128]], channel_multiplier=-1))
                for h in range(2):
                    rows = slice(64 * h, 64 * h + 64)
                    link(gp.affine_select(out=R.delta[rows, :], in_=R.delta[rows, :], compare_op=ALU.not_equal,
                                     fill=1.0, base=0, pattern=[[-1, 64]], channel_multiplier=1))
                    c = R.causal[rows, :].rearrange("p (h t) -> p h t", h=H0)
                    link(gp.affine_select(out=c, in_=c, compare_op=ALU.is_ge, fill=NEG, base=0,
                                     pattern=[[0, H0], [-1, S]], channel_multiplier=1))
                link(gp.affine_select(out=R.bd16[:], in_=R.bd16[:], compare_op=ALU.is_ge, fill=0.0, base=0,
                                 pattern=[[-C0, H0]], channel_multiplier=1))
                link(gp.affine_select(out=R.bd16[:], in_=R.bd16[:], compare_op=ALU.is_ge, fill=0.0, base=C0 - 1,
                                 pattern=[[C0, H0]], channel_multiplier=-1))
                link(gp.affine_select(out=R.bd8[:], in_=R.bd8[:], compare_op=ALU.is_ge, fill=0.0, base=0,
                                 pattern=[[-C2, H2], [0, C2]], channel_multiplier=1))
                link(gp.tensor_scalar(R.bd16q[:], R.bd16[:], 1.0 / C0 ** 0.5, None, ALU.mult))
                link(gp.affine_select(out=R.bd8[:], in_=R.bd8[:], compare_op=ALU.is_ge, fill=0.0, base=C2 - 1,
                                 pattern=[[C2, H2], [0, C2]], channel_multiplier=-1))


def stage_stats(nc, R, name, src=None, eps=LN_EPS):
    src = R.X if src is None else src
    with Stage(nc, name) as st:
        raw, t0, t1 = R.stats, R.t0, R.t1
        chain, rooted, var_ready = st.sem("chain"), st.sem("rooted"), st.sem("var_ready")
        with nc.Block() as block:
            @block.vector
            def _(dve):
                with dve.Fori(0, NG) as g:
                    for k in range(4):
                        i = g * 4 + k
                        dve.bn_stats(tile_of(raw, i), tile_of(src, i)).then_inc(chain, 1)
                dve.wait_ge(chain, NT)
                m0, v0, m1, v1 = (raw[:, :, c] for c in (1, 2, 4, 5))
                dve.tensor_tensor(R.mean[:], m0, m1, ALU.add).then_inc(chain, 1)
                dve.tensor_tensor(t0[:], m0, m1, ALU.subtract).then_inc(chain, 1)
                dve.tensor_tensor(t1[:], v0, v1, ALU.add).then_inc(chain, 1)
                dve.wait_ge(chain, NT + 3)
                dve.tensor_scalar(R.mean[:], R.mean[:], 0.5, None, ALU.mult).then_inc(chain, 1)
                dve.tensor_tensor(t0[:], t0[:], t0[:], ALU.mult).then_inc(chain, 1)
                dve.tensor_scalar(t1[:], t1[:], 1.0 / D, eps, ALU.mult, ALU.add).then_inc(chain, 1)
                dve.wait_ge(chain, NT + 6)
                dve.scalar_tensor_tensor(out=t0[:], in0=t0[:], scalar=0.25, in1=t1[:], op0=ALU.mult,
                                         op1=ALU.add).then_inc(var_ready, 1)
                dve.wait_ge(rooted, 1)
                dve.reciprocal(R.rstd[:], t1[:]).then_inc(chain, 1)

            @block.scalar
            def _(act):
                act.wait_ge(var_ready, 1)
                act.activation(t1[:], t0[:], ACT.Sqrt).then_inc(rooted, 1)



def stage_norm_T(nc, R, name):
    with Stage(nc, name) as st:
        xh = st.sb("xh", [P, 2, 4, P])
        ps = [st.ps(f"ps{k}", [P, GW]) for k in range(2)]
        normed, turned, moved = (st.sem(n) for n in ("normed", "turned", "moved"))
        with nc.Block() as block:
            @block.vector
            def _(dve):
                def body(g, s, j):
                    dve.wait_ge(turned, free_at(g))
                    for k in range(4):
                        i = g * 4 + k
                        norm = dve.tensor_scalar(xh[:, s, k, :], tile_of(R.X, i), R.mean[:, ds(i, 1)],
                                                 R.rstd[:, ds(i, 1)], ALU.subtract, ALU.mult)
                    norm.then_inc(normed, 1)
                two_slots(dve, NG, body)

            @block.tensor
            def _(pe):
                pe.sem_inc(turned, 2)

                def body(g, s, j):
                    pe.wait_ge(moved, free_at(g))
                    pe.wait_ge(normed, g + 1)
                    for k in range(4):
                        t = pe.transpose(ps[s][:, k * P:(k + 1) * P], xh[:, s, k, :], R.ident[:])
                    t.then_inc(turned, 1)
                two_slots(pe, NG, body)

            @block.scalar
            def _(act):
                act.sem_inc(moved, 2)

                def body(g, s, j):
                    act.wait_ge(turned, done_at(g))
                    act.activation(R.XT[:, ds(g * GW, GW)], ps[s][:], ACT.Copy).then_inc(moved, 1)
                two_slots(act, NG, body)


def stage_gates(nc, R, A):
    with Stage(nc, "gates") as st:
        wq, wk, wv = (st.sb(n, [P, 2 * H0]) for n in ("wq", "wk", "wv"))
        bias = st.sb("bias", [1, 2 * H0])
        qs, ks = st.sb("qs", [P, 2, P]), st.sb("ks", [P, 2, P])
        G = st.sb("G", [P, NT, 2 * H0])
        ig, fg = st.sb("ig", [P, NT * H0]), st.sb("fg", [P, NT * H0])
        t0, t1 = st.sb("t0", [P, NT * H0]), st.sb("t1", [P, NT * H0])
        ps = [st.ps(f"ps{k}", [P, 512]) for k in range(2)]
        pc = st.ps("pc", [P, 512])
        wload, xload = st.sem("wload"), [st.sem("xload0"), st.sem("xload1")]
        summed, moved, split, absd, exped, logged, logf, cum, end = (
            st.sem(n) for n in ("summed", "moved", "split", "absd", "exped", "logged", "logf", "cum", "end"))
        with nc.Block() as block:
            @block.sync
            def _(sp):
                for n, w in enumerate((wq, wk, wv)):
                    sp.dma_start(w[:], A["gate_wT"][n * P:(n + 1) * P, :]).then_inc(wload, 16)
                sp.dma_start(bias[:], A["gate_b"]).then_inc(wload, 16)

                def body(i, s, j):
                    sp.wait_ge(summed, free_at(i))
                    sp.dma_start(qs[:, s, :], R.XT[:, ds(i * P, P)]).then_inc(xload[s], 16)
                    sp.dma_start(ks[:, s, :], A["ctxT"][:, ds(i * P, P)]).then_inc(xload[s], 16)
                two_slots(sp, NT, body)

            @block.tensor
            def _(pe):
                pe.sem_inc(summed, 2)
                pe.wait_ge(wload, 64)

                def body(i, s, j):
                    pe.wait_ge(xload[s], j * 32 + 32)
                    pe.wait_ge(moved, free_at(i))
                    o = ps[s][:, 0:2 * H0]
                    pe.matmul(o, qs[:, s, :], wq[:], start=True, stop=False)
                    pe.matmul(o, ks[:, s, :], wk[:], start=False, stop=False)
                    pe.matmul(o, ks[:, s, :], wv[:], start=False, stop=False)
                    pe.matmul(o, R.ones[0:1, 0:P], bias[:], start=False, stop=True).then_inc(summed, 1)
                two_slots(pe, NT, body)
                pe.wait_ge(logf, 1)
                pe.matmul(pc[:], R.tri_incl[:], t0[:], start=True, stop=True).then_inc(cum, 1)

            @block.scalar
            def _(act):
                act.sem_inc(moved, 2)

                def body(i, s, j):
                    act.wait_ge(summed, done_at(i))
                    act.activation(tile_of(G, i), ps[s][:, 0:2 * H0], ACT.Copy).then_inc(moved, 1)
                two_slots(act, NT, body)
                act.wait_ge(absd, 1)
                act.activation(t1[:], t0[:], ACT.Exp, scale=-1.0).then_inc(exped, 1)
                act.wait_ge(exped, 1)
                act.activation(t1[:], t1[:], ACT.Ln, bias=1.0).then_inc(logged, 1)

            @block.vector
            def _(dve):
                dve.wait_ge(moved, NT + 2)
                v = lambda t: t[:].rearrange("p (i h) -> p i h", i=NT)
                dve.tensor_copy(v(ig), G[:, :, 0:H0]).then_inc(split, 1)
                dve.tensor_copy(v(fg), G[:, :, H0:]).then_inc(split, 1)
                dve.wait_ge(split, 2)
                dve.scalar_tensor_tensor(out=t0[:], in0=fg[:], scalar=-1.0, in1=fg[:], op0=ALU.mult,
                                         op1=ALU.max).then_inc(absd, 1)
                dve.wait_ge(logged, 1)
                dve.scalar_tensor_tensor(out=t0[:], in0=fg[:], scalar=0.0, in1=t1[:], op0=ALU.min,
                                         op1=ALU.subtract).then_inc(logf, 1)
                dve.wait_ge(cum, 1)
                dve.tensor_copy(R.cs[:], pc[:])
                dve.tensor_tensor(R.g[:].rearrange("p i h -> p (i h)"), ig[:], pc[:], ALU.subtract)


def stage_hop(nc, R, A):
    NV = S // 2
    RO = S // 4
    with Stage(nc, "hop") as st:
        idx = st.sb("idx", [P, NV], I32)
        rows = st.sb("rows", [P, NV, D])
        rows_s = st.sb("rows_s", [P, 2, 2, P])
        rT = [st.ps(f"rT{k}", [P, 512]) for k in range(2)]
        out = [st.ps(f"out{k}", [P, 512]) for k in range(4)]
        bd = st.sb("bd", [P, 2, 4, H0, S])
        qv = st.sb("qv", [P, 2, 4, P])
        kh = st.sb("kh", [P, 2, 4, 512])
        iload, gathered = st.sem("iload"), st.sem("gathered")
        rows_in, turned, spread, prod, moved = (st.sem(n) for n in ("rows_in", "turned", "spread", "prod", "moved"))
        stored = [st.sem(f"stored{k}") for k in range(2)]
        with nc.Block() as block:
            @block.sync
            def _(sp):
                with nc.allow_non_contiguous_dma("4096 indices"):
                    sp.dma_start(idx[:], A["hopsT"]).then_inc(iload, 16)
                for k in range(2):
                    sp.sem_inc(stored[k], 16)

                def body(r, s, j):
                    sp.wait_ge(moved, r * 4 + 4 + 4)
                    sp.dma_start(R.khop[:, ds(4 * r, 4), :], kh[:, s, :, :]).then_inc(stored[s], 16)
                two_slots(sp, RO, body)
                for k in range(2):
                    sp.wait_ge(stored[k], 16 * (RO // 2) + 16)

            @block.gpsimd
            def _(gp):
                gp.wait_ge(iload, 16)
                for n in range(NV):
                    gp.indirect_dma_start(out=rows[:, n, :], out_offset=None, in_=A["rpe"],
                                          in_offset=bass.IndirectOffsetOnAxis(ap=idx[:, n:n + 1], axis=0)
                                          ).then_inc(gathered, 16)

            @block.scalar
            def _(act):
                act.sem_inc(moved, 4)
                act.wait_ge(gathered, 16 * NV)

                def front(r, s, j):
                    act.wait_ge(turned, free_at(r))
                    act.activation(rows_s[:, s, :, :], tiles_of(rows, 2 * r, 2), ACT.Copy).then_inc(rows_in, 1)

                def back(r, s, j):
                    act.wait_ge(stored[s], j * 16 + 16)
                    for k in range(4):
                        act.wait_ge(prod, r * 4 + k + 1 + 8)
                        act.activation(kh[:, s, k, :], out[k][:], ACT.Copy).then_inc(moved, 1)
                skewed(act, RO, front, back)

            @block.tensor
            def _(pe):
                pe.sem_inc(turned, 2)
                pe.sem_inc(prod, 8)

                def front(r, s, j):
                    pe.wait_ge(rows_in, r + 1)
                    pe.wait_ge(spread, free_at(r))
                    for k in range(2):
                        t = pe.transpose(rT[s][:, k * P:(k + 1) * P], rows_s[:, s, k, :], R.ident[:])
                    t.then_inc(turned, 1)

                def back(r, s, j):
                    pe.wait_ge(spread, done_at(r))
                    for k in range(4):
                        pe.wait_ge(moved, r * 4 + k + 1)
                        pe.matmul(out[k][:], qv[:, s, k, :], bd[:, s, k, :, :].rearrange("p h m -> p (h m)"),
                                  start=True, stop=True).then_inc(prod, 1)
                skewed(pe, RO, front, back)

            @block.vector
            def _(dve):
                dve.sem_inc(spread, 2)
                q3 = R.XT[:].rearrange("p (b v) -> p v b", v=S)

                def body(r, s, j):
                    dve.wait_ge(prod, r * 4 + 4)
                    dve.tensor_copy(qv[:, s, :, :], q3[:, ds(4 * r, 4), :])
                    dve.wait_ge(turned, done_at(r))
                    for k in range(4):
                        sp = dve.tensor_tensor(bd[:, s, k, :, :], bcast_mid(rT[s][:, k * S:k * S + S], H0),
                                               bcast_in(R.bd16[:], S), ALU.mult)
                    sp.then_inc(spread, 1)
                two_slots(dve, RO, body)


def stage_mlstm(nc, R, A):
    with Stage(nc, "mlstm") as st:
        qT = st.sb("qT", [P, 2, P])
        kT = st.sb("kT", [P, 2, P])
        vv = st.sb("vv", [P, 2, 2, D])
        kh = st.sb("kh", [P, 2, 512])
        kbd = st.sb("kbd", [P, 2, 2, H0, S])
        vbd = st.sb("vbd", [P, 2, 2, D])
        dg = st.sb("dg", [P, 2, 512])
        arg = st.sb("arg", [P, 2, 512])
        dec = st.sb("dec", [P, 2, 512])
        cc = st.sb("cc", [P, 2, 512])
        cT = st.sb("cT", [P, 2, 512])
        psA = [st.ps(f"psA{k}", [P, 512]) for k in range(2)]
        psQ = [st.ps(f"psQ{k}", [P, 512]) for k in range(2)]
        psT = [st.ps(f"psT{k}", [P, 512]) for k in range(2)]
        psH = [st.ps(f"psH{k}", [P, 512]) for k in range(2)]
        load = [st.sem(f"load{k}") for k in range(2)]
        kh_load = [st.sem(f"kh_load{k}") for k in range(2)]
        diag, bias_sum, scores, spread, argd, decd, csum, ct, ctm, hd, hm, qk_read, chain = (
            st.sem(n) for n in ("diag", "bias_sum", "scores", "spread", "argd", "decd", "csum",
                                "ct", "ctm", "hd", "hm", "qk_read", "chain"))
        with nc.Block() as block:
            @block.sync
            def _(sp):
                def body(i, s, j):
                    sp.wait_ge(hd, free_at(i))
                    c = A["ctx"][ds(i * P, P), :].rearrange("(b t) d -> t b d", b=2)
                    sp.dma_start(qT[:, s, :], R.XT[:, ds(i * P, P)]).then_inc(load[s], 16)
                    sp.dma_start(kT[:, s, :], A["ctxT"][:, ds(i * P, P)]).then_inc(load[s], 16)
                    for h in range(2):
                        sp.dma_start(vv[64 * h:64 * h + 64, s, :, :], c).then_inc(load[s], 16)
                    sp.dma_start(kh[:, s, :], R.khop[ds(2 * i, 2), :, :].rearrange("b v n -> (b v) n")
                                 ).then_inc(kh_load[s], 16)
                two_slots(sp, NT, body)

            @block.gpsimd
            def _(gp):
                def body(i, s, j):
                    gp.wait_ge(load[s], j * 64 + 64)
                    for b in range(2):
                        gp.tensor_tensor(kbd[:, s, b, :, :], bcast_mid(kT[:, s, b * S:b * S + S], H0),
                                         bcast_in(R.bd16q[:], S), ALU.mult)
                    gp.tensor_tensor(vbd[:, s, :, :], vv[:, s, :, :], bcast_mid(R.vmask128, 2),
                                     ALU.mult).then_inc(spread, 1)
                two_slots(gp, NT, body)

            @block.tensor
            def _(pe):
                for q in (bias_sum, scores, ct, hd):
                    pe.sem_inc(q, 2)

                def front(i, s, j):
                    pe.wait_ge(diag, i + 1)
                    pe.wait_ge(argd, free_at(i))
                    pe.matmul(psA[s][:], R.same2[:], dg[:, s, :], start=True, stop=False)
                    pe.matmul(psA[s][:], R.ident_bf[:], R.causal[:], start=False, stop=True).then_inc(bias_sum, 1)
                    pe.wait_ge(spread, i + 1)
                    pe.wait_ge(load[s], j * 64 + 64)
                    pe.wait_ge(qk_read, free_at(i))
                    for b in range(2):
                        q = pe.matmul(psQ[s][64 * b:64 * b + 64, :], qT[:, s, b * S:b * S + S],
                                      kbd[:, s, b, :, :].rearrange("p h t -> p (h t)"), start=True, stop=True)
                    q.then_inc(scores, 1)

                def back(i, s, j):
                    pe.wait_ge(csum, i + 1 + 2)
                    pe.wait_ge(ctm, free_at(i))
                    for k in range(4):
                        t = pe.transpose(psT[s][:, k * P:k * P + P], cc[:, s, k * P:k * P + P], R.ident[:])
                    t.then_inc(ct, 1)
                    pe.wait_ge(ctm, done_at(i))
                    pe.wait_ge(hm, free_at(i))
                    for b in range(2):
                        for k in range(4):
                            h = pe.matmul(psH[s][64 * b:64 * b + 64, 32 * k:32 * k + 32],
                                          cT[:, s, k * P + 64 * b:k * P + 64 * b + 64],
                                          vbd[:, s, b, 32 * k:32 * k + 32], start=True, stop=True)
                    h.then_inc(hd, 1)
                skewed(pe, NT, front, back)

            @block.vector
            def _(dve):
                for q in (argd, csum, qk_read):
                    dve.sem_inc(q, 2)

                def front(i, s, j):
                    dve.wait_ge(bias_sum, free_at(i))
                    dve.tensor_tensor(dg[:, s, :].rearrange("p (h t) -> p h t", h=H0),
                                      bcast_in(tile_of(R.g, i), S), bcast_mid(R.delta[:], H0),
                                      ALU.mult).then_inc(diag, 1)

                def mid(i, s, j):
                    link = Chain(dve, chain, i * 4)
                    a = psA[s][:].rearrange("p (h t) -> p h t", h=H0)
                    dve.wait_ge(bias_sum, done_at(i))
                    link(dve.tensor_reduce(tile_of(R.rowmax, i), a, AX_X, ALU.max))
                    dve.wait_ge(decd, free_at(i))
                    dve.tensor_tensor(arg[:, s, :].rearrange("p (h t) -> p h t", h=H0), a,
                                      bcast_in(tile_of(R.rowmax, i), S), ALU.subtract).then_inc(argd, 1)
                    dve.wait_ge(scores, done_at(i))
                    dve.wait_ge(kh_load[s], j * 16 + 16)
                    dve.wait_ge(ct, free_at(i))
                    link(dve.tensor_tensor(kh[:, s, :], psQ[s][:], kh[:, s, :], ALU.add))
                    dve.wait_ge(decd, done_at(i))
                    link(dve.tensor_tensor(cc[:, s, :], kh[:, s, :], dec[:, s, :], ALU.mult))
                    dve.sem_inc(qk_read, 1)
                    link(dve.tensor_reduce(tile_of(R.rowsum, i), cc[:, s, :].rearrange("p (h t) -> p h t", h=H0),
                                           AX_X, ALU.add))
                    dve.sem_inc(csum, 1)

                def back(i, s, j):
                    mid(i, s, j)
                skewed(dve, NT, front, back)

            @block.scalar
            def _(act):
                for q in (decd, ctm, hm):
                    act.sem_inc(q, 2)

                def front(i, s, j):
                    act.wait_ge(argd, done_at(i))
                    act.wait_ge(qk_read, free_at(i))
                    act.activation(dec[:, s, :], arg[:, s, :], ACT.Exp).then_inc(decd, 1)

                def back(i, s, j):
                    front(i, s, j)
                    act.wait_ge(ct, done_at(i))
                    act.activation(cT[:, s, :], psT[s][:], ACT.Copy).then_inc(ctm, 1)
                    act.wait_ge(hd, done_at(i))
                    act.activation(tile_of(R.Y, i), psH[s][:, 0:D], ACT.Copy).then_inc(hm, 1)
                two_slots(act, NT, back)


def stage_headnorm(nc, R, A):
    N = NT * H0
    with Stage(nc, "headnorm") as st:
        en, nrm, mu, var, t0 = (st.sb(n, [P, N]) for n in ("en", "nrm", "mu", "var", "t0"))
        w, b = st.sb("w", [P, D]), st.sb("b", [P, D])
        sq = st.sb("sq", [P, N * C0])
        loaded, chain, ex, ready, rooted, squared, cent = (
            st.sem(n) for n in ("loaded", "chain", "ex", "ready", "rooted", "squared", "cent"))
        y = R.Y[:].rearrange("p i (h c) -> p (i h) c", c=C0)
        with nc.Block() as block:
            @block.sync
            def _(sp):
                sp.dma_start(w[:], A["ln_w"].partition_broadcast(P)).then_inc(loaded, 16)
                sp.dma_start(b[:], A["ln_b"].partition_broadcast(P)).then_inc(loaded, 16)

            @block.vector
            def _(dve):
                link = Chain(dve, chain)
                rs, rm = (t[:].rearrange("p i h -> p (i h)") for t in (R.rowsum, R.rowmax))
                link(dve.tensor_tensor(t0[:], R.cs[:], rm, ALU.add))
                dve.sem_inc(ready, 1)
                link(dve.scalar_tensor_tensor(out=nrm[:], in0=rs, scalar=-1.0, in1=rs, op0=ALU.mult, op1=ALU.max))
                dve.wait_ge(ex, 1)
                link(dve.tensor_tensor(nrm[:], nrm[:], en[:], ALU.max))
                link(dve.tensor_scalar(nrm[:], nrm[:], 1e-6, None, ALU.add))
                link(dve.reciprocal(t0[:], nrm[:]))
                link(dve.tensor_tensor(y, y, bcast_in(t0[:], C0), ALU.mult))
                link(dve.tensor_reduce(mu[:], y, AX_X, ALU.add))
                link(dve.tensor_scalar(mu[:], mu[:], 1.0 / C0, None, ALU.mult))
                dve.tensor_tensor(y, y, bcast_in(mu[:], C0), ALU.subtract).then_inc(cent, 1)
                dve.wait_ge(squared, 1)
                link(dve.tensor_reduce(var[:], sq[:].rearrange("p (n c) -> p n c", c=C0), AX_X, ALU.add))
                link(dve.tensor_scalar(var[:], var[:], 1.0 / C0, LN_EPS, ALU.mult, ALU.add))
                dve.sem_inc(ready, 1)
                dve.wait_ge(rooted, 1)
                link(dve.reciprocal(var[:], t0[:]))
                dve.wait_ge(loaded, 32)
                link(dve.tensor_tensor(y, y, bcast_in(var[:], C0), ALU.mult))
                link(dve.tensor_scalar(w[:], w[:], 1.0, None, ALU.add))
                link(dve.tensor_tensor(R.Y[:], R.Y[:], bcast_mid(w[:], NT), ALU.mult))
                link(dve.tensor_tensor(R.Y[:], R.Y[:], bcast_mid(b[:], NT), ALU.add))
                link(dve.tensor_tensor(R.X[:], R.X[:], R.Y[:], ALU.add))

            @block.scalar
            def _(act):
                act.wait_ge(ready, 1)
                act.activation(en[:], t0[:], ACT.Exp, scale=-1.0).then_inc(ex, 1)
                act.wait_ge(cent, 1)
                act.activation(sq[:], R.Y[:].rearrange("p i d -> p (i d)"), ACT.Square).then_inc(squared, 1)
                act.wait_ge(ready, 2)
                act.activation(t0[:], var[:], ACT.Sqrt).then_inc(rooted, 1)


def stage_scan(nc, R, A):
    NB = B // 8
    with Stage(nc, "scan") as st:
        wx = st.sb("wx", [P, 3, P])
        uc = st.sb("uc", [P, 3, P])
        bias = st.sb("bias", [P, 4])
        cin = st.sb("cin", [P, 1])
        c = st.sb("c", [P, 2, S])
        gates = st.sb("gates", [P, 2, 3, S])
        fc, ig = st.sb("fc", [P, S]), st.sb("ig", [P, S])
        ps = [[st.ps(f"ps{k}_{q}", [P, 512]) for q in range(3)] for k in range(2)]
        loaded, start, cstep, gact, part, xpart, hstep, freed, zero = (
            st.sem(n) for n in ("loaded", "start", "cstep", "gact", "part", "xpart", "hstep", "freed", "zero"))
        with nc.Block() as block:
            @block.sync
            def _(sp):
                sp.dma_start(wx[:], A["lstm_wT"].rearrange("n i m -> i n m")[:, 0:3, :]).then_inc(loaded, 16)
                sp.dma_start(uc[:], A["lstm_uT"].rearrange("n i m -> i n m")[:, 0:3, :]).then_inc(loaded, 16)
                with nc.allow_non_contiguous_dma("bias columns"):
                    sp.dma_start(bias[:], A["lstm_bT"]).then_inc(loaded, 16)
                    sp.dma_start(cin[:], A["in_c"].rearrange("(p a) -> p a", a=1)).then_inc(loaded, 16)

            @block.vector
            def _(dve):
                dve.memset(c[:], 0.0).then_inc(zero, 1)
                dve.wait_ge(loaded, 64)
                dve.wait_ge(zero, 1)
                dve.tensor_scalar(c[:, 0, :], c[:, 0, :], cin[:, 0:1], None, ALU.add).then_inc(cstep, 1)

                def body(t, s, j):
                    dve.wait_ge(gact, t * 3 + 1 + 48)
                    dve.wait_ge(cstep, t + 1)
                    dve.tensor_tensor(fc[:], gates[:, s, 0, :], c[:, s, :], ALU.mult).then_inc(part, 1)
                    dve.wait_ge(gact, t * 3 + 3 + 48)
                    dve.tensor_tensor(ig[:], gates[:, s, 1, :], gates[:, s, 2, :], ALU.mult).then_inc(part, 1)
                    dve.wait_ge(part, t * 2 + 2)
                    dve.tensor_tensor(c[:, 1 - s, :], fc[:], ig[:], ALU.add).then_inc(cstep, 1)
                two_slots(dve, B, body)

            @block.tensor
            def _(pe):
                pe.wait_ge(loaded, 64)

                def xparts(n, s, j):
                    pe.wait_ge(gact, n * 24 + 24)
                    for q in range(3):
                        x = pe.matmul(ps[s][q][:], wx[:, q, :], R.XT[:, ds(n * 512, 512)],
                                      start=True, stop=False, skip_group_check=True)

                def steps(n, s, j):
                    for k in range(8):
                        t = n * 8 + k
                        pe.wait_ge(cstep, t + 1)
                        for q in range(3):
                            pe.matmul(ps[s][q][:, k * S:k * S + S], uc[:, q, :], c[:, k % 2, :], start=False,
                                      stop=True, skip_group_check=True).then_inc(hstep, 1)

                skewed(pe, NB, xparts, steps)

            @block.scalar
            def _(act):
                act.sem_inc(gact, 48)

                def steps(n, s, j):
                    for k in range(8):
                        t = n * 8 + k
                        for q, f in enumerate((ACT.Sigmoid, ACT.Sigmoid, ACT.Tanh)):
                            act.wait_ge(hstep, t * 3 + q + 1)
                            act.activation(gates[:, k % 2, q, :], ps[s][q][:, k * S:k * S + S], f,
                                           bias=bias[:, q:q + 1]).then_inc(gact, 1)
                two_slots(act, NB, steps)
        wo, uo = st.sb("wo", [P, P]), st.sb("uo", [P, P])
        hT = st.sb("hT", [P, 2, GW])
        cb = st.sb("cb", [P, S])
        ws = st.sem("ws")
        prod, tanhd, turned, added = (st.sem(n) for n in ("prod", "tanhd", "turned", "added"))
        with nc.Block() as block:
            @block.sync
            def _(sp):
                sp.dma_start(wo[:], A["lstm_wT"][3]).then_inc(ws, 16)
                sp.dma_start(uo[:], A["lstm_uT"][3]).then_inc(ws, 16)

            @block.tensor
            def _(pe):
                pe.sem_inc(prod, 2)
                pe.sem_inc(turned, 2)
                pe.wait_ge(ws, 32)

                def front(g, s, j):
                    pe.wait_ge(tanhd, free_at(g))
                    pe.matmul(ps[s][0][:], wo[:], R.XT[:, ds(g * GW, GW)], start=True, stop=False)
                    pe.matmul(ps[s][0][:].rearrange("p (b t) -> p b t", b=8), uo[:], bcast_mid(c[:, 0, :], 8),
                              start=False, stop=True).then_inc(prod, 1)

                def back(g, s, j):
                    pe.wait_ge(tanhd, done_at(g))
                    pe.wait_ge(added, free_at(g))
                    for k in range(4):
                        t = pe.transpose(ps[s][1][:, k * P:k * P + P], hT[:, s, k * P:k * P + P], R.ident[:])
                    t.then_inc(turned, 1)
                skewed(pe, NG, front, back)

            @block.scalar
            def _(act):
                act.sem_inc(tanhd, 2)

                def body(g, s, j):
                    act.wait_ge(prod, done_at(g))
                    act.wait_ge(turned, free_at(g))
                    act.activation(hT[:, s, :], ps[s][0][:], ACT.Tanh, bias=bias[:, 3:4]).then_inc(tanhd, 1)
                two_slots(act, NG, body)

            @block.vector
            def _(dve):
                dve.sem_inc(added, 2)

                def body(g, s, j):
                    dve.wait_ge(turned, done_at(g))
                    x = tiles_of(R.X, g * 4, 4)
                    dve.tensor_tensor(x, ps[s][1][:].rearrange("p (k d) -> p k d", k=4), x,
                                      ALU.add).then_inc(added, 1)
                two_slots(dve, NG, body)



def stage_attend(nc, R, A):
    NH = 8
    with Stage(nc, "attend") as st:
        wq, wk, wv = (st.sb(n, [P, H1 * C1]) for n in ("wq", "wk", "wv"))
        wo = st.sb("wo", [P, HP1, D])
        bq, bk, bv = (st.sb(n, [P, HP1]) for n in ("bq", "bk", "bv"))
        bo, row = st.sb("bo", [1, D]), st.sb("row", [1, D])
        xh = st.sb("xh", [P, 2, 4, P])
        xT = st.sb("xT", [P, GW])
        cT = st.sb("cT", [P, 2, GW])
        c2 = st.sb("c2", [P, 8, 2, S])
        qT = st.sb("qT", [P, HP1, GW])
        kbd = st.sb("kbd", [P, HP1, 8, 2, S])
        vbd = st.sb("vbd", [P, 8, HP1, 2, C1])
        top = st.sb("top", [P, 2, 8])
        tot, rs = st.sb("tot", [P, 2, 8]), st.sb("rs", [P, 2, 8])
        arg, pr, pT, o, oT = (st.sb(n, [P, 2, 512]) for n in ("arg", "pr", "pT", "o", "oT"))
        psA = [st.ps(f"psA{k}", [P, 512]) for k in range(2)]
        psS = [st.ps(f"psS{k}", [P, 512]) for k in range(2)]
        psP, psO, psV, psY = (st.ps(n, [P, 512]) for n in ("psP", "psO", "psV", "psY"))
        wload, cload = st.sem("wload"), [st.sem("cload0"), st.sem("cload1")]
        values_in = st.sem("values_in")
        normed, a_full, a_free, zero, rowd, rowm, biasd, group_s, group_v = (
            st.sem(n) for n in ("normed", "a_full", "a_free", "zero", "rowd", "rowm", "biasd", "group_s", "group_v"))
        s_done, argd, expd, sumd, ptd, ptm, pvd, od, otd, otm, yd, added, chain = (
            st.sem(n) for n in ("s_done", "argd", "expd", "sumd", "ptd", "ptm", "pvd", "od", "otd", "otm",
                                "yd", "added", "chain"))
        NA = 1 + 8 + 8 + 16
        heads = lambda ap: ap.rearrange("p (h t) -> p h t", h=8)
        with nc.Block() as block:
            @block.sync
            def _(sp):
                for w, a in ((wq, A["a1_wq"]), (wk, A["a1_wk"]), (wv, A["a1_wv"]), (wo, A["a1_wo"]), (bq, A["a1_bqT"]),
                             (bk, A["a1_bkT"]), (bv, A["a1_bvT"]), (bo, A["a1_bo"])):
                    sp.dma_start(w[:], a).then_inc(wload, 16)

                def body(g, s, j):
                    sp.wait_ge(group_s, free_at(g))
                    src = A["ctxT"][:, ds(g * GW, GW)]
                    sp.dma_start(cT[:, s, :], src).then_inc(cload[s], 16)
                    sp.wait_ge(values_in, g + 1)
                    for h in range(2):
                        sp.dma_start(c2[:, :, h, :], src.rearrange("p (b t) -> p b t", b=8)).then_inc(cload[s], 16)
                two_slots(sp, NG, body)

            @block.gpsimd
            def _(gp):
                gp.memset(kbd[:], 0.0).then_inc(zero, 1)
                gp.memset(vbd[:], 0.0).then_inc(zero, 1)

            @block.tensor
            def _(pe):
                pe.sem_inc(values_in, 1)
                for q in (s_done, group_s):
                    pe.sem_inc(q, 2)
                for q in (ptd, pvd, otd, yd):
                    pe.sem_inc(q, 2)
                pe.wait_ge(wload, 128)
                for h in range(HP1):
                    m = pe.matmul(psY[0:1, 0:D], bv[:, h:h + 1], wo[:, h, :], start=(h == 0), stop=(h == HP1 - 1))
                m.then_inc(rowd, 1)
                pe.wait_ge(rowm, 1)

                def body(g, s, j):
                    na = [0]

                    def bank():
                        pe.wait_ge(a_free, g * NA + na[0] + 1)
                        na[0] += 1
                        return psA[(s + na[0] - 1) % 2]

                    pe.wait_ge(normed, g + 1)
                    b = bank()
                    for k in range(4):
                        t = pe.transpose(b[:, k * P:k * P + P], xh[:, s, k, :], R.ident[:])
                    t.then_inc(a_full, 1)
                    pe.wait_ge(cload[s], j * 48 + 48)
                    for h in range(HP1):
                        b = bank()
                        pe.matmul(b[:], wk[:, h * P:h * P + P], cT[:, s, :], start=True, stop=True).then_inc(a_full, 1)
                    pe.wait_ge(a_free, g * NA + 1 + 2)
                    for h in range(HP1):
                        b = bank()
                        pe.matmul(b[:], wq[:, h * P:h * P + P], xT[:], start=True, stop=True).then_inc(a_full, 1)
                    for n in range(8):
                        for h in range(2):
                            b = bank()
                            pe.matmul(b[:], c2[:, n, :, :].rearrange("p a t -> p (a t)"), wv[:, h * 512:h * 512 + 512], start=True,
                                      stop=True).then_inc(a_full, 1)
                    pe.wait_ge(a_free, g * NA + NA + 2)
                    pe.sem_inc(values_in, 1)

                    def scores(n):
                        pe.wait_ge(argd, g * NH + n + 1)
                        for b in range(2):
                            for k in range(4):
                                h, nb = (n % 2) * 4 + k, (n // 2) * 2 + b
                                m = pe.matmul(psS[n % 2][64 * b:64 * b + 64, k * P:k * P + P],
                                              qT[:, h, nb * S:nb * S + S],
                                              kbd[:, h, nb, :, :].rearrange("p a t -> p (a t)"),
                                              start=True, stop=True)
                        m.then_inc(s_done, 1)

                    def turn_p(n):
                        pe.wait_ge(expd, g * NH + n + 1 + 2)
                        pe.wait_ge(ptm, g * NH + n + 1)
                        for k in range(4):
                            t = pe.transpose(psP[:, k * P:k * P + P], pr[:, n % 2, k * P:k * P + P], R.ident[:])
                        t.then_inc(ptd, 1)

                    def values(n):
                        pe.wait_ge(ptm, g * NH + n + 1 + 1)
                        pe.wait_ge(od, g * NH + n + 2)
                        for b in range(2):
                            for k in range(4):
                                h, nb = (n % 2) * 4 + k, (n // 2) * 2 + b
                                m = pe.matmul(psV[64 * b:64 * b + 64, k * P:k * P + P],
                                              pT[:, n % 2, k * P + 64 * b:k * P + 64 * b + 64],
                                              vbd[:, nb, h, :, :].rearrange("p a t -> p (a t)"),
                                              start=True, stop=True)
                        m.then_inc(pvd, 1)

                    def turn_o(n):
                        pe.wait_ge(od, g * NH + n + 3)
                        pe.wait_ge(otm, g * NH + n + 1)
                        for k in range(4):
                            t = pe.transpose(psO[:, k * P:k * P + P], o[:, n % 2, k * P:k * P + P], R.ident[:])
                        t.then_inc(otd, 1)

                    def project(n):
                        pe.wait_ge(otm, g * NH + n + 1 + 1)
                        if n % 2 == 0:
                            pe.wait_ge(added, g * 4 + n // 2 + 1)
                            pe.matmul(psY[:, 0:D], R.ones[0:1, 0:P], row[:], start=True, stop=False)
                        for k in range(4):
                            m = pe.matmul(psY[:, 0:D], oT[:, n % 2, k * P:k * P + P], wo[:, (n % 2) * 4 + k, :],
                                          start=False, stop=(n % 2 == 1 and k == 3))
                        m.then_inc(yd, 1)

                    for n in range(NH + 4):
                        for lag, step in enumerate((scores, turn_p, values, turn_o, project)):
                            if 0 <= n - lag < NH:
                                step(n - lag)
                    pe.wait_ge(yd, g * NH + NH + 2)
                    pe.sem_inc(group_s, 1)
                two_slots(pe, NG, body)

            @block.scalar
            def _(act):
                act.sem_inc(a_free, 2)
                act.sem_inc(expd, 2)
                act.sem_inc(ptm, 1)
                act.sem_inc(otm, 1)
                act.wait_ge(rowd, 1)
                act.wait_ge(zero, 2)
                act.wait_ge(biasd, 1)

                def body(g, s, j):
                    na = [0]

                    def moved(src, dsts, **kw):
                        act.wait_ge(a_full, g * NA + na[0] + 1)
                        for dst, rows in dsts:
                            f = ACT.Identity if kw else ACT.Copy
                            bias = {"bias": kw["bias"][rows, :]} if kw else {}
                            if kw.get("scale"):
                                bias["scale"] = kw["scale"]
                            m = act.activation(dst, src(psA[(s + na[0]) % 2][rows, :]), f, **bias)
                        m.then_inc(a_free, 1)
                        na[0] += 1

                    allr, lo, hi = slice(0, P), slice(0, 64), slice(64, P)
                    same = lambda ap: ap
                    moved(same, [(xT[:], allr)])
                    toks = lambda ap: ap.rearrange("p (b t) -> p b t", b=8)
                    for h in range(HP1):
                        moved(toks, [(kbd[lo, h, :, 0, :], lo), (kbd[hi, h, :, 1, :], hi)], bias=bk[:, h:h + 1])
                    for h in range(HP1):
                        moved(same, [(qT[:, h, :], allr)], bias=bq[:, h:h + 1], scale=C1 ** -0.5)
                    for n in range(8):
                        for h in range(2):
                            act.wait_ge(a_full, g * NA + na[0] + 1)
                            src = psA[(s + na[0]) % 2][:].rearrange("p (k a d) -> p k a d", k=4, a=2)
                            act.activation(vbd[lo, n, 4 * h:4 * h + 4, 0, :], src[lo, :, 0, :], ACT.Copy)
                            act.activation(vbd[hi, n, 4 * h:4 * h + 4, 1, :], src[hi, :, 1, :],
                                           ACT.Copy).then_inc(a_free, 1)
                            na[0] += 1

                    def exps(n):
                        act.wait_ge(argd, g * NH + n + 1 + 2)
                        act.wait_ge(ptd, g * NH + n + 1)
                        act.wait_ge(sumd, g * NH + n + 1)
                        act.activation(pr[:, n % 2, :], arg[:, n % 2, :], ACT.Exp).then_inc(expd, 1)

                    def move_p(n):
                        act.wait_ge(ptd, g * NH + n + 1 + 2)
                        act.wait_ge(pvd, g * NH + n + 1)
                        act.activation(pT[:, n % 2, :], psP[:], ACT.Copy).then_inc(ptm, 1)

                    def move_o(n):
                        act.wait_ge(otd, g * NH + n + 1 + 2)
                        act.wait_ge(yd, g * NH + n + 1)
                        act.activation(oT[:, n % 2, :], psO[:], ACT.Copy).then_inc(otm, 1)

                    for n in range(NH + 3):
                        for lag, step in enumerate((exps, move_p, None, move_o)):
                            if step and 0 <= n - lag < NH:
                                step(n - lag)
                two_slots(act, NG, body)

            @block.vector
            def _(dve):
                dve.sem_inc(argd, 2)
                dve.sem_inc(sumd, 2)
                dve.sem_inc(od, 2)
                dve.sem_inc(added, 1)
                dve.wait_ge(rowd, 1)
                dve.tensor_tensor(row[:], psY[0:1, 0:D], bo[:], ALU.add).then_inc(rowm, 1)
                dve.tensor_scalar(bq[:], bq[:], C1 ** -0.5, None, ALU.mult).then_inc(biasd, 1)

                def norm(g, s, j):
                    dve.wait_ge(group_s, free_at(g))
                    for k in range(4):
                        i = g * 4 + k
                        m = dve.tensor_scalar(xh[:, s, k, :], tile_of(R.X, i), R.mean[:, ds(i, 1)],
                                              R.rstd[:, ds(i, 1)], ALU.subtract, ALU.mult)
                    m.then_inc(normed, 1)

                def body(g, s, j):
                    link = Chain(dve, chain, g * NH * 2)

                    def soft(n):
                        dve.wait_ge(s_done, g * NH + n + 1 + 2)
                        dve.wait_ge(argd, g * NH + n + 1)
                        link(dve.tensor_reduce(top[:, n % 2, :], heads(psS[n % 2][:]), AX_X, ALU.max))
                        dve.wait_ge(expd, g * NH + n + 1)
                        dve.tensor_tensor(heads(arg[:, n % 2, :]), heads(psS[n % 2][:]),
                                          bcast_in(top[:, n % 2, :], S), ALU.subtract).then_inc(argd, 1)

                    def sums(n):
                        dve.wait_ge(expd, g * NH + n + 1 + 2)
                        dve.wait_ge(od, g * NH + n + 1)
                        link(dve.tensor_reduce(tot[:, n % 2, :], heads(pr[:, n % 2, :]), AX_X, ALU.add))
                        dve.reciprocal(rs[:, n % 2, :], tot[:, n % 2, :]).then_inc(sumd, 1)

                    def scale(n):
                        dve.wait_ge(pvd, g * NH + n + 1 + 2)
                        dve.wait_ge(sumd, g * NH + n + 1 + 2)
                        dve.wait_ge(otd, g * NH + n + 1)
                        dve.tensor_tensor(heads(o[:, n % 2, :]), heads(psV[:]), bcast_in(rs[:, n % 2, :], C1),
                                          ALU.mult).then_inc(od, 1)

                    def add(n):
                        if n % 2:
                            i = g * 4 + n // 2
                            dve.wait_ge(yd, g * NH + n + 1 + 2)
                            dve.tensor_tensor(tile_of(R.X, i), psY[:, 0:D], tile_of(R.X, i), ALU.add).then_inc(added, 1)

                    for n in range(NH + 4):
                        for lag, step in enumerate((soft, sums, scale, None, add)):
                            if step and 0 <= n - lag < NH:
                                step(n - lag)
                skewed(dve, NG, norm, body)


def stage_logits(nc, R, A, name, w_dram, E):
    with Stage(nc, name) as st:
        w = st.sb("w", [P, E])
        xs = st.sb("xs", [P, 2, P])
        ps = [st.ps(f"ps{k}", [P, 512]) for k in range(2)]
        wload, xload = st.sem("wload"), [st.sem("xload0"), st.sem("xload1")]
        prod, moved = st.sem("prod"), st.sem("moved")
        with nc.Block() as block:
            @block.sync
            def _(sp):
                sp.dma_start(w[:], w_dram).then_inc(wload, 16)

                def body(i, s, j):
                    sp.wait_ge(prod, free_at(i))
                    sp.dma_start(xs[:, s, :], R.XT[:, ds(i * P, P)]).then_inc(xload[s], 16)
                two_slots(sp, NT, body)

            @block.tensor
            def _(pe):
                pe.sem_inc(prod, 2)
                pe.wait_ge(wload, 16)

                def body(i, s, j):
                    pe.wait_ge(xload[s], j * 16 + 16)
                    pe.wait_ge(moved, free_at(i))
                    pe.matmul(ps[s][:, 0:E], xs[:, s, :], w[:], start=True, stop=True).then_inc(prod, 1)
                two_slots(pe, NT, body)

            @block.scalar
            def _(act):
                act.sem_inc(moved, 2)

                def body(i, s, j):
                    act.wait_ge(prod, done_at(i))
                    act.activation(R.lg[:, ds(i * E, E)], ps[s][:, 0:E], ACT.Copy).then_inc(moved, 1)
                two_slots(act, NT, body)


def stage_route(nc, R, name, E, two, capacity):
    N = NT * E
    with Stage(nc, name) as st:
        rev, eq, hot0, hot1, lg2 = (st.sb(n, [P, w]) for n, w in (
            ("rev", E), ("eq", N), ("hot0", N), ("hot1", N), ("lg2", N)))
        m0, m1, r, ex, w0, w1 = (st.sb(n, [P, NT]) for n in ("m0", "m1", "r", "ex", "w0", "w1"))
        ps = st.ps("ps", [P, 512])
        chain, ready, exd, revd, pos = (st.sem(n) for n in ("chain", "ready", "exd", "revd", "pos"))
        v = lambda t: t.rearrange("p (i e) -> p i e", e=E)
        with nc.Block() as block:
            @block.gpsimd
            def _(gp):
                gp.iota(rev[:].bitcast(I32), pattern=[[-1, E]], base=E, channel_multiplier=0).then_inc(revd, 1)

            @block.vector
            def _(dve):
                link = Chain(dve, chain)
                dve.wait_ge(revd, 1)
                link(dve.tensor_copy(rev[:], rev[:].bitcast(I32)))

                def first_largest(lg, m, hot):
                    link(dve.tensor_reduce(m[:], v(lg), AX_X, ALU.max))
                    link(dve.tensor_tensor(v(eq[:]), v(lg), bcast_in(m[:], E), ALU.is_equal))
                    link(dve.tensor_tensor(v(eq[:]), v(eq[:]), bcast_mid(rev[:], NT), ALU.mult))
                    link(dve.tensor_reduce(r[:], v(eq[:]), AX_X, ALU.max))
                    link(dve.tensor_tensor(v(hot), v(eq[:]), bcast_in(r[:], E), ALU.is_equal))

                first_largest(R.lg[:, 0:N], m0, hot0[:] if two else R.wt[:, 0:N])
                if two:
                    link(dve.scalar_tensor_tensor(out=lg2[:], in0=hot0[:], scalar=-3e38, in1=R.lg[:, 0:N],
                                                  op0=ALU.mult, op1=ALU.add))
                    first_largest(lg2[:], m1, hot1[:])
                    dve.tensor_tensor(m1[:], m1[:], m0[:], ALU.subtract).then_inc(ready, 1)
                    dve.wait_ge(exd, 1)
                    link(dve.tensor_scalar(w0[:], ex[:], 1.0, None, ALU.add))
                    link(dve.reciprocal(w1[:], w0[:]))
                    link(dve.tensor_tensor(w0[:], ex[:], w1[:], ALU.mult))
                    link(dve.tensor_tensor(lg2[:], hot0[:], hot1[:], ALU.add))
                    dve.sem_inc(ready, 1)
                    link(dve.tensor_tensor(v(hot0[:]), v(hot0[:]), bcast_in(w1[:], E), ALU.mult))
                    link(dve.tensor_tensor(v(hot1[:]), v(hot1[:]), bcast_in(w0[:], E), ALU.mult))
                    link(dve.tensor_tensor(R.wt[:, 0:N], hot0[:], hot1[:], ALU.add))
                    if capacity:
                        dve.wait_ge(pos, 1)
                        link(dve.tensor_scalar(eq[:], ps[:], float(capacity), None, ALU.is_lt))
                        link(dve.tensor_tensor(R.wt[:, 0:N], R.wt[:, 0:N], eq[:], ALU.mult))

            if two:
                @block.scalar
                def _(act):
                    act.wait_ge(ready, 1)
                    act.activation(ex[:], m1[:], ACT.Exp).then_inc(exd, 1)

            if capacity:
                @block.tensor
                def _(pe):
                    pe.wait_ge(ready, 2)
                    pe.matmul(ps[:], R.tri_strict[:], lg2[:], start=True, stop=True).then_inc(pos, 1)


def stage_experts1(nc, R, A):
    with Stage(nc, "experts1") as st:
        we = st.sb("we", [P, E1 * D])
        xs = st.sb("xs", [P, 2, P])
        acc = st.sb("acc", [P, 2, D])
        ps = [[st.ps(f"ps{k}_{h}", [P, 512]) for h in range(2)] for k in range(2)]
        wload, xload = st.sem("wload"), [st.sem("xload0"), st.sem("xload1")]
        prod, used, chain = st.sem("prod"), st.sem("used"), st.sem("chain")
        with nc.Block() as block:
            @block.sync
            def _(sp):
                sp.dma_start(we[:].rearrange("p (e f) -> p e f", e=E1), A["f1_we"].rearrange("e d f -> d e f")
                             ).then_inc(wload, 16)

                def body(i, s, j):
                    sp.wait_ge(prod, free_at(i))
                    sp.dma_start(xs[:, s, :], R.XT[:, ds(i * P, P)]).then_inc(xload[s], 16)
                two_slots(sp, NT, body)

            @block.tensor
            def _(pe):
                pe.sem_inc(prod, 2)
                pe.wait_ge(wload, 16)

                def body(i, s, j):
                    pe.wait_ge(xload[s], j * 16 + 16)
                    pe.wait_ge(used, i + 1)
                    for h in range(2):
                        m = pe.matmul(ps[s][h][:], xs[:, s, :], we[:, h * 512:h * 512 + 512], start=True, stop=True)
                    m.then_inc(prod, 1)
                two_slots(pe, NT, body)

            @block.vector
            def _(dve):
                dve.sem_inc(used, 2)
                dve.sem_inc(chain, 2)

                def body(i, s, j):
                    dve.wait_ge(prod, done_at(i))
                    for e in range(E1):
                        dve.wait_ge(chain, i * 9 + max(e + 1, 2))
                        prev = tile_of(R.X, i) if e == 0 else acc[:, e % 2, :]
                        src = ps[s][e // 4][:, (e % 4) * D:(e % 4) * D + D]
                        w = R.wt[:, ds(i * E1 + e, 1)]
                        if e == 1:
                            m = dve.tensor_scalar(acc[:, 1, :], src, w, None, ALU.mult)
                        else:
                            m = dve.scalar_tensor_tensor(out=acc[:, e % 2, :], in0=src, scalar=w, in1=prev,
                                                         op0=ALU.mult, op1=ALU.add)
                        m.then_inc(chain, 1)
                    dve.wait_ge(chain, i * 9 + E1 + 2)
                    dve.sem_inc(used, 1)
                    dve.tensor_tensor(tile_of(R.X, i), acc[:, 0, :], acc[:, 1, :], ALU.add).then_inc(chain, 1)
                two_slots(dve, NT, body)


def stage_linear2(nc, R, A):
    W = D + H2
    EK, EL = 1e-6, 1e-6
    with Stage(nc, "linear2") as st:
        w3 = st.sb("w3", [P, 3, D])
        dw = st.sb("dw", [P, C2, D])
        db = st.sb("db", [1, D])
        gm, bt = st.sb("gm", [P, D]), st.sb("bt", [P, D])
        em = st.sb("em", [P, NT])
        mask = st.sb("mask", [P, W])
        cT = st.sb("cT", [P, 2, P])
        xh, xT = st.sb("xh", [P, 2, P]), st.sb("xT", [P, 2, P])
        n3 = st.sb("n3", [P, 2, 3, D])
        s6, mv, sd, rr = (st.sb(n, [P, 2, 3, w]) for n, w in (("s6", 6), ("mv", 2), ("sd", 1), ("rr", 1)))
        n3b = st.sb("n3b", [P, 2, 3, D])
        va = st.sb("va", [P, 2, W])
        kvm = st.sb("kvm", [P, 2, 2, W])
        qT, at = st.sb("qT", [P, 2, P]), st.sb("at", [P, 2, P])
        spread = st.sb("spread", [P, 2, C2, 2, H2, 4])
        den = st.sb("den", [P, 2, H2])
        rd = st.sb("rd", [P, 2, H2])
        o1, o2 = st.sb("o1", [P, 2, D]), st.sb("o2", [P, 2, D])
        t6, tv, ts, tr = (st.sb(n, [P, 2, w]) for n, w in (("t6", 6), ("tv", 2), ("ts", 1), ("tr", 1)))
        psX, psQ, psT, psA, psO = (st.ps(n, [P, 512]) for n in ("psX", "psQ", "psT", "psA", "psO"))
        psK = st.ps("psK", [P, 2, 512])
        wload, xload = st.sem("wload"), [st.sem("xload0"), st.sem("xload1")]
        names = ("ready", "normed", "xt", "xm", "proj", "varr", "root", "n3d", "gdone", "feat", "kvd", "kvmd", "qt",
                 "qm", "attd", "atn", "spreadd", "outd", "var2", "root2", "od1", "od2", "chain", "va_set",
                 "stats_in")
        q = {n: st.sem(n) for n in names}
        with nc.Block() as block:
            @block.sync
            def _(sp):
                for n, a in enumerate((A["l2_wq"], A["l2_wk"], A["l2_wv"])):
                    sp.dma_start(w3[:, n, :], a).then_inc(wload, 16)
                sp.dma_start(dw[:], A["l2_dw"]).then_inc(wload, 16)
                sp.dma_start(db[:], A["l2_db"]).then_inc(wload, 16)
                sp.dma_start(gm[:], A["l2_g"].partition_broadcast(P)).then_inc(wload, 16)
                sp.dma_start(bt[:], A["l2_b"].partition_broadcast(P)).then_inc(wload, 16)
                sp.dma_start(em[:], A["l2_mask"]).then_inc(wload, 16)

                def body(i, s, j):
                    sp.wait_ge(q["proj"], free_at(i))
                    sp.dma_start(cT[:, s, :], A["ctxT"][:, ds(i * P, P)]).then_inc(xload[s], 16)
                two_slots(sp, NT, body)

            @block.tensor
            def _(pe):
                for z in (q["xt"], q["proj"], q["kvd"], q["qt"], q["attd"], q["outd"]):
                    pe.sem_inc(z, 2)
                pe.wait_ge(wload, 128)

                def front(i, s, j):
                    pe.wait_ge(q["normed"], i + 1)
                    pe.wait_ge(q["xm"], i + 1)
                    pe.transpose(psX[:, 0:P], xh[:, s, :], R.ident[:]).then_inc(q["xt"], 1)
                    pe.wait_ge(q["xm"], i + 2)
                    pe.wait_ge(xload[s], j * 16 + 16)
                    pe.wait_ge(q["n3d"], i + 1)
                    pe.matmul(psQ[:, 0:D], xT[:, s, :], w3[:, 0, :], start=True, stop=True)
                    pe.matmul(psQ[:, D:3 * D], cT[:, s, :], w3[:, 1:3, :].rearrange("p a d -> p (a d)"), start=True,
                              stop=True).then_inc(q["proj"], 1)

                def back(i, s, j):
                    pe.wait_ge(q["feat"], i + 1)
                    pe.wait_ge(q["kvmd"], i + 1)
                    for b in range(2):
                        r = slice(64 * b, 64 * b + 64)
                        m = pe.matmul(psK[:, b, 0:W], n3b[r, s, 1, :], va[r, s, :], start=True, stop=True)
                    m.then_inc(q["kvd"], 1)
                    pe.wait_ge(q["qm"], i + 1)
                    pe.transpose(psT[:, 0:P], n3b[:, s, 0, :], R.ident[:]).then_inc(q["qt"], 1)
                    pe.wait_ge(q["qm"], i + 2)
                    pe.wait_ge(q["kvmd"], i + 2)
                    pe.wait_ge(q["atn"], i + 1)
                    for b in range(2):
                        m = pe.matmul(psA[64 * b:64 * b + 64, 0:W], qT[:, s, 64 * b:64 * b + 64], kvm[:, s, b, :],
                                      start=True, stop=True)
                    m.then_inc(q["attd"], 1)
                    pe.wait_ge(q["spreadd"], i + 1)
                    pe.wait_ge(q["od1"], i + 1)
                    for e in range(C2):
                        pe.matmul(psO[:, 0:D], spread[:, s, e, :, :, :].rearrange("p b h n -> p (b h n)"), dw[:, e, :],
                                  start=(e == 0), stop=False)
                    pe.matmul(psO[:, 0:D], R.ones[0:1, 0:P], db[:], start=False, stop=True).then_inc(q["outd"], 1)
                skewed(pe, NT, front, back)

            @block.scalar
            def _(act):
                act.sem_inc(q["xm"], 1)
                act.sem_inc(q["qm"], 1)

                def front(i, s, j):
                    act.wait_ge(q["xt"], done_at(i))
                    act.wait_ge(q["proj"], free_at(i))
                    act.activation(xT[:, s, :], psX[:, 0:P], ACT.Copy).then_inc(q["xm"], 1)
                    act.wait_ge(q["varr"], i + 1)
                    act.activation(sd[:, s, :, :].rearrange("p a b -> p (a b)"), mv[:, s, :, 1], ACT.Sqrt).then_inc(q["root"], 1)

                def back(i, s, j):
                    act.wait_ge(q["qt"], done_at(i))
                    act.wait_ge(q["attd"], free_at(i))
                    act.activation(qT[:, s, :], psT[:, 0:P], ACT.Copy).then_inc(q["qm"], 1)
                    act.wait_ge(q["var2"], i + 1)
                    act.activation(ts[:, s, :], tv[:, s, 1:2], ACT.Sqrt).then_inc(q["root2"], 1)
                skewed(act, NT, front, back)

            @block.gpsimd
            def _(gp):
                gp.sem_inc(q["gdone"], 2)
                gp.wait_ge(wload, 128)

                def body(i, s, j):
                    gp.wait_ge(q["n3d"], i + 2)
                    gp.tensor_tensor(n3[:, s, :, :], n3[:, s, :, :], bcast_mid(gm[:], 3), ALU.mult).then_inc(q["va_set"], 1)
                    gp.wait_ge(q["va_set"], i + 2)
                    gp.tensor_tensor(n3[:, s, :, :], n3[:, s, :, :], bcast_mid(bt[:], 3), ALU.add).then_inc(q["gdone"], 1)
                two_slots(gp, NT, body)

            @block.vector
            def _(dve):
                for z in (q["n3d"], q["kvmd"], q["atn"], q["od1"]):
                    dve.sem_inc(z, 1)
                dve.tensor_copy(mask[:, 0:D], R.bd8[:].rearrange("p a b -> p (a b)")).then_inc(q["ready"], 1)
                dve.tensor_copy(mask[:, D:W], R.bd8[:, :, 0]).then_inc(q["ready"], 1)
                for s in range(2):
                    dve.memset(va[:, s, D:W], 1.0).then_inc(q["ready"], 1)
                dve.wait_ge(q["ready"], 4)
                dve.sem_inc(q["va_set"], 1)
                dve.wait_ge(wload, 128)
                KF, KB = 9, 9

                def front(i, s, j):
                    link = Chain(dve, q["chain"], i * KF)
                    dve.wait_ge(q["xt"], free_at(i))
                    dve.tensor_scalar(xh[:, s, :], tile_of(R.X, i), R.mean[:, ds(i, 1)], R.rstd[:, ds(i, 1)],
                                      ALU.subtract, ALU.mult).then_inc(q["normed"], 1)
                    dve.wait_ge(q["proj"], done_at(i))
                    for n in range(3):
                        dve.bn_stats(s6[:, s, n, :], psQ[:, n * D:n * D + D]).then_inc(q["chain"], 1)
                    dve.wait_ge(q["chain"], i * KF + 3)
                    dve.sem_inc(q["stats_in"], 1)
                    for n in range(3):
                        dve.bn_aggr(mv[:, s, n, :], s6[:, s, n, :]).then_inc(q["chain"], 1)
                    dve.wait_ge(q["chain"], i * KF + 6)
                    dve.tensor_scalar(mv[:, s, :, 1], mv[:, s, :, 1], EL, None, ALU.add).then_inc(q["varr"], 1)
                    dve.wait_ge(q["root"], i + 1)
                    dve.reciprocal(rr[:, s, :, :].rearrange("p a b -> p (a b)"),
                                   sd[:, s, :, :].rearrange("p a b -> p (a b)")).then_inc(q["chain"], 1)
                    dve.wait_ge(q["chain"], i * KF + 7)
                    for n in range(3):
                        m = dve.tensor_scalar(n3[:, s, n, :], psQ[:, n * D:n * D + D], mv[:, s, n, 0:1],
                                              rr[:, s, n, :], ALU.subtract, ALU.mult)
                        if n < 2:
                            m.then_inc(q["chain"], 1)
                    m.then_inc(q["n3d"], 1)

                def back(i, s, j):
                    link = Chain(dve, q["ready"], i * KB + 4)
                    dve.wait_ge(q["gdone"], done_at(i))
                    dve.wait_ge(q["kvd"], free_at(i))
                    dve.wait_ge(q["qt"], free_at(i))
                    link(dve.tensor_scalar(n3b[:, s, 0:2, :], n3[:, s, 0:2, :], 0.0, EK, ALU.max, ALU.add))
                    link(dve.tensor_scalar(n3b[:, s, 1, :], n3b[:, s, 1, :], em[:, ds(i, 1)], None, ALU.mult))
                    dve.tensor_scalar(va[:, s, 0:D], n3[:, s, 2, :], em[:, ds(i, 1)], None,
                                      ALU.mult).then_inc(q["feat"], 1)
                    dve.wait_ge(q["kvd"], done_at(i))
                    dve.wait_ge(q["attd"], free_at(i))
                    kv = psK[:, :, 0:W]
                    dve.tensor_tensor(kvm[:, s, :, :], kv, bcast_mid(mask[:], 2), ALU.mult).then_inc(q["kvmd"], 1)
                    dve.wait_ge(q["attd"], done_at(i))
                    link(dve.tensor_scalar(den[:, s, :], psA[:, D:W], EK, None, ALU.add))
                    link(dve.reciprocal(rd[:, s, :], den[:, s, :]))
                    dve.tensor_tensor(at[:, s, :].rearrange("p (h c) -> p h c", h=H2),
                                      psA[:, 0:D].rearrange("p (h c) -> p h c", h=H2),
                                      bcast_in(rd[:, s, :], C2), ALU.mult).then_inc(q["atn"], 1)
                    dve.wait_ge(q["atn"], i + 2)
                    dve.wait_ge(q["outd"], free_at(i))
                    for b in range(2):
                        m = dve.tensor_tensor(spread[:, s, :, b, :, :],
                                              at[:, s, :].rearrange("p (h e a) -> p e h a", h=H2, a=1)
                                              .broadcast_to([P, C2, H2, 4]),
                                              R.bd16[:, 4 * b:4 * b + 4].rearrange("p (x y n) -> p x y n", x=1, y=1)
                                              .broadcast_to([P, C2, H2, 4]), ALU.mult)
                    m.then_inc(q["spreadd"], 1)
                    dve.wait_ge(q["outd"], done_at(i))
                    link(dve.bn_stats(t6[:, s, :], psO[:, 0:D]))
                    dve.sem_inc(q["stats_in"], 1)
                    link(dve.bn_aggr(tv[:, s, :], t6[:, s, :]))
                    dve.tensor_scalar(tv[:, s, 1:2], tv[:, s, 1:2], EL, None, ALU.add).then_inc(q["var2"], 1)
                    dve.wait_ge(q["root2"], i + 1)
                    link(dve.reciprocal(tr[:, s, :], ts[:, s, :]))
                    dve.tensor_scalar(o1[:, s, :], psO[:, 0:D], tv[:, s, 0:1], tr[:, s, :], ALU.subtract,
                                      ALU.mult).then_inc(q["od1"], 1)
                    dve.wait_ge(q["od1"], i + 2)
                    link(dve.tensor_tensor(o2[:, s, :], o1[:, s, :], gm[:], ALU.mult))
                    link(dve.tensor_tensor(o2[:, s, :], o2[:, s, :], bt[:], ALU.add))
                    dve.tensor_tensor(tile_of(R.X, i), o2[:, s, :], tile_of(R.X, i), ALU.add)
                skewed(dve, NT, front, back)


def stage_experts2(nc, R, A):
    NC = I2 // P
    with Stage(nc, "experts2") as st:
        w1 = st.sb("w1", [P, E2, I2])
        b1 = st.sb("b1", [E2, I2])
        wo = st.sb("wo", [P, NC, D])
        bo = st.sb("bo", [1, D])
        xh = st.sb("xh", [P, 2, 4, D])
        xm = st.sb("xm", [P, 2, E2, D])
        xmT = st.sb("xmT", [P, 2, E2, 4, P])
        hots = st.sb("hots", [P, 2, 4, E2])
        hotT = st.sb("hotT", [E2, 2, GW])
        hT = st.sb("hT", [P, 2, NC, GW])
        psT, psH, psY = ([st.ps(f"{n}{k}", [P, 512]) for k in range(2)] for n in ("psT", "psH", "psY"))
        psB = st.ps("psB", [P, 512])
        wload = st.sem("wload")
        normed, masked, turned, tmoved, hot, hotm, hid, act_d, yd, added = (
            st.sem(n) for n in ("normed", "masked", "turned", "tmoved", "hot", "hotm", "hid", "act_d", "yd", "added"))
        with nc.Block() as block:
            @block.sync
            def _(sp):
                sp.dma_start(w1[:], A["f2_w1"].rearrange("e d i -> d e i")).then_inc(wload, 16)
                sp.dma_start(b1[:], A["f2_b1"]).then_inc(wload, 16)
                sp.dma_start(wo[:], A["f2_wo"].rearrange("(c p) d -> p c d", p=P)).then_inc(wload, 16)
                sp.dma_start(bo[:], A["f2_bo"]).then_inc(wload, 16)

            @block.vector
            def _(dve):
                dve.sem_inc(added, 2)

                def front(g, s, j):
                    dve.wait_ge(added, g + 1)
                    dve.wait_ge(turned, g * 4 + 1)
                    dve.tensor_copy(hots[:, s, :, :].rearrange("p k e -> p (k e)"), R.wt[:, ds(g * 4 * E2, 4 * E2)])
                    for k in range(4):
                        i = g * 4 + k
                        n = dve.tensor_scalar(xh[:, s, k, :], tile_of(R.X, i), R.mean[:, ds(i, 1)],
                                              R.rstd[:, ds(i, 1)], ALU.subtract, ALU.mult)
                    n.then_inc(normed, 1)
                    dve.wait_ge(normed, g + 1)
                    for k in range(4):
                        dve.wait_ge(turned, g * 4 + k + 1)
                        dve.tensor_tensor(xm[:, k % 2, :, :], bcast_mid(xh[:, s, k, :], E2),
                                          bcast_in(R.wt[:, ds((g * 4 + k) * E2, E2)], D), ALU.mult
                                          ).then_inc(masked, 1)

                def back(g, s, j):
                    dve.wait_ge(yd, done_at(g))
                    dve.tensor_tensor(tiles_of(R.Y, g * 4, 4), psY[s][:].rearrange("p (k d) -> p k d", k=4),
                                      xh[:, s, :, :], ALU.add).then_inc(added, 1)
                skewed(dve, NG, front, back)

            @block.tensor
            def _(pe):
                pe.sem_inc(turned, 2)
                pe.sem_inc(hot, 1)
                pe.sem_inc(hid, 2)
                pe.sem_inc(yd, 2)
                pe.wait_ge(wload, 64)

                def first(g, s, j):
                    pe.wait_ge(hotm, g + 1)
                    pe.wait_ge(normed, g + 1)
                    for k in range(4):
                        t = pe.transpose(psB[0:E2, k * P:k * P + P], hots[:, s, k, :], R.ident[:])
                    t.then_inc(hot, 1)
                    for k in range(4):
                        pe.wait_ge(masked, g * 4 + k + 1)
                        pe.wait_ge(tmoved, g * 4 + k + 1)
                        for e in range(E2):
                            t = pe.transpose(psT[k % 2][:, e * P:e * P + P], xm[:, k % 2, e, :], R.ident[:])
                        t.then_inc(turned, 1)

                def second(g, s, j):
                    pe.wait_ge(tmoved, g * 4 + 4 + 2)
                    pe.wait_ge(hotm, g + 1 + 1)
                    for c in range(NC):
                        pe.wait_ge(act_d, g * NC + c + 1)
                        cols = slice(c * P, c * P + P)
                        for e in range(E2):
                            pe.matmul(psH[c % 2][:], w1[:, e, cols], xmT[:, s, e, :, :].rearrange("p k t -> p (k t)"),
                                      start=(e == 0), stop=False)
                        pe.matmul(psH[c % 2][:], b1[:, cols], hotT[:, s, :], start=False, stop=True).then_inc(hid, 1)

                def third(g, s, j):
                    pe.wait_ge(act_d, g * NC + NC + 2)
                    pe.wait_ge(added, free_at(g))
                    for k in range(4):
                        y = psY[s][:, k * P:k * P + P]
                        for c in range(NC):
                            pe.matmul(y, hT[:, s, c, k * P:k * P + P], wo[:, c, :], start=(c == 0), stop=False)
                        m = pe.matmul(y, R.ones[0:1, 0:P], bo[:], start=False, stop=True)
                    m.then_inc(yd, 1)
                three_steps(pe, NG, first, second, third)

            @block.scalar
            def _(act):
                act.sem_inc(tmoved, 2)
                act.sem_inc(hotm, 1)
                act.sem_inc(act_d, 2)

                def front(g, s, j):
                    act.wait_ge(hot, g + 1 + 1)
                    act.wait_ge(hid, g * NC + 1)
                    act.activation(hotT[:, s, :], psB[0:E2, :], ACT.Copy).then_inc(hotm, 1)
                    for k in range(4):
                        act.wait_ge(turned, g * 4 + k + 1 + 2)
                        act.activation(xmT[:, s, :, k, :], psT[k % 2][:].rearrange("p (e t) -> p e t", e=E2), ACT.Copy
                                       ).then_inc(tmoved, 1)

                def back(g, s, j):
                    act.wait_ge(yd, free_at(g))
                    for c in range(NC):
                        act.wait_ge(hid, g * NC + c + 1 + 2)
                        act.activation(hT[:, s, c, :], psH[c % 2][:], ACT.Gelu).then_inc(act_d, 1)

                front(0, 0, 0)
                with act.Fori(0, NG // 2 - 1) as j:
                    back(2 * j, 0, j)
                    front(2 * j + 1, 1, j)
                    back(2 * j + 1, 1, j)
                    front(2 * j + 2, 0, j + 1)
                back(NG - 2, 0, NG // 2 - 1)
                front(NG - 1, 1, NG // 2 - 1)
                back(NG - 1, 1, NG // 2 - 1)


def stage_norm_add(nc, R, name, gamma, beta):
    with Stage(nc, name) as st:
        gm, bt = st.sb("gm", [P, D]), st.sb("bt", [P, D])
        loaded, shifted, scaled = st.sem("loaded"), st.sem("shifted"), st.sem("scaled")
        with nc.Block() as block:
            @block.sync
            def _(sp):
                sp.dma_start(gm[:], gamma.partition_broadcast(P)).then_inc(loaded, 16)
                sp.dma_start(bt[:], beta.partition_broadcast(P)).then_inc(loaded, 16)

            @block.gpsimd
            def _(gp):
                gp.wait_ge(loaded, 32)
                with gp.Fori(0, NG) as g:
                    x = tiles_of(R.X, g * 4, 4)
                    gp.tensor_tensor(x, x, bcast_mid(bt[:], 4), ALU.add).then_inc(shifted, 1)

            @block.vector
            def _(dve):
                dve.wait_ge(loaded, 32)
                with dve.Fori(0, NG) as g:
                    for k in range(4):
                        i = g * 4 + k
                        y = tile_of(R.Y, i)
                        dve.scalar_tensor_tensor(out=y, in0=y, scalar=R.mean[:, ds(i, 1)], in1=gm[:],
                                                 op0=ALU.subtract, op1=ALU.mult).then_inc(scaled, 1)
                    dve.wait_ge(shifted, g + 1)
                    for k in range(4):
                        i = g * 4 + k
                        dve.wait_ge(scaled, i + 1)
                        dve.scalar_tensor_tensor(out=tile_of(R.X, i), in0=tile_of(R.Y, i), scalar=R.rstd[:, ds(i, 1)],
                                                 in1=tile_of(R.X, i), op0=ALU.mult, op1=ALU.add)


def stage_bilinear3(nc, R, A):
    with Stage(nc, "bilinear3") as st:
        wq, wkv, wo = st.sb("wq", [P, D]), st.sb("wkv", [P, 2 * D]), st.sb("wo", [P, D])
        mask = st.sb("mask", [P, D])
        cT = st.sb("cT", [P, 2, GW])
        qT = st.sb("qT", [P, 2, GW])
        kv = st.sb("kv", [P, 2, 4, 2, D])
        mT = st.sb("mT", [P, 2, 2, 4, D])
        gg = st.sb("gg", [P, 2, 2, 4, D])
        psQ = st.ps("psQ", [P, 512])
        psK = [st.ps(f"psK{k}", [P, 512]) for k in range(2)]
        psM = [st.ps(f"psM{k}", [P, 512]) for k in range(2)]
        psG = [st.ps(f"psG{k}", [P, 512]) for k in range(2)]
        psY = st.ps("psY", [P, 512])
        wload, cload = st.sem("wload"), [st.sem("cload0"), st.sem("cload1")]
        qd, qm, kd, km, md, mm, gd, gmv, yd, added, ready = (
            st.sem(n) for n in ("qd", "qm", "kd", "km", "md", "mm", "gd", "gmv", "yd", "added", "ready"))
        with nc.Block() as block:
            @block.sync
            def _(sp):
                sp.dma_start(wq[:], A["l3_wqT"]).then_inc(wload, 16)
                sp.dma_start(wkv[:, 0:D], A["l3_wkT"]).then_inc(wload, 16)
                sp.dma_start(wkv[:, D:], A["l3_wvT"]).then_inc(wload, 16)
                sp.dma_start(wo[:], A["l3_woT"]).then_inc(wload, 16)

                def body(g, s, j):
                    sp.wait_ge(kd, 2 * g + 2)
                    sp.dma_start(cT[:, s, :], A["ctxT"][:, ds(g * GW, GW)]).then_inc(cload[s], 16)
                two_slots(sp, NG, body)

            @block.tensor
            def _(pe):
                pe.sem_inc(qd, 2)
                pe.sem_inc(kd, 4)
                for z in (md, gd, yd):
                    pe.sem_inc(z, 2)
                pe.wait_ge(wload, 64)

                def first(g, s, j):
                    pe.wait_ge(cload[s], j * 16 + 16)
                    for h in range(2):
                        pe.wait_ge(km, 2 * g + h + 1)
                        for k in range(2):
                            t = 2 * h + k
                            m = pe.matmul(psK[h][:, 256 * k:256 * k + 256], cT[:, s, t * P:t * P + P], wkv[:],
                                          start=True, stop=True)
                        m.then_inc(kd, 1)
                    pe.wait_ge(qm, g + 1)
                    pe.matmul(psQ[:], wq[:], R.XT[:, ds(g * GW, GW)], start=True, stop=True).then_inc(qd, 1)

                def second(g, s, j):
                    pe.wait_ge(km, 2 * g + 2 + 2)
                    pe.wait_ge(mm, g + 1)
                    for b in range(2):
                        r = slice(64 * b, 64 * b + 64)
                        for k in range(4):
                            m = pe.matmul(psM[b][:, k * P:k * P + P], kv[r, s, k, 1, :], kv[r, s, k, 0, :],
                                          start=True, stop=True)
                    m.then_inc(md, 1)

                def third(g, s, j):
                    pe.wait_ge(mm, g + 2)
                    pe.wait_ge(gmv, g + 1)
                    for b in range(2):
                        for k in range(4):
                            m = pe.matmul(psG[b][:, k * P:k * P + P], mT[:, s, b, k, :], wo[:], start=True, stop=True)
                    m.then_inc(gd, 1)

                def fourth(g, s, j):
                    pe.wait_ge(gmv, g + 2)
                    pe.wait_ge(added, g + 1)
                    pe.wait_ge(qm, g + 2)
                    for b in range(2):
                        for k in range(4):
                            m = pe.matmul(psY[64 * b:64 * b + 64, k * P:k * P + P],
                                          qT[:, s, k * P + 64 * b:k * P + 64 * b + 64], gg[:, s, b, k, :],
                                          start=True, stop=True)
                    m.then_inc(yd, 1)

                first(0, 0, 0)
                second(0, 0, 0)

                def round_of(u, s, j, j1):
                    first(u + 1, 1 - s, j1)
                    third(u, s, j)
                    second(u + 1, 1 - s, j1)
                    fourth(u, s, j)
                with pe.Fori(0, NG // 2 - 1) as j:
                    round_of(2 * j, 0, j, j)
                    round_of(2 * j + 1, 1, j, j + 1)
                last = NG // 2 - 1
                round_of(NG - 2, 0, last, last)
                third(NG - 1, 1, last)
                fourth(NG - 1, 1, last)

            @block.scalar
            def _(act):
                act.sem_inc(km, 2)
                act.sem_inc(qm, 1)
                act.sem_inc(gmv, 1)

                def front(g, s, j):
                    for h in range(2):
                        act.wait_ge(kd, 2 * g + h + 1 + 4)
                        act.wait_ge(md, free_at(g))
                        act.activation(kv[:, s, 2 * h:2 * h + 2, :, :].rearrange("p a b d -> p (a b d)"), psK[h][:],
                                       ACT.Copy).then_inc(km, 1)
                    act.wait_ge(qd, done_at(g))
                    act.wait_ge(yd, free_at(g))
                    act.activation(qT[:, s, :], psQ[:], ACT.Copy).then_inc(qm, 1)

                def back(g, s, j):
                    act.wait_ge(gd, done_at(g))
                    act.wait_ge(yd, free_at(g))
                    act.activation(gg[:, s, 0, :, :].rearrange("p k d -> p (k d)"), psG[0][:], ACT.Copy)
                    act.activation(gg[:, s, 1, :, :].rearrange("p k d -> p (k d)"), psG[1][:],
                                   ACT.Copy).then_inc(gmv, 1)
                skewed(act, NG, front, back)

            @block.vector
            def _(dve):
                dve.tensor_scalar(mask[:], R.bd8[:].rearrange("p a b -> p (a b)"), C2 ** -0.5, None,
                                  ALU.mult).then_inc(ready, 1)
                dve.sem_inc(mm, 1)
                dve.sem_inc(added, 1)
                dve.wait_ge(ready, 1)

                def front(g, s, j):
                    dve.wait_ge(md, done_at(g))
                    dve.wait_ge(gd, free_at(g))
                    for b in range(2):
                        m = dve.tensor_tensor(mT[:, s, b, :, :], psM[b][:].rearrange("p (k d) -> p k d", k=4),
                                              bcast_mid(mask[:], 4), ALU.mult)
                    m.then_inc(mm, 1)

                def back(g, s, j):
                    dve.wait_ge(yd, done_at(g))
                    x = tiles_of(R.X, g * 4, 4)
                    dve.tensor_tensor(x, psY[:].rearrange("p (k d) -> p k d", k=4), x, ALU.add).then_inc(added, 1)
                skewed(dve, NG, front, back)


def stage_experts3(nc, R, A):
    NC = I3 // P
    with Stage(nc, "experts3") as st:
        fc = st.sb("fc", [P, E3, I3])
        proj = st.sb("proj", [P, E3, NC, D])
        hT = st.sb("hT", [P, 2, NC, GW])
        psH = [st.ps(f"psH{k}", [P, 512]) for k in range(4)]
        psY = [st.ps(f"psY{k}", [P, 512]) for k in range(2)]
        wload, hid, gelud, yd, used = (st.sem(n) for n in ("wload", "hid", "gelud", "yd", "used"))
        with nc.Block() as block:
            @block.sync
            def _(sp):
                sp.dma_start(fc[:], A["f3_fc"].rearrange("e d i -> d e i")).then_inc(wload, 16)
                sp.dma_start(proj[:], A["f3_proj"].rearrange("e (c p) d -> p e c d", p=P)).then_inc(wload, 16)

            @block.tensor
            def _(pe):
                pe.sem_inc(yd, 2)
                pe.wait_ge(wload, 32)

                def hidden(g, e):
                    for c in range(NC):
                        pe.wait_ge(gelud, (g * E3 + e) * NC + c + 1)
                        pe.matmul(psH[c][:], fc[:, e, c * P:c * P + P], R.XT[:, ds(g * GW, GW)], start=True,
                                  stop=True).then_inc(hid, 1)

                def project(g, e):
                    pe.wait_ge(gelud, (g * E3 + e) * NC + NC + 4)
                    pe.wait_ge(used, (g * E3 + e) * 4 + 4)
                    for k in range(4):
                        for c in range(NC):
                            m = pe.matmul(psY[e % 2][:, k * P:k * P + P], hT[:, e % 2, c, k * P:k * P + P],
                                          proj[:, e, c, :], start=(c == 0), stop=(c == NC - 1))
                    m.then_inc(yd, 1)

                def group(g, last=False):
                    for e in range(E3):
                        if e < E3 - 1:
                            hidden(g, e + 1)
                        elif not last:
                            hidden(g + 1, 0)
                        project(g, e)
                hidden(0, 0)
                with pe.Fori(0, NG - 1) as g:
                    group(g)
                group(NG - 1, last=True)

            @block.scalar
            def _(act):
                act.sem_inc(gelud, 4)
                with act.Fori(0, NG) as g:
                    for e in range(E3):
                        act.wait_ge(yd, g * E3 + e + 1)
                        for c in range(NC):
                            act.wait_ge(hid, (g * E3 + e) * NC + c + 1)
                            act.activation(hT[:, e % 2, c, :], psH[c][:], ACT.Gelu).then_inc(gelud, 1)

            @block.vector
            def _(dve):
                dve.sem_inc(used, 8)
                with dve.Fori(0, NG) as g:
                    for e in range(E3):
                        dve.wait_ge(yd, g * E3 + e + 1 + 2)
                        for k in range(4):
                            i = g * 4 + k
                            dve.wait_ge(used, (g * E3 + e) * 4 + k + 1 + 4)
                            x = tile_of(R.X, i)
                            dve.scalar_tensor_tensor(out=x, in0=psY[e % 2][:, k * P:k * P + P],
                                                     scalar=R.wt[:, ds(i * E3 + e, 1)], in1=x, op0=ALU.mult,
                                                     op1=ALU.add).then_inc(used, 1)


def program(nc, A, out):
    ctx = ExitStack()
    with ctx:
        def sb(name, shape, dt=F32):
            return ctx.enter_context(nc.sbuf_tensor(name, shape, dt))

        R = Resident()
        R.X = sb("X", [P, NT, D])
        R.ident, R.same2, R.tri_incl, R.tri_strict = (
            sb(n, [P, P]) for n in ("ident", "same2", "tri_incl", "tri_strict"))
        R.ident_bf, R.causal = sb("ident_bf", [P, P], BF16), sb("causal", [P, 512], BF16)
        R.delta, R.ones = sb("delta", [P, S]), sb("ones", [P, 512])
        R.bd16, R.bd16q = sb("bd16", [P, H0]), sb("bd16q", [P, H0])
        R.bd8 = sb("bd8", [P, H2, C2])
        R.vmask = sb("vmask", [P, 4, 2, C0])
        R.vmask128 = R.vmask[:].rearrange("p a b c -> p (a b c)")
        R.stats, R.t0, R.t1 = sb("stats", [P, NT, 6]), sb("t0", [P, NT]), sb("t1", [P, NT])
        R.mean, R.rstd = sb("mean", [P, NT]), sb("rstd", [P, NT])
        R.cs, R.g = sb("cs", [P, NT * H0]), sb("g", [P, NT, H0])
        R.rowmax, R.rowsum = sb("rowmax", [P, NT, H0]), sb("rowsum", [P, NT, H0])
        R.khop = nc.dram_tensor("khop", (B, S, H0 * S), F32, kind="Internal").ap()

        def finish():
            with Stage(nc, "store") as st:
                stored = st.sem("stored")
                with nc.Block() as block:
                    @block.sync
                    def _(sp):
                        sp.dma_start(out.rearrange("(i p) d -> p i d", p=P), R.X[:]).then_inc(stored, 16)
                        sp.wait_ge(stored, 16)

        stage_setup(nc, R, A)
        with nc.sbuf_tensor("XT", [P, TOK], F32) as R.XT:
            stage_stats(nc, R, "stats0")
            stage_norm_T(nc, R, "norm0")
            stage_gates(nc, R, A)
            stage_hop(nc, R, A)
            with nc.sbuf_tensor("Y", [P, NT, D], F32) as R.Y:
                stage_mlstm(nc, R, A)
                stage_headnorm(nc, R, A)
            stage_stats(nc, R, "stats1")
            stage_norm_T(nc, R, "norm1")
            stage_scan(nc, R, A)
        R.lg, R.wt = sb("lg", [P, 512]), sb("wt", [P, 512])
        stage_stats(nc, R, "stats2")
        stage_attend(nc, R, A)
        R.XT = sb("XTb", [P, TOK])
        stage_stats(nc, R, "stats3")
        stage_norm_T(nc, R, "norm3")
        stage_logits(nc, R, A, "logits3", A["f1_wrT"], E1)
        stage_route(nc, R, "route3", E1, True, CAP)
        stage_experts1(nc, R, A)
        stage_stats(nc, R, "stats4")
        stage_linear2(nc, R, A)
        stage_stats(nc, R, "stats5")
        stage_norm_T(nc, R, "norm5")
        stage_logits(nc, R, A, "logits5", A["f2_wr"], E2)
        stage_route(nc, R, "route5", E2, False, 0)
        with nc.sbuf_tensor("Y2", [P, NT, D], F32) as R.Y:
            stage_experts2(nc, R, A)
            stage_stats(nc, R, "stats5y", R.Y, 1e-12)
            stage_norm_add(nc, R, "add5", A["f2_g"], A["f2_b"])
        stage_stats(nc, R, "stats6")
        stage_norm_T(nc, R, "norm6")
        stage_bilinear3(nc, R, A)
        stage_stats(nc, R, "stats7")
        stage_norm_T(nc, R, "norm7")
        stage_logits(nc, R, A, "logits7", A["f3_gate"], E3)
        stage_route(nc, R, "route7", E3, True, 0)
        stage_experts3(nc, R, A)
        finish()


def laid_out(a):
    import numpy as np

    f = lambda n: np.asarray(a[n])
    c = np.ascontiguousarray
    ctx = f("ctx_1024").reshape(TOK, D)
    return {
        "x": f("x").reshape(TOK, D), "ctx": ctx, "ctxT": c(ctx.T),
        "hopsT": c(f("itok_SxS2_0_2016").reshape(S // 2, 2 * S).T), "rpe": f("L0_xattn_rpe"),
        "gate_wT": c(np.concatenate([f("L0_xattn_igate_w"), f("L0_xattn_fgate_w")]).T),
        "gate_b": np.concatenate([f("L0_xattn_igate_b"), f("L0_xattn_fgate_b")])[None],
        "ln_w": f("L0_xattn_ln_w"), "ln_b": f("L0_xattn_ln_b"),
        "lstm_wT": c(np.stack([f(f"L0_ffn_w{g}").T for g in "fico"])),
        "lstm_uT": c(np.stack([f(f"L0_ffn_u{g}").T for g in "fico"])),
        "lstm_bT": c(np.stack([f(f"L0_ffn_b{g}") for g in "fico"]).T),
        "in_c": f("L0_ffn_in_c"),
        "a1_wq": f("L1_xattn_Wq").reshape(D, H1 * C1), "a1_wk": f("L1_xattn_Wk").reshape(D, H1 * C1),
        "a1_wv": f("L1_xattn_Wv").reshape(D, H1 * C1),
        "a1_wo": c(f("L1_xattn_Wo").reshape(HP1, 2 * C1, D).transpose(1, 0, 2)),
        "a1_bqT": c(f("L1_xattn_bq").reshape(HP1, 2 * C1).T), "a1_bkT": c(f("L1_xattn_bk").reshape(HP1, 2 * C1).T),
        "a1_bvT": c(f("L1_xattn_bv").reshape(HP1, 2 * C1).T), "a1_bo": f("L1_xattn_bo")[None],
        "f1_wrT": c(f("L1_ffn_Wr").T), "f1_we": f("L1_ffn_We"),
        "l2_wq": f("L2_xattn_wq"), "l2_wk": f("L2_xattn_wk"), "l2_wv": f("L2_xattn_wv"),
        "l2_g": f("L2_xattn_ln_gamma"), "l2_b": f("L2_xattn_ln_beta"), "l2_dw": np.tile(f("L2_xattn_dense_w").reshape(H2, C2, D), (P // H2, 1, 1)),
        "f2_wr": f("L2_ffn_W_router"), "f2_w1": f("L2_ffn_W1"), "f2_b1": f("L2_ffn_b1"), "f2_wo": f("L2_ffn_Wo"),
        "f2_bo": f("L2_ffn_bo")[None], "f2_g": f("L2_ffn_ln_gamma"), "f2_b": f("L2_ffn_ln_beta"),
        "l3_wqT": c(f("L3_xattn_Wq").T), "l3_wkT": c(f("L3_xattn_Wk").T), "l3_wvT": c(f("L3_xattn_Wv").T),
        "l3_woT": c(f("L3_xattn_Wo").T), "f3_gate": f("L3_ffn_gate_w"), "f3_fc": f("L3_ffn_fc_w"),
        "f3_proj": f("L3_ffn_proj_w"),
        "l2_db": f("L2_xattn_dense_b")[None], "l2_mask": c(f("mask_BxS2_ff1").reshape(NT, P).T),
    }


def build(nc, arrays):
    A = {
        name: nc.dram_tensor(f"in_{name}", a.shape, mybir.dt.from_np(a.dtype), kind="ExternalInput").ap()
        for name, a in arrays.items()}
    out = nc.dram_tensor("out", (TOK, D), F32, kind="ExternalOutput").ap()
    program(nc, A, out)


def kernel(**inputs):
    import concourse.bacc as bacc
    from concourse.bass_utils import run_bass_kernel_spmd

    arrays = laid_out(inputs)
    nc = bacc.Bacc("TRN2", target_bir_lowering=False, num_devices=1)
    build(nc, arrays)
    got = run_bass_kernel_spmd(nc, [{f"in_{n}": a for n, a in arrays.items()}], core_ids=[0])
    return got.results[0]["out"].reshape(B, S, D)
```

```python
from contextlib import ExitStack

import concourse.bass as bass
from concourse import mybir

F32 = mybir.dt.float32
BF16 = mybir.dt.bfloat16
I32 = mybir.dt.int32
ALU = mybir.AluOpType
ACT = mybir.ActivationFunctionType
AX_X = mybir.AxisListType.X
ds = bass.ds

P = 128
B, S, D = 128, 64, 128
TOK = B * S
NT = TOK // P
NG = NT // 4
GW = 4 * P
LN_EPS = 1e-5

H0, C0 = 8, 16
H1, C1 = 16, 64
HP1 = H1 // 2
E1, CAP = 8, 25
H2, C2 = 16, 8
E2, I2 = 4, 512
E3, I3 = 8, 512
NEG = -1e30


def tile_of(t, i):
    return t[:, ds(i, 1), :].rearrange("p a w -> p (a w)")


def tiles_of(t, i, n):
    return t[:, ds(i, n), :]


def skewed(eng, units, front, back):
    front(0, 0, 0)
    with eng.Fori(0, units // 2 - 1) as j:
        front(2 * j + 1, 1, j)
        back(2 * j, 0, j)
        front(2 * j + 2, 0, j + 1)
        back(2 * j + 1, 1, j)
    last = units // 2 - 1
    front(units - 1, 1, last)
    back(units - 2, 0, last)
    back(units - 1, 1, last)


def two_slots(eng, units, body):
    with eng.Fori(0, units // 2) as j:
        body(2 * j, 0, j)
        body(2 * j + 1, 1, j)


def pipelined(eng, units, steps):
    deepest = max(lag for lag, _ in steps)
    full = (deepest + 1) // 2 * 2

    def one_round(n, j=None):
        for lag, step in steps:
            if j is not None:
                step(2 * j + (n - lag), (n - lag) % 2, j + (n - lag) // 2)
            elif 0 <= n - lag < units:
                step(n - lag, (n - lag) % 2, (n - lag) // 2)

    for n in range(full):
        one_round(n)
    with eng.Fori(0, (units - full) // 2) as j:
        one_round(full, j)
        one_round(full + 1, j)
    for n in range(units, units + deepest):
        one_round(n)


def octets(eng, total, steps):
    lags = [lag for lag, _ in steps]
    before = (max(lags) + 7) // 8 * 8

    def one_round(n, j=None):
        for lag, step in steps:
            c = n - lag
            if j is not None:
                step(8 * j + c, c, j)
            elif 0 <= c < total:
                step(c, c, 0)

    for n in range(min(lags), before):
        one_round(n)
    with eng.Fori(0, (total - 8 - before) // 8) as j:
        for k in range(8):
            one_round(before + k, j)
    for n in range(total - 8, total + max(lags)):
        one_round(n)


def three_steps(eng, units, first, second, third):
    first(0, 0, 0)
    with eng.Fori(0, units // 2 - 1) as j:
        second(2 * j, 0, j)
        first(2 * j + 1, 1, j)
        third(2 * j, 0, j)
        second(2 * j + 1, 1, j)
        first(2 * j + 2, 0, j + 1)
        third(2 * j + 1, 1, j)
    last = units // 2 - 1
    second(units - 2, 0, last)
    first(units - 1, 1, last)
    third(units - 2, 0, last)
    second(units - 1, 1, last)
    third(units - 1, 1, last)


class Chain:

    def __init__(self, eng, sem, base=0):
        self.eng, self.sem, self.base, self.n = eng, sem, base, 0

    def __call__(self, ins):
        self.n += 1
        ins.then_inc(self.sem, 1)
        self.eng.wait_ge(self.sem, self.base + self.n)


def free_at(u):
    return u + 1


def done_at(u, n=2):
    return u + 1 + n


def bcast_mid(ap, n):
    return ap.rearrange("p (a w) -> p a w", a=1).broadcast_to([ap.shape[0], n, ap.shape[1]])


def bcast_in(ap, n):
    return ap.rearrange("p (w a) -> p w a", a=1).broadcast_to([ap.shape[0], ap.shape[1], n])


class Stage:

    def __init__(self, nc, name):
        self.nc, self.name, self.ctx, self.sems = nc, name, ExitStack(), []

    def __enter__(self):
        self.ctx.__enter__()
        return self

    def __exit__(self, *e):
        if not e[0]:
            self.nc.clear_and_free_semaphores(self.sems)
            self.nc.all_engine_barrier()
        return self.ctx.__exit__(*e)

    def sb(self, name, shape, dt=F32):
        return self.ctx.enter_context(self.nc.sbuf_tensor(f"{self.name}_{name}", shape, dt))

    def ps(self, name, shape, dt=F32):
        return self.ctx.enter_context(self.nc.psum_tensor(f"{self.name}_{name}", shape, dt))

    def sem(self, name):
        self.sems.append(self.nc.alloc_semaphore(name=f"{self.name}_{name}"))
        return self.sems[-1]


class Resident:
    pass


def stage_setup(nc, R, A):
    with Stage(nc, "setup") as st:
        loaded, made, zeroed = st.sem("loaded"), st.sem("made"), st.sem("zeroed")
        with nc.Block() as block:
            @block.sync
            def _(sp):
                sp.dma_start(R.X[:], A["x"].rearrange("(i p) d -> p i d", p=P)).then_inc(loaded, 16)
                sp.wait_ge(loaded, 16)

            @block.vector
            def _(dve):
                for t in (R.ident, R.same2, R.tri_incl, R.tri_strict, R.delta, R.bd16, R.bd8,
                          R.vmask, R.causal, R.ident_bf):
                    dve.memset(t[:], 0.0).then_inc(zeroed, 1)
                dve.memset(R.ones[:], 1.0)
                dve.wait_ge(zeroed, 10)
                for h in range(2):
                    rows = slice(64 * h, 64 * h + 64)
                    for t in (R.same2, R.tri_incl, R.tri_strict):
                        dve.memset(t[rows, 64 * h:64 * h + 64], 1.0).then_inc(zeroed, 1)
                    dve.memset(R.vmask[rows, :, h, :], 1.0).then_inc(zeroed, 1)
                dve.memset(R.bd16[:], 1.0).then_inc(zeroed, 1)
                dve.memset(R.bd8[:], 1.0).then_inc(zeroed, 1)

            @block.gpsimd
            def _(gp):
                gp.wait_ge(zeroed, 20)
                link = Chain(gp, made)
                for t in (R.ident, R.ident_bf):
                    link(gp.affine_select(out=t[:], in_=t[:], compare_op=ALU.not_equal, fill=1.0, base=0,
                                     pattern=[[-1, 128]], channel_multiplier=1))
                link(gp.affine_select(out=R.tri_incl[:], in_=R.tri_incl[:], compare_op=ALU.is_ge, fill=0.0,
                                 base=0, pattern=[[1, 128]], channel_multiplier=-1))
                link(gp.affine_select(out=R.tri_strict[:], in_=R.tri_strict[:], compare_op=ALU.is_gt, fill=0.0,
                                 base=0, pattern=[[1, 128]], channel_multiplier=-1))
                for h in range(2):
                    rows = slice(64 * h, 64 * h + 64)
                    link(gp.affine_select(out=R.delta[rows, :], in_=R.delta[rows, :], compare_op=ALU.not_equal,
                                     fill=1.0, base=0, pattern=[[-1, 64]], channel_multiplier=1))
                    c = R.causal[rows, :].rearrange("p (h t) -> p h t", h=H0)
                    link(gp.affine_select(out=c, in_=c, compare_op=ALU.is_ge, fill=NEG, base=0,
                                     pattern=[[0, H0], [-1, S]], channel_multiplier=1))
                link(gp.affine_select(out=R.bd16[:], in_=R.bd16[:], compare_op=ALU.is_ge, fill=0.0, base=0,
                                 pattern=[[-C0, H0]], channel_multiplier=1))
                link(gp.affine_select(out=R.bd16[:], in_=R.bd16[:], compare_op=ALU.is_ge, fill=0.0, base=C0 - 1,
                                 pattern=[[C0, H0]], channel_multiplier=-1))
                link(gp.affine_select(out=R.bd8[:], in_=R.bd8[:], compare_op=ALU.is_ge, fill=0.0, base=0,
                                 pattern=[[-C2, H2], [0, C2]], channel_multiplier=1))
                link(gp.tensor_scalar(R.bd16q[:], R.bd16[:], 1.0 / C0 ** 0.5, None, ALU.mult))
                link(gp.affine_select(out=R.bd8[:], in_=R.bd8[:], compare_op=ALU.is_ge, fill=0.0, base=C2 - 1,
                                 pattern=[[C2, H2], [0, C2]], channel_multiplier=-1))


def stage_stats(nc, R, name, src=None, eps=LN_EPS):
    src = R.X if src is None else src
    with Stage(nc, name) as st:
        raw, t0, t1 = R.stats, R.t0, R.t1
        chain, rooted, var_ready = st.sem("chain"), st.sem("rooted"), st.sem("var_ready")
        with nc.Block() as block:
            @block.vector
            def _(dve):
                with dve.Fori(0, NG) as g:
                    for k in range(4):
                        i = g * 4 + k
                        dve.bn_stats(tile_of(raw, i), tile_of(src, i)).then_inc(chain, 1)
                dve.wait_ge(chain, NT)
                m0, v0, m1, v1 = (raw[:, :, c] for c in (1, 2, 4, 5))
                dve.tensor_tensor(R.mean[:], m0, m1, ALU.add).then_inc(chain, 1)
                dve.tensor_tensor(t0[:], m0, m1, ALU.subtract).then_inc(chain, 1)
                dve.tensor_tensor(t1[:], v0, v1, ALU.add).then_inc(chain, 1)
                dve.wait_ge(chain, NT + 3)
                dve.tensor_scalar(R.mean[:], R.mean[:], 0.5, None, ALU.mult).then_inc(chain, 1)
                dve.tensor_tensor(t0[:], t0[:], t0[:], ALU.mult).then_inc(chain, 1)
                dve.tensor_scalar(t1[:], t1[:], 1.0 / D, eps, ALU.mult, ALU.add).then_inc(chain, 1)
                dve.wait_ge(chain, NT + 6)
                dve.scalar_tensor_tensor(out=t0[:], in0=t0[:], scalar=0.25, in1=t1[:], op0=ALU.mult,
                                         op1=ALU.add).then_inc(var_ready, 1)
                dve.wait_ge(rooted, 1)
                dve.reciprocal(R.rstd[:], t1[:]).then_inc(chain, 1)

            @block.scalar
            def _(act):
                act.wait_ge(var_ready, 1)
                act.activation(t1[:], t0[:], ACT.Sqrt).then_inc(rooted, 1)



def stage_norm_T(nc, R, name, w=None, E=0, logits=None, ctxT=None, w_ctx=(), bias=None):
    with Stage(nc, name) as st:
        xh = st.sb("xh", [P, 2, 4, P])
        ps = [st.ps(f"ps{k}", [P, GW]) for k in range(2)]
        normed, turned, moved = (st.sem(n) for n in ("normed", "turned", "moved"))
        if w is not None:
            xs = st.sb("xs", [P, 2, GW])
            ws = st.sb("ws", [P, E])
            psL = [st.ps(f"psL{k}", [P, GW]) for k in range(2)]
            wload, prod, taken, ready = (st.sem(n) for n in ("wload", "prod", "taken", "ready"))
        if ctxT is not None:
            wc = st.sb("wc", [P, len(w_ctx), E])
            bb = st.sb("bb", [P, E])
            cs = st.sb("cs", [P, 2, GW])
            cload = [st.sem(f"cload{k}") for k in range(2)]
        n_loads = 16 * (1 + (len(w_ctx) + 1 if ctxT is not None else 0))
        with nc.Block() as block:
            if w is not None:
                @block.sync
                def _(sp):
                    sp.dma_start(ws[:], w).then_inc(wload, 16)
                    if ctxT is not None:
                        for n, part in enumerate(w_ctx):
                            sp.dma_start(wc[:, n, :], part).then_inc(wload, 16)
                        sp.dma_start(bb[:], bias.partition_broadcast(P)).then_inc(wload, 16)

                        def body(g, s, j):
                            sp.wait_ge(prod, free_at(g))
                            sp.dma_start(cs[:, s, :], ctxT[:, ds(g * GW, GW)]).then_inc(cload[s], 16)
                        two_slots(sp, NG, body)

            @block.vector
            def _(dve):
                if ctxT is not None:
                    dve.wait_ge(wload, n_loads)
                    dve.tensor_tensor(wc[:, 0, :], wc[:, 0, :], wc[:, 1, :], ALU.add).then_inc(ready, 1)
                if w is not None:
                    dve.sem_inc(taken, 2)

                def normalise(g, s, j):
                    dve.wait_ge(turned, free_at(g))
                    for k in range(4):
                        i = g * 4 + k
                        norm = dve.tensor_scalar(xh[:, s, k, :], tile_of(R.X, i), R.mean[:, ds(i, 1)],
                                                 R.rstd[:, ds(i, 1)], ALU.subtract, ALU.mult)
                    norm.then_inc(normed, 1)

                def take(g, s, j):
                    dve.wait_ge(prod, done_at(g))
                    dst = logits[:, ds(g * 4 * E, 4 * E)]
                    if ctxT is None:
                        m = dve.tensor_copy(dst, psL[s][:, 0:4 * E])
                    else:
                        m = dve.tensor_tensor(dst.rearrange("p (k e) -> p k e", k=4),
                                              psL[s][:, 0:4 * E].rearrange("p (k e) -> p k e", k=4),
                                              bcast_mid(bb[:], 4), ALU.add)
                    m.then_inc(taken, 1)
                pipelined(dve, NG, ((4, take), (0, normalise)) if w is not None else ((0, normalise),))

            @block.tensor
            def _(pe):
                pe.sem_inc(turned, 2)
                if w is not None:
                    pe.sem_inc(prod, 2)
                    pe.wait_ge(wload, n_loads)
                if ctxT is not None:
                    pe.wait_ge(ready, 1)

                def turn(g, s, j):
                    pe.wait_ge(moved, free_at(g))
                    pe.wait_ge(normed, g + 1)
                    for k in range(4):
                        t = pe.transpose(ps[s][:, k * P:(k + 1) * P], xh[:, s, k, :], R.ident[:])
                    t.then_inc(turned, 1)

                def score(g, s, j):
                    pe.wait_ge(moved, done_at(g))
                    pe.wait_ge(taken, free_at(g))
                    if ctxT is not None:
                        pe.wait_ge(cload[s], j * 16 + 16)
                    for k in range(4):
                        o, cols = psL[s][:, k * E:k * E + E], slice(k * P, k * P + P)
                        m = pe.matmul(o, xs[:, s, cols], ws[:], start=True, stop=(ctxT is None))
                        if ctxT is not None:
                            m = pe.matmul(o, cs[:, s, cols], wc[:, 0, :], start=False, stop=True)
                    m.then_inc(prod, 1)
                pipelined(pe, NG, ((3, score), (1, turn)) if w is not None else ((1, turn),))

            @block.scalar
            def _(act):
                act.sem_inc(moved, 2)

                def move(g, s, j):
                    act.wait_ge(turned, done_at(g))
                    if w is not None:
                        act.wait_ge(prod, free_at(g))
                        act.activation(xs[:, s, :], ps[s][:], ACT.Copy)
                    act.activation(R.XT[:, ds(g * GW, GW)], ps[s][:], ACT.Copy).then_inc(moved, 1)
                pipelined(act, NG, ((2, move),))


def stage_gates(nc, R, A):
    with Stage(nc, "gates") as st:
        ig, fg = st.sb("ig", [P, NT * H0]), st.sb("fg", [P, NT * H0])
        t0, t1 = st.sb("t0", [P, NT * H0]), st.sb("t1", [P, NT * H0])
        pc = st.ps("pc", [P, 512])
        split, absd, exped, logged, logf, cum = (
            st.sem(n) for n in ("split", "absd", "exped", "logged", "logf", "cum"))
        with nc.Block() as block:
            @block.tensor
            def _(pe):
                pe.wait_ge(logf, 1)
                pe.matmul(pc[:], R.tri_incl[:], t0[:], start=True, stop=True).then_inc(cum, 1)

            @block.scalar
            def _(act):
                act.wait_ge(absd, 1)
                act.activation(t1[:], t0[:], ACT.Exp, scale=-1.0).then_inc(exped, 1)
                act.wait_ge(exped, 1)
                act.activation(t1[:], t1[:], ACT.Ln, bias=1.0).then_inc(logged, 1)

            @block.vector
            def _(dve):
                v = lambda t: t[:].rearrange("p (i h) -> p i h", i=NT)
                G = R.G[:].rearrange("p (i n) -> p i n", i=NT)
                dve.tensor_copy(v(ig), G[:, :, 0:H0]).then_inc(split, 1)
                dve.tensor_copy(v(fg), G[:, :, H0:]).then_inc(split, 1)
                dve.wait_ge(split, 2)
                dve.scalar_tensor_tensor(out=t0[:], in0=fg[:], scalar=-1.0, in1=fg[:], op0=ALU.mult,
                                         op1=ALU.max).then_inc(absd, 1)
                dve.wait_ge(logged, 1)
                dve.scalar_tensor_tensor(out=t0[:], in0=fg[:], scalar=0.0, in1=t1[:], op0=ALU.min,
                                         op1=ALU.subtract).then_inc(logf, 1)
                dve.wait_ge(cum, 1)
                dve.tensor_copy(R.cs[:], pc[:])
                dve.tensor_tensor(R.g[:].rearrange("p i h -> p (i h)"), ig[:], pc[:], ALU.subtract)


def stage_hop(nc, R, A):
    NV = S // 2
    RO = S // 4
    with Stage(nc, "hop") as st:
        idx = st.sb("idx", [P, NV], I32)
        rows = st.sb("rows", [P, NV, D])
        rows_s = st.sb("rows_s", [P, 2, 2, P])
        rT = [st.ps(f"rT{k}", [P, 512]) for k in range(2)]
        out = [st.ps(f"out{k}", [P, 512]) for k in range(4)]
        bd = st.sb("bd", [P, 2, 4, H0, S])
        qv = st.sb("qv", [P, 2, 4, P])
        kh = st.sb("kh", [P, 2, 4, 512])
        iload, gathered = st.sem("iload"), st.sem("gathered")
        rows_in, turned, spread, prod, moved = (st.sem(n) for n in ("rows_in", "turned", "spread", "prod", "moved"))
        stored = [st.sem(f"stored{k}") for k in range(2)]
        with nc.Block() as block:
            @block.sync
            def _(sp):
                with nc.allow_non_contiguous_dma("4096 indices"):
                    sp.dma_start(idx[:], A["hopsT"]).then_inc(iload, 16)
                for k in range(2):
                    sp.sem_inc(stored[k], 16)

                def body(r, s, j):
                    sp.wait_ge(moved, r * 4 + 4 + 4)
                    sp.dma_start(R.khop[:, ds(4 * r, 4), :], kh[:, s, :, :]).then_inc(stored[s], 16)
                two_slots(sp, RO, body)
                for k in range(2):
                    sp.wait_ge(stored[k], 16 * (RO // 2) + 16)

            @block.gpsimd
            def _(gp):
                gp.wait_ge(iload, 16)
                for n in range(NV):
                    gp.indirect_dma_start(out=rows[:, n, :], out_offset=None, in_=A["rpe"],
                                          in_offset=bass.IndirectOffsetOnAxis(ap=idx[:, n:n + 1], axis=0)
                                          ).then_inc(gathered, 16)

            @block.scalar
            def _(act):
                act.sem_inc(moved, 4)
                act.wait_ge(gathered, 16 * NV)

                def front(r, s, j):
                    act.wait_ge(turned, free_at(r))
                    act.activation(rows_s[:, s, :, :], tiles_of(rows, 2 * r, 2), ACT.Copy).then_inc(rows_in, 1)

                def back(r, s, j):
                    act.wait_ge(stored[s], j * 16 + 16)
                    for k in range(4):
                        act.wait_ge(prod, r * 4 + k + 1 + 8)
                        act.activation(kh[:, s, k, :], out[k][:], ACT.Copy).then_inc(moved, 1)
                skewed(act, RO, front, back)

            @block.tensor
            def _(pe):
                pe.sem_inc(turned, 2)
                pe.sem_inc(prod, 8)

                def front(r, s, j):
                    pe.wait_ge(rows_in, r + 1)
                    pe.wait_ge(spread, free_at(r))
                    for k in range(2):
                        t = pe.transpose(rT[s][:, k * P:(k + 1) * P], rows_s[:, s, k, :], R.ident[:])
                    t.then_inc(turned, 1)

                def back(r, s, j):
                    pe.wait_ge(spread, done_at(r))
                    for k in range(4):
                        pe.wait_ge(moved, r * 4 + k + 1)
                        pe.matmul(out[k][:], qv[:, s, k, :], bd[:, s, k, :, :].rearrange("p h m -> p (h m)"),
                                  start=True, stop=True).then_inc(prod, 1)
                skewed(pe, RO, front, back)

            @block.vector
            def _(dve):
                dve.sem_inc(spread, 2)
                q3 = R.XT[:].rearrange("p (b v) -> p v b", v=S)

                def body(r, s, j):
                    dve.wait_ge(prod, r * 4 + 4)
                    dve.tensor_copy(qv[:, s, :, :], q3[:, ds(4 * r, 4), :])
                    dve.wait_ge(turned, done_at(r))
                    for k in range(4):
                        sp = dve.tensor_tensor(bd[:, s, k, :, :], bcast_mid(rT[s][:, k * S:k * S + S], H0),
                                               bcast_in(R.bd16[:], S), ALU.mult)
                    sp.then_inc(spread, 1)
                two_slots(dve, RO, body)


def stage_mlstm(nc, R, A):
    with Stage(nc, "mlstm") as st:
        qT = st.sb("qT", [P, 2, P])
        kT = st.sb("kT", [P, 2, P])
        vv = st.sb("vv", [P, 2, 2, D])
        kh = st.sb("kh", [P, 2, 512])
        kbd = st.sb("kbd", [P, 2, 2, H0, S])
        vbd = st.sb("vbd", [P, 2, 2, D])
        dg = st.sb("dg", [P, 2, 512])
        arg = st.sb("arg", [P, 2, 512])
        dec = st.sb("dec", [P, 2, 512])
        cc = st.sb("cc", [P, 2, 512])
        cT = st.sb("cT", [P, 2, 512])
        psA = [st.ps(f"psA{k}", [P, 512]) for k in range(2)]
        psQ = [st.ps(f"psQ{k}", [P, 512]) for k in range(2)]
        psT = [st.ps(f"psT{k}", [P, 512]) for k in range(2)]
        psH = [st.ps(f"psH{k}", [P, 512]) for k in range(2)]
        qk_load, v_load, kh_load = ([st.sem(f"{n}{k}") for k in range(2)] for n in ("qk_load", "v_load", "kh_load"))
        diag, bias_sum, scores, kspread, vspread, argd, decd, ccd, ct, ctm, hd, hm, mchain, cchain = (
            st.sem(n) for n in ("diag", "bias_sum", "scores", "kspread", "vspread", "argd", "decd", "ccd",
                                "ct", "ctm", "hd", "hm", "mchain", "cchain"))
        heads = lambda ap: ap.rearrange("p (h t) -> p h t", h=H0)
        with nc.Block() as block:
            @block.sync
            def _(sp):
                def load_qk(i, s, j):
                    sp.wait_ge(scores, free_at(i))
                    sp.dma_start(qT[:, s, :], R.XT[:, ds(i * P, P)]).then_inc(qk_load[s], 16)
                    sp.dma_start(kT[:, s, :], A["ctxT"][:, ds(i * P, P)]).then_inc(qk_load[s], 16)

                def load_hop(i, s, j):
                    sp.wait_ge(ccd, free_at(i))
                    sp.dma_start(kh[:, s, :], R.khop[ds(2 * i, 2), :, :].rearrange("b v n -> (b v) n")
                                 ).then_inc(kh_load[s], 16)

                def load_v(i, s, j):
                    sp.wait_ge(vspread, free_at(i))
                    c = A["ctx"][ds(i * P, P), :].rearrange("(b t) d -> t b d", b=2)
                    for h in range(2):
                        sp.dma_start(vv[64 * h:64 * h + 64, s, :, :], c).then_inc(v_load[s], 16)
                pipelined(sp, NT, ((2, load_hop), (4, load_v), (0, load_qk)))

            @block.gpsimd
            def _(gp):
                gp.sem_inc(vspread, 2)

                def spread_k(i, s, j):
                    gp.wait_ge(qk_load[s], j * 32 + 32)
                    gp.wait_ge(scores, free_at(i))
                    for b in range(2):
                        m = gp.tensor_tensor(kbd[:, s, b, :, :], bcast_mid(kT[:, s, b * S:b * S + S], H0),
                                             bcast_in(R.bd16q[:], S), ALU.mult)
                    m.then_inc(kspread, 1)

                def spread_v(i, s, j):
                    gp.wait_ge(v_load[s], j * 32 + 32)
                    gp.wait_ge(hd, free_at(i))
                    gp.tensor_tensor(vbd[:, s, :, :], vv[:, s, :, :], bcast_mid(R.vmask128, 2),
                                     ALU.mult).then_inc(vspread, 1)
                pipelined(gp, NT, ((6, spread_v), (1, spread_k)))

            @block.tensor
            def _(pe):
                for q in (bias_sum, scores, ct, hd):
                    pe.sem_inc(q, 2)

                def gate_sum(i, s, j):
                    pe.wait_ge(diag, i + 1)
                    pe.wait_ge(argd, free_at(i))
                    pe.matmul(psA[s][:], R.same2[:], dg[:, s, :], start=True, stop=False)
                    pe.matmul(psA[s][:], R.ident_bf[:], R.causal[:], start=False, stop=True).then_inc(bias_sum, 1)

                def q_k(i, s, j):
                    pe.wait_ge(kspread, i + 1)
                    pe.wait_ge(qk_load[s], j * 32 + 32)
                    pe.wait_ge(ccd, free_at(i))
                    for b in range(2):
                        q = pe.matmul(psQ[s][64 * b:64 * b + 64, :], qT[:, s, b * S:b * S + S],
                                      kbd[:, s, b, :, :].rearrange("p h t -> p (h t)"), start=True, stop=True)
                    q.then_inc(scores, 1)

                def turn_c(i, s, j):
                    pe.wait_ge(ccd, done_at(i))
                    pe.wait_ge(ctm, free_at(i))
                    for k in range(4):
                        t = pe.transpose(psT[s][:, k * P:k * P + P], cc[:, s, k * P:k * P + P], R.ident[:])
                    t.then_inc(ct, 1)

                def c_v(i, s, j):
                    pe.wait_ge(ctm, done_at(i))
                    pe.wait_ge(vspread, done_at(i))
                    pe.wait_ge(hm, free_at(i))
                    for b in range(2):
                        for k in range(4):
                            h = pe.matmul(psH[s][64 * b:64 * b + 64, 32 * k:32 * k + 32],
                                          cT[:, s, k * P + 64 * b:k * P + 64 * b + 64],
                                          vbd[:, s, b, 32 * k:32 * k + 32], start=True, stop=True)
                    h.then_inc(hd, 1)
                pipelined(pe, NT, ((5, turn_c), (7, c_v), (2, q_k), (1, gate_sum)))

            @block.vector
            def _(dve):
                for q in (argd, ccd):
                    dve.sem_inc(q, 2)

                def diagonal(i, s, j):
                    dve.wait_ge(bias_sum, free_at(i))
                    dve.tensor_tensor(heads(dg[:, s, :]), bcast_in(tile_of(R.g, i), S), bcast_mid(R.delta[:], H0),
                                      ALU.mult).then_inc(diag, 1)

                def exponent(i, s, j):
                    dve.wait_ge(bias_sum, done_at(i))
                    dve.tensor_reduce(tile_of(R.rowmax, i), heads(psA[s][:]), AX_X, ALU.max).then_inc(mchain, 1)
                    dve.wait_ge(mchain, i + 1)
                    dve.wait_ge(decd, free_at(i))
                    dve.tensor_tensor(heads(arg[:, s, :]), heads(psA[s][:]), bcast_in(tile_of(R.rowmax, i), S),
                                      ALU.subtract).then_inc(argd, 1)

                def weigh(i, s, j):
                    link = Chain(dve, cchain, i * 3)
                    dve.wait_ge(scores, done_at(i))
                    dve.wait_ge(kh_load[s], j * 16 + 16)
                    link(dve.tensor_tensor(kh[:, s, :], psQ[s][:], kh[:, s, :], ALU.add))
                    dve.wait_ge(decd, done_at(i))
                    dve.wait_ge(ct, free_at(i))
                    link(dve.tensor_tensor(cc[:, s, :], kh[:, s, :], dec[:, s, :], ALU.mult))
                    dve.sem_inc(ccd, 1)
                    link(dve.tensor_reduce(tile_of(R.rowsum, i), heads(cc[:, s, :]), AX_X, ALU.add))
                pipelined(dve, NT, ((4, weigh), (2, exponent), (0, diagonal)))

            @block.scalar
            def _(act):
                for q in (decd, ctm, hm):
                    act.sem_inc(q, 2)

                def decay(i, s, j):
                    act.wait_ge(argd, done_at(i))
                    act.wait_ge(ccd, free_at(i))
                    act.activation(dec[:, s, :], arg[:, s, :], ACT.Exp).then_inc(decd, 1)

                def move_c(i, s, j):
                    act.wait_ge(ct, done_at(i))
                    act.wait_ge(hd, free_at(i))
                    act.activation(cT[:, s, :], psT[s][:], ACT.Copy).then_inc(ctm, 1)

                def move_h(i, s, j):
                    act.wait_ge(hd, done_at(i))
                    act.activation(tile_of(R.Y, i), psH[s][:, 0:D], ACT.Copy).then_inc(hm, 1)
                pipelined(act, NT, ((6, move_c), (3, decay), (8, move_h)))


def stage_headnorm(nc, R, A):
    N = NT * H0
    with Stage(nc, "headnorm") as st:
        en, nrm, mu, var, t0 = (st.sb(n, [P, N]) for n in ("en", "nrm", "mu", "var", "t0"))
        w, b = st.sb("w", [P, D]), st.sb("b", [P, D])
        sq = st.sb("sq", [P, N * C0])
        loaded, chain, ex, ready, rooted, squared, cent = (
            st.sem(n) for n in ("loaded", "chain", "ex", "ready", "rooted", "squared", "cent"))
        y = R.Y[:].rearrange("p i (h c) -> p (i h) c", c=C0)
        with nc.Block() as block:
            @block.sync
            def _(sp):
                sp.dma_start(w[:], A["ln_w"].partition_broadcast(P)).then_inc(loaded, 16)
                sp.dma_start(b[:], A["ln_b"].partition_broadcast(P)).then_inc(loaded, 16)

            @block.vector
            def _(dve):
                link = Chain(dve, chain)
                rs, rm = (t[:].rearrange("p i h -> p (i h)") for t in (R.rowsum, R.rowmax))
                link(dve.tensor_tensor(t0[:], R.cs[:], rm, ALU.add))
                dve.sem_inc(ready, 1)
                link(dve.scalar_tensor_tensor(out=nrm[:], in0=rs, scalar=-1.0, in1=rs, op0=ALU.mult, op1=ALU.max))
                dve.wait_ge(ex, 1)
                link(dve.tensor_tensor(nrm[:], nrm[:], en[:], ALU.max))
                link(dve.tensor_scalar(nrm[:], nrm[:], 1e-6, None, ALU.add))
                link(dve.reciprocal(t0[:], nrm[:]))
                link(dve.tensor_tensor(y, y, bcast_in(t0[:], C0), ALU.mult))
                link(dve.tensor_reduce(mu[:], y, AX_X, ALU.add))
                link(dve.tensor_scalar(mu[:], mu[:], 1.0 / C0, None, ALU.mult))
                dve.tensor_tensor(y, y, bcast_in(mu[:], C0), ALU.subtract).then_inc(cent, 1)
                dve.wait_ge(squared, 1)
                link(dve.tensor_reduce(var[:], sq[:].rearrange("p (n c) -> p n c", c=C0), AX_X, ALU.add))
                link(dve.tensor_scalar(var[:], var[:], 1.0 / C0, LN_EPS, ALU.mult, ALU.add))
                dve.sem_inc(ready, 1)
                dve.wait_ge(rooted, 1)
                link(dve.reciprocal(var[:], t0[:]))
                dve.wait_ge(loaded, 32)
                link(dve.tensor_tensor(y, y, bcast_in(var[:], C0), ALU.mult))
                link(dve.tensor_scalar(w[:], w[:], 1.0, None, ALU.add))
                link(dve.tensor_tensor(R.Y[:], R.Y[:], bcast_mid(w[:], NT), ALU.mult))
                link(dve.tensor_tensor(R.Y[:], R.Y[:], bcast_mid(b[:], NT), ALU.add))
                link(dve.tensor_tensor(R.X[:], R.X[:], R.Y[:], ALU.add))

            @block.scalar
            def _(act):
                act.wait_ge(ready, 1)
                act.activation(en[:], t0[:], ACT.Exp, scale=-1.0).then_inc(ex, 1)
                act.wait_ge(cent, 1)
                act.activation(sq[:], R.Y[:].rearrange("p i d -> p (i d)"), ACT.Square).then_inc(squared, 1)
                act.wait_ge(ready, 2)
                act.activation(t0[:], var[:], ACT.Sqrt).then_inc(rooted, 1)


def stage_scan(nc, R, A):
    NB = B // 8
    with Stage(nc, "scan") as st:
        wx = st.sb("wx", [P, 3, P])
        uc = st.sb("uc", [P, 3, P])
        bias = st.sb("bias", [P, 4])
        cin = st.sb("cin", [P, 1])
        c = st.sb("c", [P, 2, S])
        gates = st.sb("gates", [P, 2, 3, S])
        fc, ig = st.sb("fc", [P, S]), st.sb("ig", [P, S])
        ps = [[st.ps(f"ps{k}_{q}", [P, 512]) for q in range(3)] for k in range(2)]
        loaded, start, cstep, gact, part, xpart, hstep, freed, zero = (
            st.sem(n) for n in ("loaded", "start", "cstep", "gact", "part", "xpart", "hstep", "freed", "zero"))
        with nc.Block() as block:
            @block.sync
            def _(sp):
                sp.dma_start(wx[:], A["lstm_wT"].rearrange("n i m -> i n m")[:, 0:3, :]).then_inc(loaded, 16)
                sp.dma_start(uc[:], A["lstm_uT"].rearrange("n i m -> i n m")[:, 0:3, :]).then_inc(loaded, 16)
                with nc.allow_non_contiguous_dma("bias columns"):
                    sp.dma_start(bias[:], A["lstm_bT"]).then_inc(loaded, 16)
                    sp.dma_start(cin[:], A["in_c"].rearrange("(p a) -> p a", a=1)).then_inc(loaded, 16)

            @block.vector
            def _(dve):
                dve.memset(c[:], 0.0).then_inc(zero, 1)
                dve.wait_ge(loaded, 64)
                dve.wait_ge(zero, 1)
                dve.tensor_scalar(c[:, 0, :], c[:, 0, :], cin[:, 0:1], None, ALU.add).then_inc(cstep, 1)

                def body(t, s, j):
                    dve.wait_ge(gact, t * 3 + 1 + 48)
                    dve.wait_ge(cstep, t + 1)
                    dve.tensor_tensor(fc[:], gates[:, s, 0, :], c[:, s, :], ALU.mult).then_inc(part, 1)
                    dve.wait_ge(gact, t * 3 + 3 + 48)
                    dve.tensor_tensor(ig[:], gates[:, s, 1, :], gates[:, s, 2, :], ALU.mult).then_inc(part, 1)
                    dve.wait_ge(part, t * 2 + 2)
                    dve.tensor_tensor(c[:, 1 - s, :], fc[:], ig[:], ALU.add).then_inc(cstep, 1)
                two_slots(dve, B, body)

            @block.tensor
            def _(pe):
                pe.wait_ge(loaded, 64)

                def xparts(n, s, j):
                    pe.wait_ge(gact, n * 24 + 24)
                    for q in range(3):
                        x = pe.matmul(ps[s][q][:], wx[:, q, :], R.XT[:, ds(n * 512, 512)],
                                      start=True, stop=False, skip_group_check=True)

                def steps(n, s, j):
                    for k in range(8):
                        t = n * 8 + k
                        pe.wait_ge(cstep, t + 1)
                        for q in range(3):
                            pe.matmul(ps[s][q][:, k * S:k * S + S], uc[:, q, :], c[:, k % 2, :], start=False,
                                      stop=True, skip_group_check=True).then_inc(hstep, 1)

                skewed(pe, NB, xparts, steps)

            @block.scalar
            def _(act):
                act.sem_inc(gact, 48)

                def steps(n, s, j):
                    for k in range(8):
                        t = n * 8 + k
                        for q, f in enumerate((ACT.Sigmoid, ACT.Sigmoid, ACT.Tanh)):
                            act.wait_ge(hstep, t * 3 + q + 1)
                            act.activation(gates[:, k % 2, q, :], ps[s][q][:, k * S:k * S + S], f,
                                           bias=bias[:, q:q + 1]).then_inc(gact, 1)
                two_slots(act, NB, steps)
        wo, uo = st.sb("wo", [P, P]), st.sb("uo", [P, P])
        hT = st.sb("hT", [P, 2, GW])
        cb = st.sb("cb", [P, S])
        ws = st.sem("ws")
        prod, tanhd, turned, added = (st.sem(n) for n in ("prod", "tanhd", "turned", "added"))
        with nc.Block() as block:
            @block.sync
            def _(sp):
                sp.dma_start(wo[:], A["lstm_wT"][3]).then_inc(ws, 16)
                sp.dma_start(uo[:], A["lstm_uT"][3]).then_inc(ws, 16)

            @block.tensor
            def _(pe):
                pe.sem_inc(prod, 2)
                pe.sem_inc(turned, 2)
                pe.wait_ge(ws, 32)

                def front(g, s, j):
                    pe.wait_ge(tanhd, free_at(g))
                    pe.matmul(ps[s][0][:], wo[:], R.XT[:, ds(g * GW, GW)], start=True, stop=False)
                    pe.matmul(ps[s][0][:].rearrange("p (b t) -> p b t", b=8), uo[:], bcast_mid(c[:, 0, :], 8),
                              start=False, stop=True).then_inc(prod, 1)

                def back(g, s, j):
                    pe.wait_ge(tanhd, done_at(g))
                    pe.wait_ge(added, free_at(g))
                    for k in range(4):
                        t = pe.transpose(ps[s][1][:, k * P:k * P + P], hT[:, s, k * P:k * P + P], R.ident[:])
                    t.then_inc(turned, 1)
                skewed(pe, NG, front, back)

            @block.scalar
            def _(act):
                act.sem_inc(tanhd, 2)

                def body(g, s, j):
                    act.wait_ge(prod, done_at(g))
                    act.wait_ge(turned, free_at(g))
                    act.activation(hT[:, s, :], ps[s][0][:], ACT.Tanh, bias=bias[:, 3:4]).then_inc(tanhd, 1)
                two_slots(act, NG, body)

            @block.vector
            def _(dve):
                dve.sem_inc(added, 2)

                def body(g, s, j):
                    dve.wait_ge(turned, done_at(g))
                    x = tiles_of(R.X, g * 4, 4)
                    dve.tensor_tensor(x, ps[s][1][:].rearrange("p (k d) -> p k d", k=4), x,
                                      ALU.add).then_inc(added, 1)
                two_slots(dve, NG, body)



def stage_attend(nc, R, A):
    NU, UW = NT // 2, 2 * P
    NKQ = 9
    AHEAD, KQ_AHEAD, V_AHEAD = 6, 15, 9
    with Stage(nc, "attend") as st:
        wq, wk, wv = (st.sb(n, [P, H1 * C1]) for n in ("wq", "wk", "wv"))
        wo = st.sb("wo", [P, HP1, D])
        bq, bk, bv = (st.sb(n, [P, HP1]) for n in ("bq", "bk", "bv"))
        bo, row = st.sb("bo", [1, D]), st.sb("row", [1, D])
        xh, xT = st.sb("xh", [P, 2, P]), st.sb("xT", [P, UW])
        cT = st.sb("cT", [P, 2, UW])
        c2 = st.sb("c2", [P, 2, 4, 2, S])
        qT = st.sb("qT", [P, 2, HP1, UW])
        kbd = st.sb("kbd", [P, 2, HP1, 4, 2, S])
        vbd = st.sb("vbd", [P, 2, 4, HP1, 2, C1])
        top, tot, rs = st.sb("top", [P, 2, 8]), st.sb("tot", [P, 4, 8]), st.sb("rs", [P, 4, 8])
        arg, pr, pT, o, oT = (st.sb(n, [P, 2, 512]) for n in ("arg", "pr", "pT", "o", "oT"))
        psS = [st.ps(f"psS{k}", [P, 512]) for k in range(2)]
        psK, psB, psP, psO, psV, psY = (st.ps(n, [P, 512]) for n in ("psK", "psB", "psP", "psO", "psV", "psY"))
        wload, cload, c2load = st.sem("wload"), *([st.sem(f"{n}{k}") for k in range(2)] for n in ("cload", "c2load"))
        (normed, kq_full, kq_free, v_full, v_free, zero, rowd, rowm, biasd) = (
            st.sem(n) for n in ("normed", "kq_full", "kq_free", "v_full", "v_free", "zero", "rowd", "rowm", "biasd"))
        (s_done, topd, argd, expd, totd, sumd, ptd, ptm, pvd, od, otd, otm, yd, added) = (
            st.sem(n) for n in ("s_done", "topd", "argd", "expd", "totd", "sumd", "ptd", "ptm", "pvd", "od", "otd",
                                "otm", "yd", "added"))
        heads = lambda ap: ap.rearrange("p (h t) -> p h t", h=8)
        lo, hi = slice(0, 64), slice(64, P)
        unit = lambda c, j: 2 * j + c // 4
        slot = lambda c: c // 4 % 2
        place = lambda c: (slot(c), c % 4 // 2, c % 2)
        before = lambda i: i + 2
        kq_taken = lambda u, n: u * NKQ + n + 1 + KQ_AHEAD
        with nc.Block() as block:
            @block.sync
            def _(sp):
                for w, a in ((wq, A["a1_wq"]), (wk, A["a1_wk"]), (wv, A["a1_wv"]), (wo, A["a1_wo"]), (bq, A["a1_bqT"]),
                             (bk, A["a1_bkT"]), (bv, A["a1_bvT"]), (bo, A["a1_bo"])):
                    sp.dma_start(w[:], a).then_inc(wload, 16)

                def load_c(u, s, j):
                    sp.wait_ge(kq_free, kq_taken(u - 2, 3))
                    sp.dma_start(cT[:, s, :], A["ctxT"][:, ds(u * UW, UW)]).then_inc(cload[s], 16)

                def load_c2(u, s, j):
                    sp.wait_ge(v_free, u * 8 - 8 + V_AHEAD)
                    for h in range(2):
                        sp.dma_start(c2[:, s, :, h, :], A["ctxT"][:, ds(u * UW, UW)].rearrange(
                            "p (b t) -> p b t", b=4)).then_inc(c2load[s], 16)
                pipelined(sp, NU, ((1, load_c2), (0, load_c)))

            @block.gpsimd
            def _(gp):
                gp.memset(kbd[:], 0.0).then_inc(zero, 1)
                gp.memset(vbd[:], 0.0).then_inc(zero, 1)

            @block.tensor
            def _(pe):
                for q in (s_done, pvd):
                    pe.sem_inc(q, AHEAD)
                for q in (ptd, otd, yd):
                    pe.sem_inc(q, 2)
                pe.wait_ge(wload, 128)
                for h in range(HP1):
                    m = pe.matmul(psY[0:1, 0:D], bv[:, h:h + 1], wo[:, h, :], start=(h == 0), stop=(h == HP1 - 1))
                m.then_inc(rowd, 1)
                pe.wait_ge(rowm, 1)

                def project_kq(part):
                    def step(i, c, j):
                        u, s, m = unit(c, j), slot(c), c % 4
                        n = 2 * (m % 2) + part
                        if part == 2:
                            if m != 1:
                                return
                            pe.wait_ge(normed, u + 1)
                            pe.wait_ge(kq_free, kq_taken(u, 3))
                            for k in range(2):
                                t = pe.transpose(psK[:, k * P:k * P + P], xh[:, k, :], R.ident[:])
                            t.then_inc(kq_full, 1)
                            return
                        w, x = (wk, cT[:, s, :]) if m < 2 else (wq, xT[:])
                        if m == 0 and part == 0:
                            pe.wait_ge(cload[s], (2 * j + c // 4 - s) * 8 + 16)
                        pe.wait_ge(kq_free, kq_taken(u, (n if m < 2 else n + 5) - 1))
                        for a in range(2):
                            h = 2 * n + a
                            p = pe.matmul(psK[:, a * UW:a * UW + UW], w[:, h * P:h * P + P], x, start=True, stop=True)
                        p.then_inc(kq_full, 1)
                    return step

                def project_v(h):
                    def step(i, c, j):
                        s, b = slot(c), c % 4
                        if b == 0 and h == 0:
                            pe.wait_ge(c2load[s], (2 * j + c // 4 - s) * 16 + 32)
                        pe.wait_ge(v_free, i * 2 + h + V_AHEAD)
                        pe.matmul(psB[:], c2[:, s, b, :, :].rearrange("p a t -> p (a t)"),
                                  wv[:, h * 512:h * 512 + 512], start=True, stop=True).then_inc(v_full, 1)
                    return step

                def scores(i, c, j):
                    s, t, half = place(c)
                    pe.wait_ge(kq_free, kq_taken(unit(c, j), NKQ - 1))
                    pe.wait_ge(argd, free_at(i))
                    for b in range(2):
                        for k in range(4):
                            h, nb = half * 4 + k, t * 2 + b
                            m = pe.matmul(psS[c % 2][64 * b:64 * b + 64, k * P:k * P + P], qT[:, s, h, nb * S:nb * S + S],
                                          kbd[:, s, h, nb, :, :].rearrange("p a t -> p (a t)"), start=True, stop=True)
                    m.then_inc(s_done, 1)

                def turn_p(i, c, j):
                    pe.wait_ge(expd, done_at(i))
                    pe.wait_ge(ptm, before(i))
                    for k in range(4):
                        t = pe.transpose(psP[:, k * P:k * P + P], pr[:, c % 2, k * P:k * P + P], R.ident[:])
                    t.then_inc(ptd, 1)

                def values(i, c, j):
                    s, t, half = place(c)
                    pe.wait_ge(ptm, done_at(i))
                    pe.wait_ge(od, before(i))
                    pe.wait_ge(v_free, (i + 2 * t + 1 - c % 4) * 2 + 2 + V_AHEAD)
                    for b in range(2):
                        for k in range(4):
                            h, nb = half * 4 + k, t * 2 + b
                            m = pe.matmul(psV[64 * b:64 * b + 64, k * P:k * P + P],
                                          pT[:, c % 2, k * P + 64 * b:k * P + 64 * b + 64],
                                          vbd[:, s, nb, h, :, :].rearrange("p a t -> p (a t)"), start=True, stop=True)
                    m.then_inc(pvd, 1)

                def turn_o(i, c, j):
                    pe.wait_ge(od, done_at(i))
                    pe.wait_ge(otm, before(i))
                    for k in range(4):
                        t = pe.transpose(psO[:, k * P:k * P + P], o[:, c % 2, k * P:k * P + P], R.ident[:])
                    t.then_inc(otd, 1)

                def project(i, c, j):
                    pe.wait_ge(otm, done_at(i))
                    if c % 2 == 0:
                        pe.wait_ge(added, 4 * j + c // 2 + 1)
                        pe.matmul(psY[:, 0:D], R.ones[0:1, 0:P], row[:], start=True, stop=False)
                    for k in range(4):
                        m = pe.matmul(psY[:, 0:D], oT[:, c % 2, k * P:k * P + P], wo[:, (c % 2) * 4 + k, :],
                                      start=False, stop=(c % 2 == 1 and k == 3))
                    m.then_inc(yd, 1)
                octets(pe, 2 * NT, ((5, values), (-4, project_kq(0)), (3, turn_p), (1, project_v(0)), (7, turn_o),
                                    (-4, project_kq(1)), (9, project), (1, project_v(1)), (0, scores),
                                    (-4, project_kq(2))))

            @block.scalar
            def _(act):
                for q in (expd, ptm, otm):
                    act.sem_inc(q, 2)
                act.sem_inc(kq_free, KQ_AHEAD)
                act.sem_inc(v_free, V_AHEAD)
                act.wait_ge(rowd, 1)
                act.wait_ge(zero, 2)
                act.wait_ge(biasd, 1)

                def move_kq(part):
                    def step(i, c, j):
                        u, s, m = unit(c, j), slot(c), c % 4
                        n = 2 * (m % 2) + part
                        if part == 2:
                            if m == 1:
                                act.wait_ge(kq_full, u * NKQ + 4 + 1)
                                act.activation(xT[:], psK[:, 0:UW], ACT.Copy).then_inc(kq_free, 1)
                            return
                        act.wait_ge(kq_full, u * NKQ + (n if m < 2 else n + 5) + 1)
                        if n == 0:
                            act.wait_ge(s_done, u * 4 - 5 + 1 + AHEAD)
                        for a in range(2):
                            h, src = 2 * n + a, psK[:, a * UW:a * UW + UW]
                            if m < 2:
                                src = src.rearrange("p (b t) -> p b t", b=4)
                                act.activation(kbd[lo, s, h, :, 0, :], src[lo, :, :], ACT.Identity, bias=bk[lo, h:h + 1])
                                p = act.activation(kbd[hi, s, h, :, 1, :], src[hi, :, :], ACT.Identity,
                                                   bias=bk[hi, h:h + 1])
                            else:
                                p = act.activation(qT[:, s, h, :], src, ACT.Identity, bias=bq[:, h:h + 1],
                                                   scale=C1 ** -0.5)
                        p.then_inc(kq_free, 1)
                    return step

                def move_v(h):
                    def step(i, c, j):
                        s, b = slot(c), c % 4
                        act.wait_ge(v_full, i * 2 + h + 1)
                        act.wait_ge(pvd, unit(c, j) * 4 - 5 + 1 + AHEAD)
                        src = psB[:].rearrange("p (k a d) -> p k a d", k=4, a=2)
                        act.activation(vbd[lo, s, b, 4 * h:4 * h + 4, 0, :], src[lo, :, 0, :], ACT.Copy)
                        act.activation(vbd[hi, s, b, 4 * h:4 * h + 4, 1, :], src[hi, :, 1, :],
                                       ACT.Copy).then_inc(v_free, 1)
                    return step

                def exps(i, c, j):
                    act.wait_ge(argd, done_at(i))
                    act.wait_ge(ptd, free_at(i))
                    act.wait_ge(totd, free_at(i))
                    act.activation(pr[:, c % 2, :], arg[:, c % 2, :], ACT.Exp).then_inc(expd, 1)

                def move_p(i, c, j):
                    act.wait_ge(ptd, done_at(i))
                    act.wait_ge(pvd, i - 2 + 1 + AHEAD)
                    act.activation(pT[:, c % 2, :], psP[:], ACT.Copy).then_inc(ptm, 1)

                def move_o(i, c, j):
                    act.wait_ge(otd, done_at(i))
                    act.wait_ge(yd, free_at(i))
                    act.activation(oT[:, c % 2, :], psO[:], ACT.Copy).then_inc(otm, 1)
                octets(act, 2 * NT, ((4, move_p), (8, move_o), (2, exps), (-4, move_kq(0)), (1, move_v(0)),
                                     (-4, move_kq(1)), (1, move_v(1)), (-4, move_kq(2))))

            @block.vector
            def _(dve):
                for q in (argd, totd, od):
                    dve.sem_inc(q, 2)
                dve.sem_inc(sumd, 4)
                dve.sem_inc(added, 1)
                dve.wait_ge(rowd, 1)
                dve.tensor_tensor(row[:], psY[0:1, 0:D], bo[:], ALU.add).then_inc(rowm, 1)
                dve.tensor_scalar(bq[:], bq[:], C1 ** -0.5, None, ALU.mult).then_inc(biasd, 1)

                def norm(i, c, j):
                    if c % 4:
                        return
                    u = unit(c, j)
                    dve.wait_ge(kq_free, kq_taken(u - 1, 4))
                    for k in range(2):
                        t = u * 2 + k
                        m = dve.tensor_scalar(xh[:, k, :], tile_of(R.X, t), R.mean[:, ds(t, 1)],
                                              R.rstd[:, ds(t, 1)], ALU.subtract, ALU.mult)
                    m.then_inc(normed, 1)

                def soft(i, c, j):
                    dve.wait_ge(s_done, i + 1 + AHEAD)
                    dve.wait_ge(argd, before(i))
                    dve.tensor_reduce(top[:, c % 2, :], heads(psS[c % 2][:]), AX_X, ALU.max).then_inc(topd, 1)
                    dve.wait_ge(topd, i + 1)
                    dve.wait_ge(expd, free_at(i))
                    dve.tensor_tensor(heads(arg[:, c % 2, :]), heads(psS[c % 2][:]),
                                      bcast_in(top[:, c % 2, :], S), ALU.subtract).then_inc(argd, 1)

                def sums(i, c, j):
                    dve.wait_ge(expd, done_at(i))
                    dve.wait_ge(sumd, i + 1)
                    dve.tensor_reduce(tot[:, c % 4, :], heads(pr[:, c % 2, :]), AX_X, ALU.add).then_inc(totd, 1)
                    dve.wait_ge(totd, done_at(i))
                    dve.reciprocal(rs[:, c % 4, :], tot[:, c % 4, :]).then_inc(sumd, 1)

                def scale(i, c, j):
                    dve.wait_ge(pvd, i + 1 + AHEAD)
                    dve.wait_ge(sumd, i + 1 + 4)
                    dve.wait_ge(otd, free_at(i))
                    dve.tensor_tensor(heads(o[:, c % 2, :]), heads(psV[:]), bcast_in(rs[:, c % 4, :], C1),
                                      ALU.mult).then_inc(od, 1)

                def add(i, c, j):
                    if c % 2:
                        t = 4 * j + c // 2
                        dve.wait_ge(yd, done_at(i))
                        dve.tensor_tensor(tile_of(R.X, t), psY[:, 0:D], tile_of(R.X, t), ALU.add).then_inc(added, 1)
                octets(dve, 2 * NT, ((6, scale), (10, add), (3, sums), (1, soft), (-4, norm)))


def stage_route(nc, R, name, E, two, capacity):
    N = NT * E
    with Stage(nc, name) as st:
        rev, eq, hot0, hot1, lg2 = (st.sb(n, [P, w]) for n, w in (
            ("rev", E), ("eq", N), ("hot0", N), ("hot1", N), ("lg2", N)))
        m0, m1, r, ex, w0, w1 = (st.sb(n, [P, NT]) for n in ("m0", "m1", "r", "ex", "w0", "w1"))
        ps = st.ps("ps", [P, 512])
        chain, ready, exd, revd, pos = (st.sem(n) for n in ("chain", "ready", "exd", "revd", "pos"))
        v = lambda t: t.rearrange("p (i e) -> p i e", e=E)
        with nc.Block() as block:
            @block.gpsimd
            def _(gp):
                gp.iota(rev[:].bitcast(I32), pattern=[[-1, E]], base=E, channel_multiplier=0).then_inc(revd, 1)

            @block.vector
            def _(dve):
                link = Chain(dve, chain)
                dve.wait_ge(revd, 1)
                link(dve.tensor_copy(rev[:], rev[:].bitcast(I32)))

                def first_largest(lg, m, hot):
                    link(dve.tensor_reduce(m[:], v(lg), AX_X, ALU.max))
                    link(dve.tensor_tensor(v(eq[:]), v(lg), bcast_in(m[:], E), ALU.is_equal))
                    link(dve.tensor_tensor(v(eq[:]), v(eq[:]), bcast_mid(rev[:], NT), ALU.mult))
                    link(dve.tensor_reduce(r[:], v(eq[:]), AX_X, ALU.max))
                    link(dve.tensor_tensor(v(hot), v(eq[:]), bcast_in(r[:], E), ALU.is_equal))

                first_largest(R.lg[:, 0:N], m0, hot0[:] if two else R.wt[:, 0:N])
                if two:
                    link(dve.scalar_tensor_tensor(out=lg2[:], in0=hot0[:], scalar=-3e38, in1=R.lg[:, 0:N],
                                                  op0=ALU.mult, op1=ALU.add))
                    first_largest(lg2[:], m1, hot1[:])
                    dve.tensor_tensor(m1[:], m1[:], m0[:], ALU.subtract).then_inc(ready, 1)
                    dve.wait_ge(exd, 1)
                    link(dve.tensor_scalar(w0[:], ex[:], 1.0, None, ALU.add))
                    link(dve.reciprocal(w1[:], w0[:]))
                    link(dve.tensor_tensor(w0[:], ex[:], w1[:], ALU.mult))
                    link(dve.tensor_tensor(lg2[:], hot0[:], hot1[:], ALU.add))
                    dve.sem_inc(ready, 1)
                    link(dve.tensor_tensor(v(hot0[:]), v(hot0[:]), bcast_in(w1[:], E), ALU.mult))
                    link(dve.tensor_tensor(v(hot1[:]), v(hot1[:]), bcast_in(w0[:], E), ALU.mult))
                    link(dve.tensor_tensor(R.wt[:, 0:N], hot0[:], hot1[:], ALU.add))
                    if capacity:
                        dve.wait_ge(pos, 1)
                        link(dve.tensor_scalar(eq[:], ps[:], float(capacity), None, ALU.is_lt))
                        link(dve.tensor_tensor(R.wt[:, 0:N], R.wt[:, 0:N], eq[:], ALU.mult))

            if two:
                @block.scalar
                def _(act):
                    act.wait_ge(ready, 1)
                    act.activation(ex[:], m1[:], ACT.Exp).then_inc(exd, 1)

            if capacity:
                @block.tensor
                def _(pe):
                    pe.wait_ge(ready, 2)
                    pe.matmul(ps[:], R.tri_strict[:], lg2[:], start=True, stop=True).then_inc(pos, 1)


def stage_experts1(nc, R, A):
    with Stage(nc, "experts1") as st:
        we = st.sb("we", [P, E1 * D])
        xs = st.sb("xs", [P, 2, P])
        acc = st.sb("acc", [P, 2, D])
        ps = [[st.ps(f"ps{k}_{h}", [P, 512]) for h in range(2)] for k in range(2)]
        wload, xload = st.sem("wload"), [st.sem("xload0"), st.sem("xload1")]
        prod, used, chain = st.sem("prod"), st.sem("used"), st.sem("chain")
        with nc.Block() as block:
            @block.sync
            def _(sp):
                sp.dma_start(we[:].rearrange("p (e f) -> p e f", e=E1), A["f1_we"].rearrange("e d f -> d e f")
                             ).then_inc(wload, 16)

                def body(i, s, j):
                    sp.wait_ge(prod, free_at(i))
                    sp.dma_start(xs[:, s, :], R.XT[:, ds(i * P, P)]).then_inc(xload[s], 16)
                two_slots(sp, NT, body)

            @block.tensor
            def _(pe):
                pe.sem_inc(prod, 2)
                pe.wait_ge(wload, 16)

                def body(i, s, j):
                    pe.wait_ge(xload[s], j * 16 + 16)
                    pe.wait_ge(used, i + 1)
                    for h in range(2):
                        m = pe.matmul(ps[s][h][:], xs[:, s, :], we[:, h * 512:h * 512 + 512], start=True, stop=True)
                    m.then_inc(prod, 1)
                two_slots(pe, NT, body)

            @block.vector
            def _(dve):
                dve.sem_inc(used, 2)
                dve.sem_inc(chain, 2)

                def body(i, s, j):
                    dve.wait_ge(prod, done_at(i))
                    for e in range(E1):
                        dve.wait_ge(chain, i * 9 + max(e + 1, 2))
                        prev = tile_of(R.X, i) if e == 0 else acc[:, e % 2, :]
                        src = ps[s][e // 4][:, (e % 4) * D:(e % 4) * D + D]
                        w = R.wt[:, ds(i * E1 + e, 1)]
                        if e == 1:
                            m = dve.tensor_scalar(acc[:, 1, :], src, w, None, ALU.mult)
                        else:
                            m = dve.scalar_tensor_tensor(out=acc[:, e % 2, :], in0=src, scalar=w, in1=prev,
                                                         op0=ALU.mult, op1=ALU.add)
                        m.then_inc(chain, 1)
                    dve.wait_ge(chain, i * 9 + E1 + 2)
                    dve.sem_inc(used, 1)
                    dve.tensor_tensor(tile_of(R.X, i), acc[:, 0, :], acc[:, 1, :], ALU.add).then_inc(chain, 1)
                two_slots(dve, NT, body)


def stage_project2(nc, R, A, qkv, mean, rstd, nbias):
    N = 3 * NT
    with Stage(nc, "project2") as st:
        w3 = st.sb("w3", [P, 3, D])
        cT, xh, xT = (st.sb(n, [P, 2, GW]) for n in ("cT", "xh", "xT"))
        raw = st.sb("raw", [P, N, 6])
        t0, t1 = st.sb("t0", [P, N]), st.sb("t1", [P, N])
        psX = [st.ps(f"psX{k}", [P, 512]) for k in range(2)]
        psQ = [st.ps(f"psQ{k}", [P, 512]) for k in range(4)]
        wload, cload = st.sem("wload"), [st.sem("cload0"), st.sem("cload1")]
        normed, turned, xtm, prod, copied, statd, var_ready, rooted, chain = (
            st.sem(n) for n in ("normed", "turned", "xtm", "prod", "copied", "statd", "var_ready", "rooted", "chain"))
        with nc.Block() as block:
            @block.sync
            def _(sp):
                for n, a in enumerate((A["l2_wq"], A["l2_wk"], A["l2_wv"])):
                    sp.dma_start(w3[:, n, :], a).then_inc(wload, 16)

                def body(g, s, j):
                    sp.wait_ge(prod, g * 4 + 1)
                    sp.dma_start(cT[:, s, :], A["ctxT"][:, ds(g * GW, GW)]).then_inc(cload[s], 16)
                two_slots(sp, NG, body)

            @block.tensor
            def _(pe):
                pe.sem_inc(turned, 2)
                pe.sem_inc(prod, 5)
                pe.wait_ge(wload, 48)

                def front(g, s, j):
                    pe.wait_ge(xtm, free_at(g))
                    pe.wait_ge(normed, g + 1)
                    for k in range(4):
                        t = pe.transpose(psX[s][:, k * P:(k + 1) * P], xh[:, s, k * P:k * P + P], R.ident[:])
                    t.then_inc(turned, 1)

                def back(g, s, j):
                    pe.wait_ge(xtm, done_at(g))
                    pe.wait_ge(cload[s], j * 16 + 16)
                    for k in range(4):
                        cols = slice(k * P, k * P + P)
                        pe.wait_ge(copied, g * 4 + k + 1)
                        pe.matmul(psQ[k][:, 0:D], xT[:, s, cols], w3[:, 0, :], start=True, stop=True)
                        pe.matmul(psQ[k][:, D:3 * D], cT[:, s, cols], w3[:, 1:3, :].rearrange("p a d -> p (a d)"),
                                  start=True, stop=True).then_inc(prod, 1)
                skewed(pe, NG, front, back)

            @block.scalar
            def _(act):
                act.sem_inc(xtm, 2)
                act.sem_inc(copied, 4)

                def front(g, s, j):
                    act.wait_ge(turned, done_at(g))
                    act.wait_ge(prod, g * 4 + 1)
                    act.activation(xT[:, s, :], psX[s][:], ACT.Copy).then_inc(xtm, 1)

                def back(g, s, j):
                    for k in range(4):
                        act.wait_ge(prod, g * 4 + k + 1 + 5)
                        act.activation(tile_of(qkv, g * 4 + k), psQ[k][:, 0:3 * D], ACT.Copy).then_inc(copied, 1)
                skewed(act, NG, front, back)
                act.wait_ge(var_ready, 1)
                act.activation(t1[:], t0[:], ACT.Sqrt).then_inc(rooted, 1)

            @block.vector
            def _(dve):

                def front(g, s, j):
                    dve.wait_ge(turned, free_at(g))
                    for k in range(4):
                        i = g * 4 + k
                        n = dve.tensor_scalar(xh[:, s, k * P:k * P + P], tile_of(R.X, i), R.mean[:, ds(i, 1)],
                                              R.rstd[:, ds(i, 1)], ALU.subtract, ALU.mult)
                    n.then_inc(normed, 1)

                def back(g, s, j):
                    for k in range(4):
                        i = g * 4 + k
                        dve.wait_ge(copied, i + 1 + 4)
                        for n in range(3):
                            m = dve.bn_stats(tile_of(raw, i * 3 + n), qkv[:, ds(i, 1), n * D:n * D + D]
                                             .rearrange("p a d -> p (a d)"))
                        m.then_inc(statd, 1)
                skewed(dve, NG, front, back)
                dve.wait_ge(statd, NT)
                link = Chain(dve, chain)
                m0, v0, m1, v1 = (raw[:, :, c] for c in (1, 2, 4, 5))
                link(dve.tensor_tensor(mean[:], m0, m1, ALU.add))
                link(dve.tensor_tensor(t0[:], m0, m1, ALU.subtract))
                link(dve.tensor_tensor(t1[:], v0, v1, ALU.add))
                link(dve.tensor_scalar(mean[:], mean[:], 0.5, None, ALU.mult))
                link(dve.tensor_tensor(t0[:], t0[:], t0[:], ALU.mult))
                link(dve.tensor_scalar(t1[:], t1[:], 1.0 / D, 1e-6, ALU.mult, ALU.add))
                dve.scalar_tensor_tensor(out=t0[:], in0=t0[:], scalar=0.25, in1=t1[:], op0=ALU.mult,
                                         op1=ALU.add).then_inc(var_ready, 1)
                dve.wait_ge(rooted, 1)
                link(dve.reciprocal(rstd[:], t1[:]))
                dve.scalar_tensor_tensor(out=nbias[:], in0=mean[:], scalar=-1.0, in1=rstd[:], op0=ALU.mult,
                                         op1=ALU.mult)


def stage_linear2(nc, R, A, qkv, rstd, nbias):
    W = D + H2
    EK = 1e-6
    with Stage(nc, "linear2") as st:
        dw = st.sb("dw", [P, C2, D])
        db = st.sb("db", [P, D])
        gm, bt = st.sb("gm", [P, D]), st.sb("bt", [P, D])
        em = st.sb("em", [P, NT])
        mask = st.sb("mask", [P, W])
        n3 = st.sb("n3", [P, 2, 3, D])
        feat = st.sb("feat", [P, 2, 2, D])
        va = st.sb("va", [P, 2, W])
        kvm = st.sb("kvm", [P, 2, 2, W])
        qT = st.sb("qT", [P, 2, P])
        den, rd = st.sb("den", [P, 2, H2]), st.sb("rd", [P, 2, H2])
        rdm = st.sb("rdm", [P, 2, 2, H2, 4])
        spread = st.sb("spread", [P, 2, C2, 2, H2, 4])
        psK = st.ps("psK", [P, 2, 512])
        psT, psA, psO = ([st.ps(f"{n}{k}", [P, 512]) for k in range(2)] for n in ("psT", "psA", "psO"))
        names = ("wload", "ready", "n3d", "scaled", "shifted", "featd", "chain", "kvd", "kvmd", "qt", "qm", "attd",
                 "dchain", "spreadd", "outd", "outm")
        (wload, ready, n3d, scaled, shifted, featd, chain, kvd, kvmd, qt, qm, attd, dchain, spreadd, outd,
         outm) = (st.sem(n) for n in names)
        with nc.Block() as block:
            @block.sync
            def _(sp):
                sp.dma_start(dw[:], A["l2_dw"]).then_inc(wload, 16)
                sp.dma_start(db[:], A["l2_db"].partition_broadcast(P)).then_inc(wload, 16)
                sp.dma_start(gm[:], A["l2_g"].partition_broadcast(P)).then_inc(wload, 16)
                sp.dma_start(bt[:], A["l2_b"].partition_broadcast(P)).then_inc(wload, 16)
                sp.dma_start(em[:], A["l2_mask"]).then_inc(wload, 16)

            @block.scalar
            def _(act):
                act.sem_inc(qm, 2)

                def norm(i, s, j):
                    act.wait_ge(featd, free_at(i))
                    for n in range(3):
                        m = act.activation(n3[:, s, n, :], qkv[:, ds(i, 1), n * D:n * D + D].rearrange(
                            "p a d -> p (a d)"), ACT.Identity, bias=nbias[:, ds(i * 3 + n, 1)],
                            scale=rstd[:, ds(i * 3 + n, 1)])
                    m.then_inc(n3d, 1)

                def move_q(i, s, j):
                    act.wait_ge(qt, done_at(i))
                    act.wait_ge(attd, free_at(i))
                    act.activation(qT[:, s, :], psT[s][:, 0:P], ACT.Copy).then_inc(qm, 1)
                pipelined(act, NT, ((3, move_q), (0, norm)))

            @block.gpsimd
            def _(gp):
                gp.wait_ge(wload, 80)

                def affine(i, s, j):
                    gp.wait_ge(n3d, i + 1)
                    gp.tensor_tensor(n3[:, s, :, :], n3[:, s, :, :], bcast_mid(gm[:], 3), ALU.mult).then_inc(scaled, 1)
                    gp.wait_ge(scaled, i + 1)
                    gp.tensor_tensor(n3[:, s, :, :], n3[:, s, :, :], bcast_mid(bt[:], 3), ALU.add).then_inc(shifted, 1)
                two_slots(gp, NT, affine)

            @block.tensor
            def _(pe):
                for z in (kvd, qt, attd, outd):
                    pe.sem_inc(z, 2)
                pe.wait_ge(wload, 80)

                def key_values(i, s, j):
                    pe.wait_ge(featd, done_at(i))
                    pe.wait_ge(kvmd, i + 1)
                    for b in range(2):
                        r = slice(64 * b, 64 * b + 64)
                        m = pe.matmul(psK[:, b, 0:W], feat[r, s, 1, :], va[r, s, :], start=True, stop=True)
                    m.then_inc(kvd, 1)
                    pe.wait_ge(qm, free_at(i))
                    pe.transpose(psT[s][:, 0:P], feat[:, s, 0, :], R.ident[:]).then_inc(qt, 1)

                def attend(i, s, j):
                    pe.wait_ge(kvmd, i + 2)
                    pe.wait_ge(qm, done_at(i))
                    pe.wait_ge(spreadd, free_at(i))
                    for b in range(2):
                        m = pe.matmul(psA[s][64 * b:64 * b + 64, 0:W], qT[:, s, 64 * b:64 * b + 64], kvm[:, s, b, :],
                                      start=True, stop=True)
                    m.then_inc(attd, 1)

                def dense(i, s, j):
                    pe.wait_ge(spreadd, done_at(i))
                    pe.wait_ge(outm, free_at(i))
                    for e in range(C2):
                        m = pe.matmul(psO[s][:, 0:D], spread[:, s, e, :, :, :].rearrange("p b h n -> p (b h n)"),
                                      dw[:, e, :], start=(e == 0), stop=(e == C2 - 1))
                    m.then_inc(outd, 1)
                pipelined(pe, NT, ((6, dense), (4, attend), (2, key_values)))

            @block.vector
            def _(dve):
                for z in (featd, spreadd, outm):
                    dve.sem_inc(z, 2)
                dve.sem_inc(kvmd, 1)
                dve.tensor_copy(mask[:, 0:D], R.bd8[:].rearrange("p a b -> p (a b)")).then_inc(ready, 1)
                dve.tensor_copy(mask[:, D:W], R.bd8[:, :, 0]).then_inc(ready, 1)
                for s in range(2):
                    dve.memset(va[:, s, D:W], 1.0).then_inc(ready, 1)
                dve.wait_ge(ready, 4)
                dve.wait_ge(wload, 80)

                def features(i, s, j):
                    dve.wait_ge(shifted, i + 1)
                    dve.wait_ge(kvd, free_at(i))
                    dve.wait_ge(qt, free_at(i))
                    dve.tensor_scalar(feat[:, s, :, :], n3[:, s, 0:2, :], 0.0, EK, ALU.max, ALU.add).then_inc(chain, 1)
                    dve.tensor_scalar(va[:, s, 0:D], n3[:, s, 2, :], em[:, ds(i, 1)], None, ALU.mult)
                    dve.wait_ge(chain, i + 1)
                    dve.tensor_scalar(feat[:, s, 1, :], feat[:, s, 1, :], em[:, ds(i, 1)], None,
                                      ALU.mult).then_inc(featd, 1)

                def heads_only(i, s, j):
                    dve.wait_ge(kvd, done_at(i))
                    dve.wait_ge(attd, free_at(i))
                    dve.tensor_tensor(kvm[:, s, :, :], psK[:, :, 0:W], bcast_mid(mask[:], 2),
                                      ALU.mult).then_inc(kvmd, 1)

                def spreads(i, s, j):
                    link = Chain(dve, dchain, i * 3)
                    dve.wait_ge(attd, done_at(i))
                    link(dve.tensor_scalar(den[:, s, :], psA[s][:, D:W], EK, None, ALU.add))
                    link(dve.reciprocal(rd[:, s, :], den[:, s, :]))
                    link(dve.tensor_tensor(rdm[:, s, :, :, :], rd[:, s, :].rearrange("p (b h n) -> p b h n", b=1, n=1)
                                           .broadcast_to([P, 2, H2, 4]),
                                           R.bd16[:].rearrange("p (b h n) -> p b h n", b=2, h=1)
                                           .broadcast_to([P, 2, H2, 4]), ALU.mult))
                    dve.wait_ge(outd, free_at(i))
                    for b in range(2):
                        m = dve.tensor_tensor(spread[:, s, :, b, :, :],
                                              psA[s][:, 0:D].rearrange("p (h e a) -> p e h a", h=H2, a=1)
                                              .broadcast_to([P, C2, H2, 4]),
                                              rdm[:, s, b, :, :].rearrange("p (x h) n -> p x h n", x=1)
                                              .broadcast_to([P, C2, H2, 4]), ALU.mult)
                    m.then_inc(spreadd, 1)

                def move_out(i, s, j):
                    dve.wait_ge(outd, done_at(i))
                    dve.tensor_tensor(qkv[:, ds(i, 1), 0:D].rearrange("p a d -> p (a d)"), psO[s][:, 0:D], db[:],
                                      ALU.add).then_inc(outm, 1)
                pipelined(dve, NT, ((3, heads_only), (5, spreads), (7, move_out), (1, features)))


def stage_experts2(nc, R, A):
    NC = I2 // P
    with Stage(nc, "experts2") as st:
        w1 = st.sb("w1", [P, E2, I2])
        b1 = st.sb("b1", [E2, I2])
        wo = st.sb("wo", [P, NC, D])
        bo = st.sb("bo", [1, D])
        xh = st.sb("xh", [P, 2, 4, D])
        xm = st.sb("xm", [P, 2, E2, D])
        xmT = st.sb("xmT", [P, 2, E2, 4, P])
        hots = st.sb("hots", [P, 2, 4, E2])
        hotT = st.sb("hotT", [E2, 2, GW])
        hT = st.sb("hT", [P, 2, NC, GW])
        psT, psH, psY = ([st.ps(f"{n}{k}", [P, 512]) for k in range(2)] for n in ("psT", "psH", "psY"))
        psB = st.ps("psB", [P, 512])
        wload = st.sem("wload")
        normed, masked, turned, tmoved, hot, hotm, hid, act_d, yd, added = (
            st.sem(n) for n in ("normed", "masked", "turned", "tmoved", "hot", "hotm", "hid", "act_d", "yd", "added"))
        with nc.Block() as block:
            @block.sync
            def _(sp):
                sp.dma_start(w1[:], A["f2_w1"].rearrange("e d i -> d e i")).then_inc(wload, 16)
                sp.dma_start(b1[:], A["f2_b1"]).then_inc(wload, 16)
                sp.dma_start(wo[:], A["f2_wo"].rearrange("(c p) d -> p c d", p=P)).then_inc(wload, 16)
                sp.dma_start(bo[:], A["f2_bo"]).then_inc(wload, 16)

            @block.vector
            def _(dve):
                dve.sem_inc(added, 2)

                def front(g, s, j):
                    dve.wait_ge(added, g + 1)
                    dve.wait_ge(turned, g * 4 + 1)
                    dve.tensor_copy(hots[:, s, :, :].rearrange("p k e -> p (k e)"), R.wt[:, ds(g * 4 * E2, 4 * E2)])
                    for k in range(4):
                        i = g * 4 + k
                        n = dve.tensor_scalar(xh[:, s, k, :], tile_of(R.X, i), R.mean[:, ds(i, 1)],
                                              R.rstd[:, ds(i, 1)], ALU.subtract, ALU.mult)
                    n.then_inc(normed, 1)
                    dve.wait_ge(normed, g + 1)
                    for k in range(4):
                        dve.wait_ge(turned, g * 4 + k + 1)
                        dve.tensor_tensor(xm[:, k % 2, :, :], bcast_mid(xh[:, s, k, :], E2),
                                          bcast_in(R.wt[:, ds((g * 4 + k) * E2, E2)], D), ALU.mult
                                          ).then_inc(masked, 1)

                def back(g, s, j):
                    dve.wait_ge(yd, done_at(g))
                    dve.tensor_tensor(tiles_of(R.Y, g * 4, 4), psY[s][:].rearrange("p (k d) -> p k d", k=4),
                                      xh[:, s, :, :], ALU.add).then_inc(added, 1)
                skewed(dve, NG, front, back)

            @block.tensor
            def _(pe):
                pe.sem_inc(turned, 2)
                pe.sem_inc(hot, 1)
                pe.sem_inc(hid, 2)
                pe.sem_inc(yd, 2)
                pe.wait_ge(wload, 64)

                def first(g, s, j):
                    pe.wait_ge(hotm, g + 1)
                    pe.wait_ge(normed, g + 1)
                    for k in range(4):
                        t = pe.transpose(psB[0:E2, k * P:k * P + P], hots[:, s, k, :], R.ident[:])
                    t.then_inc(hot, 1)
                    for k in range(4):
                        pe.wait_ge(masked, g * 4 + k + 1)
                        pe.wait_ge(tmoved, g * 4 + k + 1)
                        for e in range(E2):
                            t = pe.transpose(psT[k % 2][:, e * P:e * P + P], xm[:, k % 2, e, :], R.ident[:])
                        t.then_inc(turned, 1)

                def second(g, s, j):
                    pe.wait_ge(tmoved, g * 4 + 4 + 2)
                    pe.wait_ge(hotm, g + 1 + 1)
                    for c in range(NC):
                        pe.wait_ge(act_d, g * NC + c + 1)
                        cols = slice(c * P, c * P + P)
                        for e in range(E2):
                            pe.matmul(psH[c % 2][:], w1[:, e, cols], xmT[:, s, e, :, :].rearrange("p k t -> p (k t)"),
                                      start=(e == 0), stop=False)
                        pe.matmul(psH[c % 2][:], b1[:, cols], hotT[:, s, :], start=False, stop=True).then_inc(hid, 1)

                def third(g, s, j):
                    pe.wait_ge(act_d, g * NC + NC + 2)
                    pe.wait_ge(added, free_at(g))
                    for k in range(4):
                        y = psY[s][:, k * P:k * P + P]
                        for c in range(NC):
                            pe.matmul(y, hT[:, s, c, k * P:k * P + P], wo[:, c, :], start=(c == 0), stop=False)
                        m = pe.matmul(y, R.ones[0:1, 0:P], bo[:], start=False, stop=True)
                    m.then_inc(yd, 1)
                three_steps(pe, NG, first, second, third)

            @block.scalar
            def _(act):
                act.sem_inc(tmoved, 2)
                act.sem_inc(hotm, 1)
                act.sem_inc(act_d, 2)

                def front(g, s, j):
                    act.wait_ge(hot, g + 1 + 1)
                    act.wait_ge(hid, g * NC + 1)
                    act.activation(hotT[:, s, :], psB[0:E2, :], ACT.Copy).then_inc(hotm, 1)
                    for k in range(4):
                        act.wait_ge(turned, g * 4 + k + 1 + 2)
                        act.activation(xmT[:, s, :, k, :], psT[k % 2][:].rearrange("p (e t) -> p e t", e=E2), ACT.Copy
                                       ).then_inc(tmoved, 1)

                def back(g, s, j):
                    act.wait_ge(yd, free_at(g))
                    for c in range(NC):
                        act.wait_ge(hid, g * NC + c + 1 + 2)
                        act.activation(hT[:, s, c, :], psH[c % 2][:], ACT.Gelu).then_inc(act_d, 1)

                front(0, 0, 0)
                with act.Fori(0, NG // 2 - 1) as j:
                    back(2 * j, 0, j)
                    front(2 * j + 1, 1, j)
                    back(2 * j + 1, 1, j)
                    front(2 * j + 2, 0, j + 1)
                back(NG - 2, 0, NG // 2 - 1)
                front(NG - 1, 1, NG // 2 - 1)
                back(NG - 1, 1, NG // 2 - 1)


def stage_norm_add(nc, R, name, gamma, beta, Y):
    with Stage(nc, name) as st:
        gm, bt = st.sb("gm", [P, D]), st.sb("bt", [P, D])
        loaded, shifted, scaled = st.sem("loaded"), st.sem("shifted"), st.sem("scaled")
        with nc.Block() as block:
            @block.sync
            def _(sp):
                sp.dma_start(gm[:], gamma.partition_broadcast(P)).then_inc(loaded, 16)
                sp.dma_start(bt[:], beta.partition_broadcast(P)).then_inc(loaded, 16)

            @block.gpsimd
            def _(gp):
                gp.wait_ge(loaded, 32)
                with gp.Fori(0, NG) as g:
                    x = tiles_of(R.X, g * 4, 4)
                    gp.tensor_tensor(x, x, bcast_mid(bt[:], 4), ALU.add).then_inc(shifted, 1)

            @block.vector
            def _(dve):
                dve.wait_ge(loaded, 32)
                with dve.Fori(0, NG) as g:
                    for k in range(4):
                        i = g * 4 + k
                        y = tile_of(Y, i)
                        dve.scalar_tensor_tensor(out=y, in0=y, scalar=R.mean[:, ds(i, 1)], in1=gm[:],
                                                 op0=ALU.subtract, op1=ALU.mult).then_inc(scaled, 1)
                    dve.wait_ge(shifted, g + 1)
                    for k in range(4):
                        i = g * 4 + k
                        dve.wait_ge(scaled, i + 1)
                        dve.scalar_tensor_tensor(out=tile_of(R.X, i), in0=tile_of(Y, i), scalar=R.rstd[:, ds(i, 1)],
                                                 in1=tile_of(R.X, i), op0=ALU.mult, op1=ALU.add)


def stage_bilinear3(nc, R, A):
    with Stage(nc, "bilinear3") as st:
        wq, wkv, wo = st.sb("wq", [P, D]), st.sb("wkv", [P, 2 * D]), st.sb("wo", [P, D])
        mask = st.sb("mask", [P, D])
        cT = st.sb("cT", [P, 2, GW])
        qT = st.sb("qT", [P, 2, GW])
        kv = st.sb("kv", [P, 2, 4, 2, D])
        mT = st.sb("mT", [P, 2, 2, 4, D])
        gg = st.sb("gg", [P, 2, 2, 4, D])
        psQ = st.ps("psQ", [P, 512])
        psK = [st.ps(f"psK{k}", [P, 512]) for k in range(2)]
        psM = [st.ps(f"psM{k}", [P, 512]) for k in range(2)]
        psG = [st.ps(f"psG{k}", [P, 512]) for k in range(2)]
        psY = st.ps("psY", [P, 512])
        wload, cload = st.sem("wload"), [st.sem("cload0"), st.sem("cload1")]
        qd, qm, kd, km, md, mm, gd, gmv, yd, added, ready = (
            st.sem(n) for n in ("qd", "qm", "kd", "km", "md", "mm", "gd", "gmv", "yd", "added", "ready"))
        with nc.Block() as block:
            @block.sync
            def _(sp):
                sp.dma_start(wq[:], A["l3_wqT"]).then_inc(wload, 16)
                sp.dma_start(wkv[:, 0:D], A["l3_wkT"]).then_inc(wload, 16)
                sp.dma_start(wkv[:, D:], A["l3_wvT"]).then_inc(wload, 16)
                sp.dma_start(wo[:], A["l3_woT"]).then_inc(wload, 16)

                def body(g, s, j):
                    sp.wait_ge(kd, 2 * g + 2)
                    sp.dma_start(cT[:, s, :], A["ctxT"][:, ds(g * GW, GW)]).then_inc(cload[s], 16)
                two_slots(sp, NG, body)

            @block.tensor
            def _(pe):
                pe.sem_inc(qd, 2)
                pe.sem_inc(kd, 4)
                for z in (md, gd, yd):
                    pe.sem_inc(z, 2)
                pe.wait_ge(wload, 64)

                def first(g, s, j):
                    pe.wait_ge(cload[s], j * 16 + 16)
                    for h in range(2):
                        pe.wait_ge(km, 2 * g + h + 1)
                        for k in range(2):
                            t = 2 * h + k
                            m = pe.matmul(psK[h][:, 256 * k:256 * k + 256], cT[:, s, t * P:t * P + P], wkv[:],
                                          start=True, stop=True)
                        m.then_inc(kd, 1)
                    pe.wait_ge(qm, g + 1)
                    pe.matmul(psQ[:], wq[:], R.XT[:, ds(g * GW, GW)], start=True, stop=True).then_inc(qd, 1)

                def second(g, s, j):
                    pe.wait_ge(km, 2 * g + 2 + 2)
                    pe.wait_ge(mm, g + 1)
                    for b in range(2):
                        r = slice(64 * b, 64 * b + 64)
                        for k in range(4):
                            m = pe.matmul(psM[b][:, k * P:k * P + P], kv[r, s, k, 1, :], kv[r, s, k, 0, :],
                                          start=True, stop=True)
                    m.then_inc(md, 1)

                def third(g, s, j):
                    pe.wait_ge(mm, g + 2)
                    pe.wait_ge(gmv, g + 1)
                    for b in range(2):
                        for k in range(4):
                            m = pe.matmul(psG[b][:, k * P:k * P + P], mT[:, s, b, k, :], wo[:], start=True, stop=True)
                    m.then_inc(gd, 1)

                def fourth(g, s, j):
                    pe.wait_ge(gmv, g + 2)
                    pe.wait_ge(added, g + 1)
                    pe.wait_ge(qm, g + 2)
                    for b in range(2):
                        for k in range(4):
                            m = pe.matmul(psY[64 * b:64 * b + 64, k * P:k * P + P],
                                          qT[:, s, k * P + 64 * b:k * P + 64 * b + 64], gg[:, s, b, k, :],
                                          start=True, stop=True)
                    m.then_inc(yd, 1)

                first(0, 0, 0)
                second(0, 0, 0)

                def round_of(u, s, j, j1):
                    first(u + 1, 1 - s, j1)
                    third(u, s, j)
                    second(u + 1, 1 - s, j1)
                    fourth(u, s, j)
                with pe.Fori(0, NG // 2 - 1) as j:
                    round_of(2 * j, 0, j, j)
                    round_of(2 * j + 1, 1, j, j + 1)
                last = NG // 2 - 1
                round_of(NG - 2, 0, last, last)
                third(NG - 1, 1, last)
                fourth(NG - 1, 1, last)

            @block.scalar
            def _(act):
                act.sem_inc(km, 2)
                act.sem_inc(qm, 1)
                act.sem_inc(gmv, 1)

                def front(g, s, j):
                    for h in range(2):
                        act.wait_ge(kd, 2 * g + h + 1 + 4)
                        act.wait_ge(md, free_at(g))
                        act.activation(kv[:, s, 2 * h:2 * h + 2, :, :].rearrange("p a b d -> p (a b d)"), psK[h][:],
                                       ACT.Copy).then_inc(km, 1)
                    act.wait_ge(qd, done_at(g))
                    act.wait_ge(yd, free_at(g))
                    act.activation(qT[:, s, :], psQ[:], ACT.Copy).then_inc(qm, 1)

                def back(g, s, j):
                    act.wait_ge(gd, done_at(g))
                    act.wait_ge(yd, free_at(g))
                    act.activation(gg[:, s, 0, :, :].rearrange("p k d -> p (k d)"), psG[0][:], ACT.Copy)
                    act.activation(gg[:, s, 1, :, :].rearrange("p k d -> p (k d)"), psG[1][:],
                                   ACT.Copy).then_inc(gmv, 1)
                skewed(act, NG, front, back)

            @block.vector
            def _(dve):
                dve.tensor_scalar(mask[:], R.bd8[:].rearrange("p a b -> p (a b)"), C2 ** -0.5, None,
                                  ALU.mult).then_inc(ready, 1)
                dve.sem_inc(mm, 1)
                dve.sem_inc(added, 1)
                dve.wait_ge(ready, 1)

                def front(g, s, j):
                    dve.wait_ge(md, done_at(g))
                    dve.wait_ge(gd, free_at(g))
                    for b in range(2):
                        m = dve.tensor_tensor(mT[:, s, b, :, :], psM[b][:].rearrange("p (k d) -> p k d", k=4),
                                              bcast_mid(mask[:], 4), ALU.mult)
                    m.then_inc(mm, 1)

                def back(g, s, j):
                    dve.wait_ge(yd, done_at(g))
                    x = tiles_of(R.X, g * 4, 4)
                    dve.tensor_tensor(x, psY[:].rearrange("p (k d) -> p k d", k=4), x, ALU.add).then_inc(added, 1)
                skewed(dve, NG, front, back)


def stage_experts3(nc, R, A):
    NC = I3 // P
    with Stage(nc, "experts3") as st:
        fc = st.sb("fc", [P, E3, I3])
        proj = st.sb("proj", [P, E3, NC, D])
        hT = st.sb("hT", [P, 2, NC, GW])
        psH = [st.ps(f"psH{k}", [P, 512]) for k in range(4)]
        psY = [st.ps(f"psY{k}", [P, 512]) for k in range(2)]
        wload, hid, gelud, yd, used = (st.sem(n) for n in ("wload", "hid", "gelud", "yd", "used"))
        with nc.Block() as block:
            @block.sync
            def _(sp):
                sp.dma_start(fc[:], A["f3_fc"].rearrange("e d i -> d e i")).then_inc(wload, 16)
                sp.dma_start(proj[:], A["f3_proj"].rearrange("e (c p) d -> p e c d", p=P)).then_inc(wload, 16)

            @block.tensor
            def _(pe):
                pe.sem_inc(yd, 2)
                pe.wait_ge(wload, 32)

                def hidden(g, e):
                    for c in range(NC):
                        pe.wait_ge(gelud, (g * E3 + e) * NC + c + 1)
                        pe.matmul(psH[c][:], fc[:, e, c * P:c * P + P], R.XT[:, ds(g * GW, GW)], start=True,
                                  stop=True).then_inc(hid, 1)

                def project(g, e):
                    pe.wait_ge(gelud, (g * E3 + e) * NC + NC + 4)
                    pe.wait_ge(used, (g * E3 + e) * 4 + 4)
                    for k in range(4):
                        for c in range(NC):
                            m = pe.matmul(psY[e % 2][:, k * P:k * P + P], hT[:, e % 2, c, k * P:k * P + P],
                                          proj[:, e, c, :], start=(c == 0), stop=(c == NC - 1))
                    m.then_inc(yd, 1)

                def group(g, last=False):
                    for e in range(E3):
                        if e < E3 - 1:
                            hidden(g, e + 1)
                        elif not last:
                            hidden(g + 1, 0)
                        project(g, e)
                hidden(0, 0)
                with pe.Fori(0, NG - 1) as g:
                    group(g)
                group(NG - 1, last=True)

            @block.scalar
            def _(act):
                act.sem_inc(gelud, 4)
                with act.Fori(0, NG) as g:
                    for e in range(E3):
                        act.wait_ge(yd, g * E3 + e + 1)
                        for c in range(NC):
                            act.wait_ge(hid, (g * E3 + e) * NC + c + 1)
                            act.activation(hT[:, e % 2, c, :], psH[c][:], ACT.Gelu).then_inc(gelud, 1)

            @block.vector
            def _(dve):
                dve.sem_inc(used, 8)
                with dve.Fori(0, NG) as g:
                    for e in range(E3):
                        dve.wait_ge(yd, g * E3 + e + 1 + 2)
                        for k in range(4):
                            i = g * 4 + k
                            dve.wait_ge(used, (g * E3 + e) * 4 + k + 1 + 4)
                            x = tile_of(R.X, i)
                            dve.scalar_tensor_tensor(out=x, in0=psY[e % 2][:, k * P:k * P + P],
                                                     scalar=R.wt[:, ds(i * E3 + e, 1)], in1=x, op0=ALU.mult,
                                                     op1=ALU.add).then_inc(used, 1)


def program(nc, A, out):
    ctx = ExitStack()
    with ctx:
        def sb(name, shape, dt=F32):
            return ctx.enter_context(nc.sbuf_tensor(name, shape, dt))

        R = Resident()
        R.X = sb("X", [P, NT, D])
        R.ident, R.same2, R.tri_incl, R.tri_strict = (
            sb(n, [P, P]) for n in ("ident", "same2", "tri_incl", "tri_strict"))
        R.ident_bf, R.causal = sb("ident_bf", [P, P], BF16), sb("causal", [P, 512], BF16)
        R.delta, R.ones = sb("delta", [P, S]), sb("ones", [P, 512])
        R.bd16, R.bd16q = sb("bd16", [P, H0]), sb("bd16q", [P, H0])
        R.bd8 = sb("bd8", [P, H2, C2])
        R.vmask = sb("vmask", [P, 4, 2, C0])
        R.vmask128 = R.vmask[:].rearrange("p a b c -> p (a b c)")
        R.stats, R.t0, R.t1 = sb("stats", [P, NT, 6]), sb("t0", [P, NT]), sb("t1", [P, NT])
        R.mean, R.rstd = sb("mean", [P, NT]), sb("rstd", [P, NT])
        R.cs, R.g = sb("cs", [P, NT * H0]), sb("g", [P, NT, H0])
        R.rowmax, R.rowsum = sb("rowmax", [P, NT, H0]), sb("rowsum", [P, NT, H0])
        R.khop = nc.dram_tensor("khop", (B, S, H0 * S), F32, kind="Internal").ap()

        def finish():
            with Stage(nc, "store") as st:
                stored = st.sem("stored")
                with nc.Block() as block:
                    @block.sync
                    def _(sp):
                        sp.dma_start(out.rearrange("(i p) d -> p i d", p=P), R.X[:]).then_inc(stored, 16)
                        sp.wait_ge(stored, 16)

        stage_setup(nc, R, A)
        with nc.sbuf_tensor("XT", [P, TOK], F32) as R.XT:
            stage_stats(nc, R, "stats0")
            with nc.sbuf_tensor("G", [P, NT * 2 * H0], F32) as R.G:
                w = [A["gate_wT"][n * P:(n + 1) * P, :] for n in range(3)]
                stage_norm_T(nc, R, "norm0", w[0], 2 * H0, R.G, A["ctxT"], w[1:], A["gate_b"])
                stage_gates(nc, R, A)
            stage_hop(nc, R, A)
            with nc.sbuf_tensor("Y", [P, NT, D], F32) as R.Y:
                stage_mlstm(nc, R, A)
                stage_headnorm(nc, R, A)
            stage_stats(nc, R, "stats1")
            stage_norm_T(nc, R, "norm1")
            stage_scan(nc, R, A)
        R.lg, R.wt = sb("lg", [P, 512]), sb("wt", [P, 512])
        stage_stats(nc, R, "stats2")
        stage_attend(nc, R, A)
        with nc.sbuf_tensor("XT3", [P, TOK], F32) as R.XT:
            stage_stats(nc, R, "stats3")
            stage_norm_T(nc, R, "norm3", A["f1_wrT"], E1, R.lg)
            stage_route(nc, R, "route3", E1, True, CAP)
            stage_experts1(nc, R, A)
        stage_stats(nc, R, "stats4")
        with (nc.sbuf_tensor("qkv", [P, NT, 3 * D], F32) as qkv, nc.sbuf_tensor("mean3", [P, 3 * NT], F32) as mean3,
              nc.sbuf_tensor("rstd3", [P, 3 * NT], F32) as rstd3, nc.sbuf_tensor("nbias3", [P, 3 * NT], F32) as nbias3):
            stage_project2(nc, R, A, qkv, mean3, rstd3, nbias3)
            stage_linear2(nc, R, A, qkv, rstd3, nbias3)
            y = qkv[:, :, 0:D]
            stage_stats(nc, R, "stats4y", y, 1e-6)
            stage_norm_add(nc, R, "add4", A["l2_g"], A["l2_b"], y)
        R.XT = sb("XT5", [P, TOK])
        stage_stats(nc, R, "stats5")
        stage_norm_T(nc, R, "norm5", A["f2_wr"], E2, R.lg)
        stage_route(nc, R, "route5", E2, False, 0)
        with nc.sbuf_tensor("Y2", [P, NT, D], F32) as R.Y:
            stage_experts2(nc, R, A)
            stage_stats(nc, R, "stats5y", R.Y, 1e-12)
            stage_norm_add(nc, R, "add5", A["f2_g"], A["f2_b"], R.Y)
        stage_stats(nc, R, "stats6")
        stage_norm_T(nc, R, "norm6")
        stage_bilinear3(nc, R, A)
        stage_stats(nc, R, "stats7")
        stage_norm_T(nc, R, "norm7", A["f3_gate"], E3, R.lg)
        stage_route(nc, R, "route7", E3, True, 0)
        stage_experts3(nc, R, A)
        finish()


def laid_out(a):
    import numpy as np

    f = lambda n: np.asarray(a[n])
    c = np.ascontiguousarray
    ctx = f("ctx_1024").reshape(TOK, D)
    return {
        "x": f("x").reshape(TOK, D), "ctx": ctx, "ctxT": c(ctx.T),
        "hopsT": c(f("itok_SxS2_0_2016").reshape(S // 2, 2 * S).T), "rpe": f("L0_xattn_rpe"),
        "gate_wT": c(np.concatenate([f("L0_xattn_igate_w"), f("L0_xattn_fgate_w")]).T),
        "gate_b": np.concatenate([f("L0_xattn_igate_b"), f("L0_xattn_fgate_b")]),
        "ln_w": f("L0_xattn_ln_w"), "ln_b": f("L0_xattn_ln_b"),
        "lstm_wT": c(np.stack([f(f"L0_ffn_w{g}").T for g in "fico"])),
        "lstm_uT": c(np.stack([f(f"L0_ffn_u{g}").T for g in "fico"])),
        "lstm_bT": c(np.stack([f(f"L0_ffn_b{g}") for g in "fico"]).T),
        "in_c": f("L0_ffn_in_c"),
        "a1_wq": f("L1_xattn_Wq").reshape(D, H1 * C1), "a1_wk": f("L1_xattn_Wk").reshape(D, H1 * C1),
        "a1_wv": f("L1_xattn_Wv").reshape(D, H1 * C1),
        "a1_wo": c(f("L1_xattn_Wo").reshape(HP1, 2 * C1, D).transpose(1, 0, 2)),
        "a1_bqT": c(f("L1_xattn_bq").reshape(HP1, 2 * C1).T), "a1_bkT": c(f("L1_xattn_bk").reshape(HP1, 2 * C1).T),
        "a1_bvT": c(f("L1_xattn_bv").reshape(HP1, 2 * C1).T), "a1_bo": f("L1_xattn_bo")[None],
        "f1_wrT": c(f("L1_ffn_Wr").T), "f1_we": f("L1_ffn_We"),
        "l2_wq": f("L2_xattn_wq"), "l2_wk": f("L2_xattn_wk"), "l2_wv": f("L2_xattn_wv"),
        "l2_g": f("L2_xattn_ln_gamma"), "l2_b": f("L2_xattn_ln_beta"), "l2_dw": np.tile(f("L2_xattn_dense_w").reshape(H2, C2, D), (P // H2, 1, 1)),
        "f2_wr": f("L2_ffn_W_router"), "f2_w1": f("L2_ffn_W1"), "f2_b1": f("L2_ffn_b1"), "f2_wo": f("L2_ffn_Wo"),
        "f2_bo": f("L2_ffn_bo")[None], "f2_g": f("L2_ffn_ln_gamma"), "f2_b": f("L2_ffn_ln_beta"),
        "l3_wqT": c(f("L3_xattn_Wq").T), "l3_wkT": c(f("L3_xattn_Wk").T), "l3_wvT": c(f("L3_xattn_Wv").T),
        "l3_woT": c(f("L3_xattn_Wo").T), "f3_gate": f("L3_ffn_gate_w"), "f3_fc": f("L3_ffn_fc_w"),
        "f3_proj": f("L3_ffn_proj_w"),
        "l2_db": f("L2_xattn_dense_b"), "l2_mask": c(f("mask_BxS2_ff1").reshape(NT, P).T),
    }


def build(nc, arrays):
    A = {
        name: nc.dram_tensor(f"in_{name}", a.shape, mybir.dt.from_np(a.dtype), kind="ExternalInput").ap()
        for name, a in arrays.items()}
    out = nc.dram_tensor("out", (TOK, D), F32, kind="ExternalOutput").ap()
    program(nc, A, out)


def kernel(**inputs):
    import concourse.bacc as bacc
    from concourse.bass_utils import run_bass_kernel_spmd

    arrays = laid_out(inputs)
    nc = bacc.Bacc("TRN2", target_bir_lowering=False, num_devices=1)
    build(nc, arrays)
    got = run_bass_kernel_spmd(nc, [{f"in_{n}": a for n, a in arrays.items()}], core_ids=[0])
    return got.results[0]["out"].reshape(B, S, D)
```

```python
from contextlib import ExitStack

import concourse.bass as bass
from concourse import mybir

F32 = mybir.dt.float32
BF16 = mybir.dt.bfloat16
I32 = mybir.dt.int32
F32R = mybir.dt.float32r
ALU = mybir.AluOpType
ACT = mybir.ActivationFunctionType
AX_X = mybir.AxisListType.X
ds = bass.ds

P = 128
B, S, D = 128, 64, 128
TOK = B * S
NT = TOK // P
NG = NT // 4
GW = 4 * P
LN_EPS = 1e-5

H0, C0 = 8, 16
H1, C1 = 16, 64
HP1 = H1 // 2
E1, CAP = 8, 25
H2, C2 = 16, 8
E2, I2 = 4, 512
E3, I3 = 8, 512
NEG = -1e30


def tile_of(t, i):
    return t[:, ds(i, 1), :].rearrange("p a w -> p (a w)")


def tiles_of(t, i, n):
    return t[:, ds(i, n), :]


def skewed(eng, units, front, back):
    front(0, 0, 0)
    with eng.Fori(0, units // 2 - 1) as j:
        front(2 * j + 1, 1, j)
        back(2 * j, 0, j)
        front(2 * j + 2, 0, j + 1)
        back(2 * j + 1, 1, j)
    last = units // 2 - 1
    front(units - 1, 1, last)
    back(units - 2, 0, last)
    back(units - 1, 1, last)


def two_slots(eng, units, body):
    with eng.Fori(0, units // 2) as j:
        body(2 * j, 0, j)
        body(2 * j + 1, 1, j)


def pipelined(eng, units, steps):
    deepest = max(lag for lag, _ in steps)
    full = (deepest + 1) // 2 * 2

    def one_round(n, j=None):
        for lag, step in steps:
            if j is not None:
                step(2 * j + (n - lag), (n - lag) % 2, j + (n - lag) // 2)
            elif 0 <= n - lag < units:
                step(n - lag, (n - lag) % 2, (n - lag) // 2)

    for n in range(full):
        one_round(n)
    with eng.Fori(0, (units - full) // 2) as j:
        one_round(full, j)
        one_round(full + 1, j)
    for n in range(units, units + deepest):
        one_round(n)


def octets(eng, total, steps):
    lags = [lag for lag, _ in steps]
    before = (max(lags) + 7) // 8 * 8

    def one_round(n, j=None):
        for lag, step in steps:
            c = n - lag
            if j is not None:
                step(8 * j + c, c, j)
            elif 0 <= c < total:
                step(c, c, 0)

    for n in range(min(lags), before):
        one_round(n)
    with eng.Fori(0, (total - 8 - before) // 8) as j:
        for k in range(8):
            one_round(before + k, j)
    for n in range(total - 8, total + max(lags)):
        one_round(n)


def take_high(dve, high, x):
    return dve.tensor_copy(high.bitcast(F32R), x)


def take_low(dve, low, x, high):
    return dve.tensor_tensor(low.bitcast(F32R), x, high, ALU.subtract)


def matmul_split(pe, out, lhsT, rhs, start=True, stop=True):
    pairs = ((0, 0), (0, 1), (1, 0))
    for n, (a, b) in enumerate(pairs):
        m = pe.matmul(out, lhsT[a].bitcast(F32R), rhs[b].bitcast(F32R), start=start and n == 0, stop=stop and n == 2)
    return m


class Chain:

    def __init__(self, eng, sem, base=0):
        self.eng, self.sem, self.base, self.n = eng, sem, base, 0

    def __call__(self, ins):
        self.n += 1
        ins.then_inc(self.sem, 1)
        self.eng.wait_ge(self.sem, self.base + self.n)


def free_at(u):
    return u + 1


def done_at(u, n=2):
    return u + 1 + n


def bcast_mid(ap, n):
    return ap.rearrange("p (a w) -> p a w", a=1).broadcast_to([ap.shape[0], n, ap.shape[1]])


def bcast_in(ap, n):
    return ap.rearrange("p (w a) -> p w a", a=1).broadcast_to([ap.shape[0], ap.shape[1], n])


class Stage:

    def __init__(self, nc, name):
        self.nc, self.name, self.ctx, self.sems = nc, name, ExitStack(), []

    def __enter__(self):
        self.ctx.__enter__()
        return self

    def __exit__(self, *e):
        if not e[0]:
            self.nc.clear_and_free_semaphores(self.sems)
            self.nc.all_engine_barrier()
        return self.ctx.__exit__(*e)

    def sb(self, name, shape, dt=F32):
        return self.ctx.enter_context(self.nc.sbuf_tensor(f"{self.name}_{name}", shape, dt))

    def ps(self, name, shape, dt=F32):
        return self.ctx.enter_context(self.nc.psum_tensor(f"{self.name}_{name}", shape, dt))

    def sem(self, name):
        self.sems.append(self.nc.alloc_semaphore(name=f"{self.name}_{name}"))
        return self.sems[-1]


class Resident:
    pass


def stage_setup(nc, R, A):
    with Stage(nc, "setup") as st:
        loaded, made, zeroed = [st.sem(f"loaded{n}") for n in range(4)], st.sem("made"), st.sem("zeroed")
        with nc.Block() as block:
            @block.sync
            def _(sp):
                for n in range(4):
                    sp.dma_start(R.X[:, n * NG:(n + 1) * NG, :],
                                 A["x"][n * NG * P:(n + 1) * NG * P, :].rearrange("(i p) d -> p i d", p=P)
                                 ).then_inc(loaded[n], 16)

            @block.vector
            def _(dve):
                for t in (R.ident, R.same2, R.tri_incl, R.tri_strict, R.delta, R.bd16, R.bd8,
                          R.vmask, R.causal, R.ident_bf):
                    dve.memset(t[:], 0.0).then_inc(zeroed, 1)
                dve.memset(R.ones[:], 1.0)
                dve.wait_ge(zeroed, 10)
                for h in range(2):
                    rows = slice(64 * h, 64 * h + 64)
                    for t in (R.same2, R.tri_incl, R.tri_strict):
                        dve.memset(t[rows, 64 * h:64 * h + 64], 1.0).then_inc(zeroed, 1)
                    dve.memset(R.vmask[rows, :, h, :], 1.0).then_inc(zeroed, 1)
                dve.memset(R.bd16[:], 1.0).then_inc(zeroed, 1)
                dve.memset(R.bd8[:], 1.0).then_inc(zeroed, 1)
                for n in range(4):
                    dve.wait_ge(loaded[n], 16)
                    with dve.Fori(0, NG // 4) as g:
                        for k in range(4):
                            i = n * NG + g * 4 + k
                            dve.bn_stats(tile_of(R.stats, i), tile_of(R.X, i))

            @block.gpsimd
            def _(gp):
                gp.wait_ge(zeroed, 20)
                link = Chain(gp, made)
                for t in (R.ident, R.ident_bf):
                    link(gp.affine_select(out=t[:], in_=t[:], compare_op=ALU.not_equal, fill=1.0, base=0,
                                     pattern=[[-1, 128]], channel_multiplier=1))
                link(gp.affine_select(out=R.tri_incl[:], in_=R.tri_incl[:], compare_op=ALU.is_ge, fill=0.0,
                                 base=0, pattern=[[1, 128]], channel_multiplier=-1))
                link(gp.affine_select(out=R.tri_strict[:], in_=R.tri_strict[:], compare_op=ALU.is_gt, fill=0.0,
                                 base=0, pattern=[[1, 128]], channel_multiplier=-1))
                for h in range(2):
                    rows = slice(64 * h, 64 * h + 64)
                    link(gp.affine_select(out=R.delta[rows, :], in_=R.delta[rows, :], compare_op=ALU.not_equal,
                                     fill=1.0, base=0, pattern=[[-1, 64]], channel_multiplier=1))
                    c = R.causal[rows, :].rearrange("p (h t) -> p h t", h=H0)
                    link(gp.affine_select(out=c, in_=c, compare_op=ALU.is_ge, fill=NEG, base=0,
                                     pattern=[[0, H0], [-1, S]], channel_multiplier=1))
                link(gp.affine_select(out=R.bd16[:], in_=R.bd16[:], compare_op=ALU.is_ge, fill=0.0, base=0,
                                 pattern=[[-C0, H0]], channel_multiplier=1))
                link(gp.affine_select(out=R.bd16[:], in_=R.bd16[:], compare_op=ALU.is_ge, fill=0.0, base=C0 - 1,
                                 pattern=[[C0, H0]], channel_multiplier=-1))
                link(gp.affine_select(out=R.bd8[:], in_=R.bd8[:], compare_op=ALU.is_ge, fill=0.0, base=0,
                                 pattern=[[-C2, H2], [0, C2]], channel_multiplier=1))
                link(gp.tensor_scalar(R.bd16q[:], R.bd16[:], 1.0 / C0 ** 0.5, None, ALU.mult))
                link(gp.affine_select(out=R.bd8[:], in_=R.bd8[:], compare_op=ALU.is_ge, fill=0.0, base=C2 - 1,
                                 pattern=[[C2, H2], [0, C2]], channel_multiplier=-1))


def stage_stats(nc, R, name, eps=LN_EPS, collected=False):
    with Stage(nc, name) as st:
        raw, t0, t1 = R.stats, R.t0, R.t1
        chain, rooted, var_ready = st.sem("chain"), st.sem("rooted"), st.sem("var_ready")
        with nc.Block() as block:
            @block.vector
            def _(dve):
                if collected:
                    dve.sem_inc(chain, NT)
                else:
                    with dve.Fori(0, NG) as g:
                        for k in range(4):
                            i = g * 4 + k
                            dve.bn_stats(tile_of(raw, i), tile_of(R.X, i)).then_inc(chain, 1)
                    dve.wait_ge(chain, NT)
                m0, v0, m1, v1 = (raw[:, :, c] for c in (1, 2, 4, 5))
                dve.tensor_tensor(R.mean[:], m0, m1, ALU.add).then_inc(chain, 1)
                dve.tensor_tensor(t0[:], m0, m1, ALU.subtract).then_inc(chain, 1)
                dve.tensor_tensor(t1[:], v0, v1, ALU.add).then_inc(chain, 1)
                dve.wait_ge(chain, NT + 3)
                dve.tensor_scalar(R.mean[:], R.mean[:], 0.5, None, ALU.mult).then_inc(chain, 1)
                dve.tensor_tensor(t0[:], t0[:], t0[:], ALU.mult).then_inc(chain, 1)
                dve.tensor_scalar(t1[:], t1[:], 1.0 / D, eps, ALU.mult, ALU.add).then_inc(chain, 1)
                dve.wait_ge(chain, NT + 6)
                dve.scalar_tensor_tensor(out=t0[:], in0=t0[:], scalar=0.25, in1=t1[:], op0=ALU.mult,
                                         op1=ALU.add).then_inc(var_ready, 1)
                dve.wait_ge(rooted, 1)
                dve.reciprocal(R.rstd[:], t1[:]).then_inc(chain, 1)

            @block.scalar
            def _(act):
                act.wait_ge(var_ready, 1)
                act.activation(t1[:], t0[:], ACT.Sqrt).then_inc(rooted, 1)



def stage_norm_T(nc, R, name, w=None, E=0, logits=None, ctxT=None, w_ctx=(), bias=None, gather=None):
    with Stage(nc, name) as st:
        xh = st.sb("xh", [P, 2, 4, P])
        ps = [st.ps(f"ps{k}", [P, GW]) for k in range(2)]
        normed, turned, moved = (st.sem(n) for n in ("normed", "turned", "moved"))
        if w is not None:
            xs = st.sb("xs", [P, 2, GW])
            ws = st.sb("ws", [P, E])
            psL = [st.ps(f"psL{k}", [P, GW]) for k in range(2)]
            wload, prod, taken, ready = (st.sem(n) for n in ("wload", "prod", "taken", "ready"))
        if ctxT is not None:
            wc = st.sb("wc", [P, len(w_ctx), E])
            bb = st.sb("bb", [P, E])
            cs = st.sb("cs", [P, 2, GW])
            cload = [st.sem(f"cload{k}") for k in range(2)]
        if gather is not None:
            table, indices, rows = gather
            idx = st.sb("idx", list(indices.shape), I32)
            iload, gathered = st.sem("iload"), st.sem("gathered")
        n_loads = 16 * (1 + (len(w_ctx) + 1 if ctxT is not None else 0))
        with nc.Block() as block:
            if gather is not None:
                @block.gpsimd
                def _(gp):
                    with nc.allow_non_contiguous_dma("4096 indices"):
                        gp.dma_start(idx[:], indices).then_inc(iload, 16)
                    gp.wait_ge(iload, 16)
                    for n in range(indices.shape[1]):
                        gp.indirect_dma_start(out=rows[:, n, :], out_offset=None, in_=table,
                                              in_offset=bass.IndirectOffsetOnAxis(ap=idx[:, n:n + 1], axis=0)
                                              ).then_inc(gathered, 16)
                    gp.wait_ge(gathered, 16 * indices.shape[1])

            if w is not None:
                @block.sync
                def _(sp):
                    sp.dma_start(ws[:], w).then_inc(wload, 16)
                    if ctxT is not None:
                        for n, part in enumerate(w_ctx):
                            sp.dma_start(wc[:, n, :], part).then_inc(wload, 16)
                        sp.dma_start(bb[:], bias.partition_broadcast(P)).then_inc(wload, 16)

                        def body(g, s, j):
                            sp.wait_ge(prod, free_at(g))
                            sp.dma_start(cs[:, s, :], ctxT[:, ds(g * GW, GW)]).then_inc(cload[s], 16)
                        two_slots(sp, NG, body)

            @block.vector
            def _(dve):
                if ctxT is not None:
                    dve.wait_ge(wload, n_loads)
                    dve.tensor_tensor(wc[:, 0, :], wc[:, 0, :], wc[:, 1, :], ALU.add).then_inc(ready, 1)
                if w is not None:
                    dve.sem_inc(taken, 2)

                def normalise(g, s, j):
                    dve.wait_ge(turned, free_at(g))
                    for k in range(4):
                        i = g * 4 + k
                        norm = dve.tensor_scalar(xh[:, s, k, :], tile_of(R.X, i), R.mean[:, ds(i, 1)],
                                                 R.rstd[:, ds(i, 1)], ALU.subtract, ALU.mult)
                    norm.then_inc(normed, 1)

                def take(g, s, j):
                    dve.wait_ge(prod, done_at(g))
                    dst = logits[:, ds(g * 4 * E, 4 * E)]
                    if ctxT is None:
                        m = dve.tensor_copy(dst, psL[s][:, 0:4 * E])
                    else:
                        m = dve.tensor_tensor(dst.rearrange("p (k e) -> p k e", k=4),
                                              psL[s][:, 0:4 * E].rearrange("p (k e) -> p k e", k=4),
                                              bcast_mid(bb[:], 4), ALU.add)
                    m.then_inc(taken, 1)
                pipelined(dve, NG, ((4, take), (0, normalise)) if w is not None else ((0, normalise),))

            @block.tensor
            def _(pe):
                pe.sem_inc(turned, 2)
                if w is not None:
                    pe.sem_inc(prod, 2)
                    pe.wait_ge(wload, n_loads)
                if ctxT is not None:
                    pe.wait_ge(ready, 1)

                def turn(g, s, j):
                    pe.wait_ge(moved, free_at(g))
                    pe.wait_ge(normed, g + 1)
                    for k in range(4):
                        t = pe.transpose(ps[s][:, k * P:(k + 1) * P], xh[:, s, k, :], R.ident[:])
                    t.then_inc(turned, 1)

                def score(g, s, j):
                    pe.wait_ge(moved, done_at(g))
                    pe.wait_ge(taken, free_at(g))
                    if ctxT is not None:
                        pe.wait_ge(cload[s], j * 16 + 16)
                    for k in range(4):
                        o, cols = psL[s][:, k * E:k * E + E], slice(k * P, k * P + P)
                        m = pe.matmul(o, xs[:, s, cols], ws[:], start=True, stop=(ctxT is None))
                        if ctxT is not None:
                            m = pe.matmul(o, cs[:, s, cols], wc[:, 0, :], start=False, stop=True)
                    m.then_inc(prod, 1)
                pipelined(pe, NG, ((3, score), (1, turn)) if w is not None else ((1, turn),))

            @block.scalar
            def _(act):
                act.sem_inc(moved, 2)

                def move(g, s, j):
                    act.wait_ge(turned, done_at(g))
                    if w is not None:
                        act.wait_ge(prod, free_at(g))
                        act.activation(xs[:, s, :], ps[s][:], ACT.Copy)
                    act.activation(R.XT[:, ds(g * GW, GW)], ps[s][:], ACT.Copy).then_inc(moved, 1)
                pipelined(act, NG, ((2, move),))


def stage_gates(nc, R, A):
    with Stage(nc, "gates") as st:
        ig, fg = st.sb("ig", [P, NT * H0]), st.sb("fg", [P, NT * H0])
        t0, t1 = st.sb("t0", [P, NT * H0]), st.sb("t1", [P, NT * H0])
        pc = st.ps("pc", [P, 512])
        split, absd, exped, logged, logf, cum = (
            st.sem(n) for n in ("split", "absd", "exped", "logged", "logf", "cum"))
        with nc.Block() as block:
            @block.tensor
            def _(pe):
                pe.wait_ge(logf, 1)
                pe.matmul(pc[:], R.tri_incl[:], t0[:], start=True, stop=True).then_inc(cum, 1)

            @block.scalar
            def _(act):
                act.wait_ge(absd, 1)
                act.activation(t1[:], t0[:], ACT.Exp, scale=-1.0).then_inc(exped, 1)
                act.wait_ge(exped, 1)
                act.activation(t1[:], t1[:], ACT.Ln, bias=1.0).then_inc(logged, 1)

            @block.vector
            def _(dve):
                v = lambda t: t[:].rearrange("p (i h) -> p i h", i=NT)
                G = R.G[:].rearrange("p (i n) -> p i n", i=NT)
                dve.tensor_copy(v(ig), G[:, :, 0:H0]).then_inc(split, 1)
                dve.tensor_copy(v(fg), G[:, :, H0:]).then_inc(split, 1)
                dve.wait_ge(split, 2)
                dve.scalar_tensor_tensor(out=t0[:], in0=fg[:], scalar=-1.0, in1=fg[:], op0=ALU.mult,
                                         op1=ALU.max).then_inc(absd, 1)
                dve.wait_ge(logged, 1)
                dve.scalar_tensor_tensor(out=t0[:], in0=fg[:], scalar=0.0, in1=t1[:], op0=ALU.min,
                                         op1=ALU.subtract).then_inc(logf, 1)
                dve.wait_ge(cum, 1)
                dve.tensor_copy(R.cs[:], pc[:])
                dve.tensor_tensor(R.g[:].rearrange("p i h -> p (i h)"), ig[:], pc[:], ALU.subtract)


def stage_hop(nc, R, rows):
    RO = S // 4
    with Stage(nc, "hop") as st:
        rows_s = st.sb("rows_s", [P, 2, 2, P])
        rT = [st.ps(f"rT{k}", [P, 512]) for k in range(2)]
        out = [st.ps(f"out{k}", [P, 512]) for k in range(4)]
        bd = st.sb("bd", [P, 2, 4, H0, S])
        qv = st.sb("qv", [P, 2, 4, P])
        kh = st.sb("kh", [P, 2, 4, 512])
        rows_in, turned, spread, prod, moved = (st.sem(n) for n in ("rows_in", "turned", "spread", "prod", "moved"))
        stored = [st.sem(f"stored{k}") for k in range(2)]
        with nc.Block() as block:
            @block.sync
            def _(sp):
                for k in range(2):
                    sp.sem_inc(stored[k], 16)

                def body(r, s, j):
                    sp.wait_ge(moved, r * 4 + 4 + 4)
                    sp.dma_start(R.khop[:, ds(4 * r, 4), :], kh[:, s, :, :]).then_inc(stored[s], 16)
                two_slots(sp, RO, body)
                for k in range(2):
                    sp.wait_ge(stored[k], 16 * (RO // 2) + 16)

            @block.scalar
            def _(act):
                act.sem_inc(moved, 4)

                def front(r, s, j):
                    act.wait_ge(turned, free_at(r))
                    act.activation(rows_s[:, s, :, :], tiles_of(rows, 2 * r, 2), ACT.Copy).then_inc(rows_in, 1)

                def back(r, s, j):
                    act.wait_ge(stored[s], j * 16 + 16)
                    for k in range(4):
                        act.wait_ge(prod, r * 4 + k + 1 + 8)
                        act.activation(kh[:, s, k, :], out[k][:], ACT.Copy).then_inc(moved, 1)
                skewed(act, RO, front, back)

            @block.tensor
            def _(pe):
                pe.sem_inc(turned, 2)
                pe.sem_inc(prod, 8)

                def front(r, s, j):
                    pe.wait_ge(rows_in, r + 1)
                    pe.wait_ge(spread, free_at(r))
                    for k in range(2):
                        t = pe.transpose(rT[s][:, k * P:(k + 1) * P], rows_s[:, s, k, :], R.ident[:])
                    t.then_inc(turned, 1)

                def back(r, s, j):
                    pe.wait_ge(spread, done_at(r))
                    for k in range(4):
                        pe.wait_ge(moved, r * 4 + k + 1)
                        pe.matmul(out[k][:], qv[:, s, k, :], bd[:, s, k, :, :].rearrange("p h m -> p (h m)"),
                                  start=True, stop=True).then_inc(prod, 1)
                skewed(pe, RO, front, back)

            @block.vector
            def _(dve):
                dve.sem_inc(spread, 2)
                q3 = R.XT[:].rearrange("p (b v) -> p v b", v=S)

                def body(r, s, j):
                    dve.wait_ge(prod, r * 4 + 4)
                    dve.tensor_copy(qv[:, s, :, :], q3[:, ds(4 * r, 4), :])
                    dve.wait_ge(turned, done_at(r))
                    for k in range(4):
                        sp = dve.tensor_tensor(bd[:, s, k, :, :], bcast_mid(rT[s][:, k * S:k * S + S], H0),
                                               bcast_in(R.bd16[:], S), ALU.mult)
                    sp.then_inc(spread, 1)
                two_slots(dve, RO, body)


def stage_mlstm(nc, R, A):
    with Stage(nc, "mlstm") as st:
        qT = st.sb("qT", [P, 2, P])
        kT = st.sb("kT", [P, 2, P])
        vv = st.sb("vv", [P, 2, 2, D])
        kh = st.sb("kh", [P, 2, 512])
        kbd = st.sb("kbd", [P, 2, 2, H0, S])
        vbd = st.sb("vbd", [P, 2, 2, D])
        dg = st.sb("dg", [P, 2, 512])
        arg = st.sb("arg", [P, 2, 512])
        dec = st.sb("dec", [P, 2, 512])
        cc = st.sb("cc", [P, 2, 512])
        cT = st.sb("cT", [P, 2, 512])
        psA = [st.ps(f"psA{k}", [P, 512]) for k in range(2)]
        psQ = [st.ps(f"psQ{k}", [P, 512]) for k in range(2)]
        psT = [st.ps(f"psT{k}", [P, 512]) for k in range(2)]
        psH = [st.ps(f"psH{k}", [P, 512]) for k in range(2)]
        qk_load, v_load, kh_load = ([st.sem(f"{n}{k}") for k in range(2)] for n in ("qk_load", "v_load", "kh_load"))
        diag, bias_sum, scores, kspread, vspread, argd, decd, ccd, ct, ctm, hd, hm, maxd, qk_sum, sumd = (
            st.sem(n) for n in ("diag", "bias_sum", "scores", "kspread", "vspread", "argd", "decd", "ccd",
                                "ct", "ctm", "hd", "hm", "maxd", "qk_sum", "sumd"))
        heads = lambda ap: ap.rearrange("p (h t) -> p h t", h=H0)
        with nc.Block() as block:
            @block.sync
            def _(sp):
                def load_qk(i, s, j):
                    sp.wait_ge(scores, free_at(i))
                    sp.dma_start(qT[:, s, :], R.XT[:, ds(i * P, P)]).then_inc(qk_load[s], 16)
                    sp.dma_start(kT[:, s, :], A["ctxT"][:, ds(i * P, P)]).then_inc(qk_load[s], 16)

                def load_hop(i, s, j):
                    sp.wait_ge(ccd, free_at(i))
                    sp.dma_start(kh[:, s, :], R.khop[ds(2 * i, 2), :, :].rearrange("b v n -> (b v) n")
                                 ).then_inc(kh_load[s], 16)

                def load_v(i, s, j):
                    sp.wait_ge(vspread, free_at(i))
                    c = A["ctx"][ds(i * P, P), :].rearrange("(b t) d -> t b d", b=2)
                    for h in range(2):
                        sp.dma_start(vv[64 * h:64 * h + 64, s, :, :], c).then_inc(v_load[s], 16)
                pipelined(sp, NT, ((2, load_hop), (4, load_v), (0, load_qk)))

            @block.gpsimd
            def _(gp):
                gp.sem_inc(vspread, 2)

                def spread_k(i, s, j):
                    gp.wait_ge(qk_load[s], j * 32 + 32)
                    gp.wait_ge(scores, free_at(i))
                    for b in range(2):
                        m = gp.tensor_tensor(kbd[:, s, b, :, :], bcast_mid(kT[:, s, b * S:b * S + S], H0),
                                             bcast_in(R.bd16q[:], S), ALU.mult)
                    m.then_inc(kspread, 1)

                def spread_v(i, s, j):
                    gp.wait_ge(v_load[s], j * 32 + 32)
                    gp.wait_ge(hd, free_at(i))
                    gp.tensor_tensor(vbd[:, s, :, :], vv[:, s, :, :], bcast_mid(R.vmask128, 2),
                                     ALU.mult).then_inc(vspread, 1)
                pipelined(gp, NT, ((6, spread_v), (1, spread_k)))

            @block.tensor
            def _(pe):
                for q in (bias_sum, scores, ct, hd):
                    pe.sem_inc(q, 2)

                def gate_sum(i, s, j):
                    pe.wait_ge(diag, i + 1)
                    pe.wait_ge(argd, free_at(i))
                    pe.matmul(psA[s][:], R.same2[:], dg[:, s, :], start=True, stop=False)
                    pe.matmul(psA[s][:], R.ident_bf[:], R.causal[:], start=False, stop=True).then_inc(bias_sum, 1)

                def q_k(i, s, j):
                    pe.wait_ge(kspread, i + 1)
                    pe.wait_ge(qk_load[s], j * 32 + 32)
                    pe.wait_ge(ccd, free_at(i))
                    for b in range(2):
                        q = pe.matmul(psQ[s][64 * b:64 * b + 64, :], qT[:, s, b * S:b * S + S],
                                      kbd[:, s, b, :, :].rearrange("p h t -> p (h t)"), start=True, stop=True)
                    q.then_inc(scores, 1)

                def turn_c(i, s, j):
                    pe.wait_ge(ccd, done_at(i))
                    pe.wait_ge(ctm, free_at(i))
                    for k in range(4):
                        t = pe.transpose(psT[s][:, k * P:k * P + P], cc[:, s, k * P:k * P + P], R.ident[:])
                    t.then_inc(ct, 1)

                def c_v(i, s, j):
                    pe.wait_ge(ctm, done_at(i))
                    pe.wait_ge(vspread, done_at(i))
                    pe.wait_ge(hm, free_at(i))
                    for b in range(2):
                        for k in range(4):
                            h = pe.matmul(psH[s][64 * b:64 * b + 64, 32 * k:32 * k + 32],
                                          cT[:, s, k * P + 64 * b:k * P + 64 * b + 64],
                                          vbd[:, s, b, 32 * k:32 * k + 32], start=True, stop=True)
                    h.then_inc(hd, 1)
                pipelined(pe, NT, ((5, turn_c), (7, c_v), (2, q_k), (1, gate_sum)))

            @block.vector
            def _(dve):
                for q in (argd, ccd, sumd):
                    dve.sem_inc(q, 2)

                def diagonal(i, s, j):
                    dve.wait_ge(bias_sum, free_at(i))
                    dve.tensor_tensor(heads(dg[:, s, :]), bcast_in(tile_of(R.g, i), S), bcast_mid(R.delta[:], H0),
                                      ALU.mult).then_inc(diag, 1)

                def row_max(i, s, j):
                    dve.wait_ge(bias_sum, done_at(i))
                    dve.tensor_reduce(tile_of(R.rowmax, i), heads(psA[s][:]), AX_X, ALU.max).then_inc(maxd, 1)

                def exponent(i, s, j):
                    dve.wait_ge(maxd, i + 1)
                    dve.wait_ge(decd, free_at(i))
                    dve.tensor_tensor(heads(arg[:, s, :]), heads(psA[s][:]), bcast_in(tile_of(R.rowmax, i), S),
                                      ALU.subtract).then_inc(argd, 1)

                def add_hop(i, s, j):
                    dve.wait_ge(scores, done_at(i))
                    dve.wait_ge(kh_load[s], j * 16 + 16)
                    dve.tensor_tensor(kh[:, s, :], psQ[s][:], kh[:, s, :], ALU.add).then_inc(qk_sum, 1)

                def weigh(i, s, j):
                    dve.wait_ge(qk_sum, i + 1)
                    dve.wait_ge(decd, done_at(i))
                    dve.wait_ge(ct, free_at(i))
                    dve.wait_ge(sumd, free_at(i))
                    dve.tensor_tensor(cc[:, s, :], kh[:, s, :], dec[:, s, :], ALU.mult).then_inc(ccd, 1)

                def row_sum(i, s, j):
                    dve.wait_ge(ccd, done_at(i))
                    dve.tensor_reduce(tile_of(R.rowsum, i), heads(cc[:, s, :]), AX_X, ALU.add).then_inc(sumd, 1)
                pipelined(dve, NT, ((4, add_hop), (0, diagonal), (4, weigh), (2, row_max), (4, row_sum), (2, exponent)))

            @block.scalar
            def _(act):
                for q in (decd, ctm, hm):
                    act.sem_inc(q, 2)

                def decay(i, s, j):
                    act.wait_ge(argd, done_at(i))
                    act.wait_ge(ccd, free_at(i))
                    act.activation(dec[:, s, :], arg[:, s, :], ACT.Exp).then_inc(decd, 1)

                def move_c(i, s, j):
                    act.wait_ge(ct, done_at(i))
                    act.wait_ge(hd, free_at(i))
                    act.activation(cT[:, s, :], psT[s][:], ACT.Copy).then_inc(ctm, 1)

                def move_h(i, s, j):
                    act.wait_ge(hd, done_at(i))
                    act.activation(tile_of(R.Y, i), psH[s][:, 0:D], ACT.Copy).then_inc(hm, 1)
                pipelined(act, NT, ((6, move_c), (3, decay), (8, move_h)))


def stage_headnorm(nc, R, A):
    N = NT * H0
    with Stage(nc, "headnorm") as st:
        en, nrm, rn, mu, var, t0 = (st.sb(n, [P, N]) for n in ("en", "nrm", "rn", "mu", "var", "t0"))
        w, b = st.sb("w", [P, D]), st.sb("b", [P, D])
        sq = st.sb("sq", [P, N * C0])
        loaded, chain, ex, ready, rooted, squared, cent, shifted = (
            st.sem(n) for n in ("loaded", "chain", "ex", "ready", "rooted", "squared", "cent", "shifted"))
        y = R.Y[:].rearrange("p i (h c) -> p (i h) c", c=C0)
        with nc.Block() as block:
            @block.sync
            def _(sp):
                sp.dma_start(w[:], A["ln_w"].partition_broadcast(P)).then_inc(loaded, 16)
                sp.dma_start(b[:], A["ln_b"].partition_broadcast(P)).then_inc(loaded, 16)

            @block.gpsimd
            def _(gp):
                gp.wait_ge(loaded, 32)
                with gp.Fori(0, NG) as g:
                    x = tiles_of(R.X, g * 4, 4)
                    gp.tensor_tensor(x, x, bcast_mid(b[:], 4), ALU.add).then_inc(shifted, 1)

            @block.vector
            def _(dve):
                link = Chain(dve, chain)
                rs, rm = (t[:].rearrange("p i h -> p (i h)") for t in (R.rowsum, R.rowmax))
                dve.tensor_tensor(t0[:], R.cs[:], rm, ALU.add).then_inc(ready, 1)
                link(dve.tensor_reduce(mu[:], y, AX_X, ALU.add))
                link(dve.tensor_scalar(mu[:], mu[:], 1.0 / C0, None, ALU.mult))
                dve.tensor_tensor(y, y, bcast_in(mu[:], C0), ALU.subtract).then_inc(cent, 1)
                link(dve.scalar_tensor_tensor(out=nrm[:], in0=rs, scalar=-1.0, in1=rs, op0=ALU.mult, op1=ALU.max))
                dve.wait_ge(ex, 1)
                link(dve.tensor_tensor(nrm[:], nrm[:], en[:], ALU.max))
                link(dve.tensor_scalar(nrm[:], nrm[:], 1e-6, None, ALU.add))
                link(dve.reciprocal(rn[:], nrm[:]))
                link(dve.tensor_tensor(nrm[:], rn[:], rn[:], ALU.mult))
                dve.wait_ge(loaded, 32)
                link(dve.tensor_scalar(w[:], w[:], 1.0, None, ALU.add))
                dve.wait_ge(squared, 1)
                link(dve.tensor_reduce(var[:], sq[:].rearrange("p (n c) -> p n c", c=C0), AX_X, ALU.add))
                link(dve.scalar_tensor_tensor(out=var[:], in0=var[:], scalar=1.0 / C0, in1=nrm[:], op0=ALU.mult,
                                              op1=ALU.mult))
                link(dve.tensor_scalar(var[:], var[:], LN_EPS, None, ALU.add))
                dve.sem_inc(ready, 1)
                link(dve.tensor_tensor(R.Y[:], R.Y[:], bcast_mid(w[:], NT), ALU.mult))
                dve.wait_ge(rooted, 1)
                link(dve.reciprocal(var[:], t0[:]))
                link(dve.tensor_tensor(var[:], var[:], rn[:], ALU.mult))
                link(dve.tensor_tensor(y, y, bcast_in(var[:], C0), ALU.mult))
                dve.wait_ge(shifted, NG)
                link(dve.tensor_tensor(R.X[:], R.X[:], R.Y[:], ALU.add))

            @block.scalar
            def _(act):
                act.wait_ge(ready, 1)
                act.activation(en[:], t0[:], ACT.Exp, scale=-1.0).then_inc(ex, 1)
                act.wait_ge(cent, 1)
                act.activation(sq[:], R.Y[:].rearrange("p i d -> p (i d)"), ACT.Square).then_inc(squared, 1)
                act.wait_ge(ready, 2)
                act.activation(t0[:], var[:], ACT.Sqrt).then_inc(rooted, 1)


def stage_scan(nc, R, A):
    DONE = 3
    NB = B // 8
    with Stage(nc, "scan") as st:
        wx = st.sb("wx", [P, 3, P])
        uc = st.sb("uc", [P, 3, P])
        bias = st.sb("bias", [P, 4])
        cin = st.sb("cin", [P, 1])
        c = st.sb("c", [P, 2, S])
        gates = st.sb("gates", [P, 2, 3, S])
        fc, ig = st.sb("fc", [P, S]), st.sb("ig", [P, S])
        wkv, wo3, heads = st.sb("wkv", [P, 2 * D]), st.sb("wo3", [P, D]), st.sb("heads", [P, D])
        cT = st.sb("cT", [P, 2, P])
        kv = st.sb("kv", [S, 2, 2 * D])
        mT = st.sb("mT", [P, 2, D])
        gb = st.sb("gb", [P, 2, 8, D])
        psKG, psM = st.ps("psKG", [P, 512]), st.ps("psM", [P, 512])
        cload, g_stored = ([st.sem(f"{n}{k}") for k in range(2)] for n in ("cload", "g_stored"))
        kg_done, kg_free, m_prod, m_done, g_free = (
            st.sem(n) for n in ("kg_done", "kg_free", "m_prod", "m_done", "g_free"))
        ps = [[st.ps(f"ps{k}_{q}", [P, 512]) for q in range(3)] for k in range(2)]
        loaded, start, cstep, gact, part, xpart, hstep, freed, zero = (
            st.sem(n) for n in ("loaded", "start", "cstep", "gact", "part", "xpart", "hstep", "freed", "zero"))
        with nc.Block() as block:
            @block.sync
            def _(sp):
                sp.dma_start(wx[:], A["lstm_wT"].rearrange("n i m -> i n m")[:, 0:3, :]).then_inc(loaded, 16)
                sp.dma_start(uc[:], A["lstm_uT"].rearrange("n i m -> i n m")[:, 0:3, :]).then_inc(loaded, 16)
                with nc.allow_non_contiguous_dma("bias columns"):
                    sp.dma_start(bias[:], A["lstm_bT"]).then_inc(loaded, 16)
                    sp.dma_start(cin[:], A["in_c"].rearrange("(p a) -> p a", a=1)).then_inc(loaded, 16)
                sp.dma_start(wkv[:, 0:D], A["l3_wkT"]).then_inc(loaded, 16)
                sp.dma_start(wkv[:, D:], A["l3_wvT"]).then_inc(loaded, 16)
                sp.dma_start(wo3[:], A["l3_woT"]).then_inc(loaded, 16)

                def load_c(i, s, j):
                    sp.wait_ge(kg_done, i * 2 - 2 + DONE)
                    sp.dma_start(cT[:, s, :], A["ctxT"][:, ds(i * P, P)]).then_inc(cload[s], 16)
                two_slots(sp, NT, load_c)

            @block.gpsimd
            def _(gp):
                gp.sem_inc(g_free, 2)

                def store(n, s, j):
                    gp.wait_ge(kg_free, n * 8 + 8 + 1)
                    gp.dma_start(R.G3[ds(n * 8, 8), :, :].rearrange("t p d -> p t d"), gb[:, s, :, :]
                                 ).then_inc(g_stored[s], 16)
                    gp.wait_ge(g_stored[s], j * 16 + 16)
                    gp.sem_inc(g_free, 1)
                two_slots(gp, NB, store)
                gp.wait_ge(kg_free, B + 2 + 1)
                gp.dma_start(R.G3[B:B + 2, :, :].rearrange("t p d -> p t d"), gb[:, 0, 0:2, :]
                             ).then_inc(g_stored[0], 16)
                gp.wait_ge(g_stored[0], 16 * (NB // 2 + 1))

            @block.vector
            def _(dve):
                for b in (c, kv, mT):
                    dve.memset(b[:], 0.0).then_inc(zero, 1)
                dve.tensor_scalar(heads[:], R.bd8[:].rearrange("p a b -> p (a b)"), C2 ** -0.5, None,
                                  ALU.mult).then_inc(zero, 1)
                dve.sem_inc(m_done, 1)
                dve.wait_ge(loaded, 112)
                dve.wait_ge(zero, 4)
                dve.tensor_scalar(c[:, 0, :], c[:, 0, :], cin[:, 0:1], None, ALU.add).then_inc(cstep, 1)

                def body(t, s, j):
                    dve.wait_ge(gact, t * 3 + 1 + 48)
                    dve.wait_ge(cstep, t + 1)
                    dve.tensor_tensor(fc[:], gates[:, s, 0, :], c[:, s, :], ALU.mult).then_inc(part, 1)
                    dve.wait_ge(gact, t * 3 + 3 + 48)
                    dve.tensor_tensor(ig[:], gates[:, s, 1, :], gates[:, s, 2, :], ALU.mult).then_inc(part, 1)
                    dve.wait_ge(part, t * 2 + 2)
                    dve.tensor_tensor(c[:, 1 - s, :], fc[:], ig[:], ALU.add).then_inc(cstep, 1)
                    mask(t, 1 - s)

                def mask(t, s):
                    dve.wait_ge(m_prod, t + 2)
                    dve.wait_ge(kg_done, t + DONE)
                    dve.tensor_tensor(mT[:, s, :], psM[:, 0:D], heads[:], ALU.mult).then_inc(m_done, 1)
                two_slots(dve, B, body)
                mask(B, 1)

            @block.tensor
            def _(pe):
                pe.wait_ge(loaded, 112)
                pe.wait_ge(zero, 4)
                pe.sem_inc(kg_done, DONE)
                pe.sem_inc(m_prod, 1)

                def context_part(t, k, keys=True, matrix=True):
                    pe.wait_ge(kg_free, t + 1)
                    pe.wait_ge(m_done, t + 1)
                    if keys:
                        pe.matmul(psKG[0:S, 0:2 * D], cT[:, k // 2 % 2, k % 2 * S:k % 2 * S + S], wkv[:],
                                  start=True, stop=True)
                    pe.matmul(psKG[:, 2 * D:3 * D], mT[:, k % 2, :], wo3[:], start=True, stop=True).then_inc(kg_done, 1)
                    if matrix:
                        last = kv[:, (k + 1) % 2, :]
                        pe.matmul(psM[:, 0:D], last[:, D:], last[:, 0:D], start=True, stop=True).then_inc(m_prod, 1)

                def xparts(n, s, j):
                    pe.wait_ge(gact, n * 24 + 24)
                    for q in range(3):
                        x = pe.matmul(ps[s][q][:], wx[:, q, :], R.XT[:, ds(n * 512, 512)],
                                      start=True, stop=False, skip_group_check=True)

                def steps(n, s, j):
                    for k in range(8):
                        t = n * 8 + k
                        pe.wait_ge(cstep, t + 1)
                        for q in range(3):
                            pe.matmul(ps[s][q][:, k * S:k * S + S], uc[:, q, :], c[:, k % 2, :], start=False,
                                      stop=True, skip_group_check=True).then_inc(hstep, 1)
                        if k % 2 == 0:
                            pe.wait_ge(cload[k // 2 % 2], (n * 2 + k // 4) * 16 + 16)
                        context_part(t, k)

                skewed(pe, NB, xparts, steps)
                context_part(B, 0, keys=False)
                context_part(B + 1, 1, keys=False, matrix=False)

            @block.scalar
            def _(act):
                act.sem_inc(gact, 48)
                act.sem_inc(kg_free, 1)
                act.wait_ge(zero, 4)

                def steps(n, s, j):
                    for k in range(8):
                        t = n * 8 + k
                        for q, f in enumerate((ACT.Sigmoid, ACT.Sigmoid, ACT.Tanh)):
                            act.wait_ge(hstep, t * 3 + q + 1)
                            act.activation(gates[:, k % 2, q, :], ps[s][q][:, k * S:k * S + S], f,
                                           bias=bias[:, q:q + 1]).then_inc(gact, 1)
                        if k == 0:
                            act.wait_ge(g_free, free_at(n))
                        act.wait_ge(kg_done, t + 1 + DONE)
                        act.wait_ge(m_prod, t + 1)
                        act.activation(kv[:, k % 2, :], psKG[0:S, 0:2 * D], ACT.Copy)
                        act.activation(gb[:, s, k, :], psKG[:, 2 * D:3 * D], ACT.Copy).then_inc(kg_free, 1)
                two_slots(act, NB, steps)
                act.wait_ge(g_free, free_at(NB))
                for k in range(2):
                    act.wait_ge(kg_done, B + k + 1 + DONE)
                    act.activation(gb[:, 0, k, :], psKG[:, 2 * D:3 * D], ACT.Copy).then_inc(kg_free, 1)
        wo, uo = st.sb("wo", [P, P]), st.sb("uo", [P, P])
        hT = st.sb("hT", [P, 2, GW])
        cb = st.sb("cb", [P, S])
        ws = st.sem("ws")
        prod, tanhd, turned, added = (st.sem(n) for n in ("prod", "tanhd", "turned", "added"))
        with nc.Block() as block:
            @block.sync
            def _(sp):
                sp.dma_start(wo[:], A["lstm_wT"][3]).then_inc(ws, 16)
                sp.dma_start(uo[:], A["lstm_uT"][3]).then_inc(ws, 16)

            @block.tensor
            def _(pe):
                pe.sem_inc(prod, 2)
                pe.sem_inc(turned, 2)
                pe.wait_ge(ws, 32)

                def front(g, s, j):
                    pe.wait_ge(tanhd, free_at(g))
                    pe.matmul(ps[s][0][:], wo[:], R.XT[:, ds(g * GW, GW)], start=True, stop=False)
                    pe.matmul(ps[s][0][:].rearrange("p (b t) -> p b t", b=8), uo[:], bcast_mid(c[:, 0, :], 8),
                              start=False, stop=True).then_inc(prod, 1)

                def back(g, s, j):
                    pe.wait_ge(tanhd, done_at(g))
                    pe.wait_ge(added, free_at(g))
                    for k in range(4):
                        t = pe.transpose(ps[s][1][:, k * P:k * P + P], hT[:, s, k * P:k * P + P], R.ident[:])
                    t.then_inc(turned, 1)
                skewed(pe, NG, front, back)

            @block.scalar
            def _(act):
                act.sem_inc(tanhd, 2)

                def body(g, s, j):
                    act.wait_ge(prod, done_at(g))
                    act.wait_ge(turned, free_at(g))
                    act.activation(hT[:, s, :], ps[s][0][:], ACT.Tanh, bias=bias[:, 3:4]).then_inc(tanhd, 1)
                two_slots(act, NG, body)

            @block.vector
            def _(dve):
                dve.sem_inc(added, 2)

                def body(g, s, j):
                    dve.wait_ge(turned, done_at(g))
                    x = tiles_of(R.X, g * 4, 4)
                    dve.tensor_tensor(x, ps[s][1][:].rearrange("p (k d) -> p k d", k=4), x,
                                      ALU.add).then_inc(added, 1)
                    dve.wait_ge(added, done_at(g))
                    for k in range(4):
                        dve.bn_stats(tile_of(R.stats, g * 4 + k), tile_of(R.X, g * 4 + k))
                two_slots(dve, NG, body)



def stage_attend(nc, R, A):
    NU, UW = NT // 2, 2 * P
    NKQ = 9
    AHEAD, KQ_AHEAD, V_AHEAD = 6, 15, 5
    with Stage(nc, "attend") as st:
        wq, wk, wv = (st.sb(n, [P, H1 * C1]) for n in ("wq", "wk", "wv"))
        wo = st.sb("wo", [P, HP1, D])
        bq, bk, bv = (st.sb(n, [P, HP1]) for n in ("bq", "bk", "bv"))
        bo, row = st.sb("bo", [1, D]), st.sb("row", [1, D])
        xh, xT = st.sb("xh", [P, 2, P]), st.sb("xT", [P, UW])
        cT = st.sb("cT", [P, 2, UW])
        cV, cV_high, cV_low = (st.sb(n, [P, 2, UW]) for n in ("cV", "cV_high", "cV_low"))
        wv_high, wv_low = st.sb("wv_high", [P, H1 * C1]), st.sb("wv_low", [P, H1 * C1])
        qT = st.sb("qT", [P, 2, HP1, UW])
        kbd = st.sb("kbd", [P, 2, HP1, 4, 2, S])
        vs = st.sb("vs", [P, 2, 4, C1])
        vbd = st.sb("vbd", [P, 2, 4, HP1, 2, C1])
        top, tot, rs = st.sb("top", [P, 2, 8]), st.sb("tot", [P, 4, 8]), st.sb("rs", [P, 4, 8])
        arg, pr, pT, o, oT = (st.sb(n, [P, 2, 512]) for n in ("arg", "pr", "pT", "o", "oT"))
        psS = [st.ps(f"psS{k}", [P, 512]) for k in range(2)]
        psK, psB, psP, psO, psV, psY = (st.ps(n, [P, 512]) for n in ("psK", "psB", "psP", "psO", "psV", "psY"))
        wload = st.sem("wload")
        cload, cVload, shifted = ([st.sem(f"{n}{k}") for k in range(2)] for n in ("cload", "cVload", "shifted"))
        (wv_split, high, cV_split, normed, kq_full, kq_free, v_full, v_free, zero, rowd, rowm, biasd) = (
            st.sem(n) for n in ("wv_split", "high", "cV_split", "normed", "kq_full", "kq_free", "v_full", "v_free", "zero", "rowd", "rowm", "biasd"))
        (s_done, topd, argd, expd, totd, sumd, ptd, ptm, pvd, od, otd, otm, yd, added) = (
            st.sem(n) for n in ("s_done", "topd", "argd", "expd", "totd", "sumd", "ptd", "ptm", "pvd", "od", "otd",
                                "otm", "yd", "added"))
        heads = lambda ap: ap.rearrange("p (h t) -> p h t", h=8)
        lo, hi = slice(0, 64), slice(64, P)
        unit = lambda c, j: 2 * j + c // 4
        slot = lambda c: c // 4 % 2
        place = lambda c: (slot(c), c % 4 // 2, c % 2)
        before = lambda i: i + 2
        kq_taken = lambda u, n: u * NKQ + n + 1 + KQ_AHEAD
        v_taken = lambda i: i + 1 + V_AHEAD
        with nc.Block() as block:
            @block.sync
            def _(sp):
                for w, a in ((wq, A["a1_wq"]), (wk, A["a1_wk"]), (wv, A["a1_wv"]), (wo, A["a1_wo"]), (bq, A["a1_bqT"]),
                             (bk, A["a1_bkT"]), (bv, A["a1_bvT"]), (bo, A["a1_bo"])):
                    sp.dma_start(w[:], a).then_inc(wload, 16)

                for k in range(2):
                    sp.sem_inc(shifted[k], 32)

                def load_c(i, c, j):
                    if c % 4 == 0:
                        u = unit(c, j)
                        sp.wait_ge(kq_free, kq_taken(u - 2, 3))
                        sp.dma_start(cT[:, slot(c), :], A["ctxT"][:, ds(u * UW, UW)]).then_inc(cload[slot(c)], 16)

                def load_cV(i, c, j):
                    if c % 4 == 0:
                        u = unit(c, j)
                        sp.wait_ge(v_free, v_taken(i - 5))
                        sp.dma_start(cV[:, slot(c), :], A["ctxT"][:, ds(u * UW, UW)]).then_inc(cVload[slot(c)], 16)

                def shift(i, c, j):
                    s, t, half = place(c)
                    hs = slice(4 * half, 4 * half + 4)
                    sp.wait_ge(v_free, v_taken(i))
                    sp.dma_start(vbd[hi, s, 2 * t, hs, 1, :], vs[lo, c % 2, :, :]).then_inc(shifted[c % 2], 16)
                    sp.dma_start(vbd[lo, s, 2 * t + 1, hs, 0, :], vs[hi, c % 2, :, :]).then_inc(shifted[c % 2], 16)
                octets(sp, 2 * NT, ((2, shift), (-2, load_cV), (-6, load_c)))

            @block.gpsimd
            def _(gp):
                gp.memset(kbd[:], 0.0).then_inc(zero, 1)
                gp.memset(vbd[:], 0.0).then_inc(zero, 1)

            @block.tensor
            def _(pe):
                for q in (s_done, pvd):
                    pe.sem_inc(q, AHEAD)
                for q in (ptd, otd, yd):
                    pe.sem_inc(q, 2)
                pe.wait_ge(wload, 128)
                for h in range(HP1):
                    m = pe.matmul(psY[0:1, 0:D], bv[:, h:h + 1], wo[:, h, :], start=(h == 0), stop=(h == HP1 - 1))
                m.then_inc(rowd, 1)
                pe.wait_ge(rowm, 1)
                pe.wait_ge(wv_split, 1)

                def project_kq(part):
                    def step(i, c, j):
                        u, s, m = unit(c, j), slot(c), c % 4
                        n = 2 * (m % 2) + part
                        if part == 2:
                            if m != 1:
                                return
                            pe.wait_ge(normed, u + 1)
                            pe.wait_ge(kq_free, kq_taken(u, 3))
                            for k in range(2):
                                t = pe.transpose(psK[:, k * P:k * P + P], xh[:, k, :], R.ident[:])
                            t.then_inc(kq_full, 1)
                            return
                        w, x = (wk, cT[:, s, :]) if m < 2 else (wq, xT[:])
                        if m == 0 and part == 0:
                            pe.wait_ge(cload[s], (2 * j + c // 4 - s) * 8 + 16)
                        pe.wait_ge(kq_free, kq_taken(u, (n if m < 2 else n + 5) - 1))
                        for a in range(2):
                            h = 2 * n + a
                            p = pe.matmul(psK[:, a * UW:a * UW + UW], w[:, h * P:h * P + P], x, start=True, stop=True)
                        p.then_inc(kq_full, 1)
                    return step

                def project_v(i, c, j):
                    s, t, half = place(c)
                    if c % 4 == 0:
                        pe.wait_ge(cV_split, unit(c, j) + 1)
                    pe.wait_ge(v_free, v_taken(i - 1))
                    matmul_split(pe, psB[:], [x[:, s, t * P:t * P + P] for x in (cV_high, cV_low)],
                                 [w[:, half * 512:half * 512 + 512] for w in (wv_high, wv_low)]).then_inc(v_full, 1)

                def scores(i, c, j):
                    s, t, half = place(c)
                    pe.wait_ge(kq_free, kq_taken(unit(c, j), NKQ - 1))
                    pe.wait_ge(argd, free_at(i))
                    for b in range(2):
                        for k in range(4):
                            h, nb = half * 4 + k, t * 2 + b
                            m = pe.matmul(psS[c % 2][64 * b:64 * b + 64, k * P:k * P + P], qT[:, s, h, nb * S:nb * S + S],
                                          kbd[:, s, h, nb, :, :].rearrange("p a t -> p (a t)"), start=True, stop=True)
                    m.then_inc(s_done, 1)

                def turn_p(i, c, j):
                    pe.wait_ge(expd, done_at(i))
                    pe.wait_ge(ptm, before(i))
                    for k in range(4):
                        t = pe.transpose(psP[:, k * P:k * P + P], pr[:, c % 2, k * P:k * P + P], R.ident[:])
                    t.then_inc(ptd, 1)

                def values(i, c, j):
                    s, t, half = place(c)
                    pe.wait_ge(ptm, done_at(i))
                    pe.wait_ge(od, before(i))
                    pe.wait_ge(v_free, v_taken(i))
                    pe.wait_ge(shifted[c % 2], (4 * j + c // 2) * 32 + 64)
                    for b in range(2):
                        for k in range(4):
                            h, nb = half * 4 + k, t * 2 + b
                            m = pe.matmul(psV[64 * b:64 * b + 64, k * P:k * P + P],
                                          pT[:, c % 2, k * P + 64 * b:k * P + 64 * b + 64],
                                          vbd[:, s, nb, h, :, :].rearrange("p a t -> p (a t)"), start=True, stop=True)
                    m.then_inc(pvd, 1)

                def turn_o(i, c, j):
                    pe.wait_ge(od, done_at(i))
                    pe.wait_ge(otm, before(i))
                    for k in range(4):
                        t = pe.transpose(psO[:, k * P:k * P + P], o[:, c % 2, k * P:k * P + P], R.ident[:])
                    t.then_inc(otd, 1)

                def project(i, c, j):
                    pe.wait_ge(otm, done_at(i))
                    if c % 2 == 0:
                        pe.wait_ge(added, 4 * j + c // 2 + 1)
                        pe.matmul(psY[:, 0:D], R.ones[0:1, 0:P], row[:], start=True, stop=False)
                    for k in range(4):
                        m = pe.matmul(psY[:, 0:D], oT[:, c % 2, k * P:k * P + P], wo[:, (c % 2) * 4 + k, :],
                                      start=False, stop=(c % 2 == 1 and k == 3))
                    m.then_inc(yd, 1)
                octets(pe, 2 * NT, ((5, values), (-4, project_kq(0)), (3, turn_p), (1, project_v), (7, turn_o),
                                    (-4, project_kq(1)), (9, project), (0, scores),
                                    (-4, project_kq(2))))

            @block.scalar
            def _(act):
                for q in (expd, ptm, otm):
                    act.sem_inc(q, 2)
                act.sem_inc(kq_free, KQ_AHEAD)
                act.sem_inc(v_free, V_AHEAD)
                act.wait_ge(rowd, 1)
                act.wait_ge(zero, 2)
                act.wait_ge(biasd, 1)

                def move_kq(part):
                    def step(i, c, j):
                        u, s, m = unit(c, j), slot(c), c % 4
                        n = 2 * (m % 2) + part
                        if part == 2:
                            if m == 1:
                                act.wait_ge(kq_full, u * NKQ + 4 + 1)
                                act.activation(xT[:], psK[:, 0:UW], ACT.Copy).then_inc(kq_free, 1)
                            return
                        act.wait_ge(kq_full, u * NKQ + (n if m < 2 else n + 5) + 1)
                        if n == 0:
                            act.wait_ge(s_done, u * 4 - 5 + 1 + AHEAD)
                        for a in range(2):
                            h, src = 2 * n + a, psK[:, a * UW:a * UW + UW]
                            if m < 2:
                                src = src.rearrange("p (b t) -> p b t", b=4)
                                act.activation(kbd[lo, s, h, :, 0, :], src[lo, :, :], ACT.Identity, bias=bk[lo, h:h + 1])
                                p = act.activation(kbd[hi, s, h, :, 1, :], src[hi, :, :], ACT.Identity,
                                                   bias=bk[hi, h:h + 1])
                            else:
                                p = act.activation(qT[:, s, h, :], src, ACT.Identity, bias=bq[:, h:h + 1],
                                                   scale=C1 ** -0.5)
                        p.then_inc(kq_free, 1)
                    return step

                def move_v(i, c, j):
                    s, t, half = place(c)
                    hs = slice(4 * half, 4 * half + 4)
                    act.wait_ge(v_full, i + 1)
                    act.wait_ge(pvd, unit(c, j) * 4 - 5 + 1 + AHEAD)
                    act.wait_ge(shifted[c % 2], (4 * j + c // 2) * 32 + 32)
                    src = psB[:].rearrange("p (k a d) -> p k a d", k=4, a=2)
                    act.activation(vbd[lo, s, 2 * t, hs, 0, :], src[lo, :, 0, :], ACT.Copy)
                    act.activation(vbd[hi, s, 2 * t + 1, hs, 1, :], src[hi, :, 1, :], ACT.Copy)
                    act.activation(vs[lo, c % 2, :, :], src[lo, :, 1, :], ACT.Copy)
                    act.activation(vs[hi, c % 2, :, :], src[hi, :, 0, :], ACT.Copy).then_inc(v_free, 1)

                def exps(i, c, j):
                    act.wait_ge(argd, done_at(i))
                    act.wait_ge(ptd, free_at(i))
                    act.wait_ge(totd, free_at(i))
                    act.activation(pr[:, c % 2, :], arg[:, c % 2, :], ACT.Exp).then_inc(expd, 1)

                def move_p(i, c, j):
                    act.wait_ge(ptd, done_at(i))
                    act.wait_ge(pvd, i - 2 + 1 + AHEAD)
                    act.activation(pT[:, c % 2, :], psP[:], ACT.Copy).then_inc(ptm, 1)

                def move_o(i, c, j):
                    act.wait_ge(otd, done_at(i))
                    act.wait_ge(yd, free_at(i))
                    act.activation(oT[:, c % 2, :], psO[:], ACT.Copy).then_inc(otm, 1)
                octets(act, 2 * NT, ((4, move_p), (8, move_o), (2, exps), (-4, move_kq(0)), (1, move_v),
                                     (-4, move_kq(1)), (-4, move_kq(2))))

            @block.vector
            def _(dve):
                for q in (argd, totd, od):
                    dve.sem_inc(q, 2)
                dve.sem_inc(sumd, 4)
                dve.sem_inc(added, 1)
                dve.wait_ge(rowd, 1)
                dve.tensor_tensor(row[:], psY[0:1, 0:D], bo[:], ALU.add).then_inc(rowm, 1)
                dve.tensor_scalar(bq[:], bq[:], C1 ** -0.5, None, ALU.mult).then_inc(biasd, 1)

                dve.wait_ge(wload, 128)
                take_high(dve, wv_high[:], wv[:]).then_inc(high, 1)
                dve.wait_ge(high, 1)
                take_low(dve, wv_low[:], wv[:], wv_high[:]).then_inc(wv_split, 1)

                def split_cV(i, c, j):
                    if c % 4 == 0:
                        u, s = unit(c, j), slot(c)
                        dve.wait_ge(cVload[s], (u - s) * 8 + 16)
                        dve.wait_ge(v_free, v_taken(i - 5))
                        take_high(dve, cV_high[:, s, :], cV[:, s, :]).then_inc(high, 1)
                        dve.wait_ge(high, u + 2)
                        take_low(dve, cV_low[:, s, :], cV[:, s, :], cV_high[:, s, :]).then_inc(cV_split, 1)

                def norm(i, c, j):
                    if c % 4:
                        return
                    u = unit(c, j)
                    dve.wait_ge(kq_free, kq_taken(u - 1, 4))
                    for k in range(2):
                        t = u * 2 + k
                        m = dve.tensor_scalar(xh[:, k, :], tile_of(R.X, t), R.mean[:, ds(t, 1)],
                                              R.rstd[:, ds(t, 1)], ALU.subtract, ALU.mult)
                    m.then_inc(normed, 1)

                def soft(i, c, j):
                    dve.wait_ge(s_done, i + 1 + AHEAD)
                    dve.wait_ge(argd, before(i))
                    dve.tensor_reduce(top[:, c % 2, :], heads(psS[c % 2][:]), AX_X, ALU.max).then_inc(topd, 1)
                    dve.wait_ge(topd, i + 1)
                    dve.wait_ge(expd, free_at(i))
                    dve.tensor_tensor(heads(arg[:, c % 2, :]), heads(psS[c % 2][:]),
                                      bcast_in(top[:, c % 2, :], S), ALU.subtract).then_inc(argd, 1)

                def sums(i, c, j):
                    dve.wait_ge(expd, done_at(i))
                    dve.wait_ge(sumd, i + 1)
                    dve.tensor_reduce(tot[:, c % 4, :], heads(pr[:, c % 2, :]), AX_X, ALU.add).then_inc(totd, 1)
                    dve.wait_ge(totd, done_at(i))
                    dve.reciprocal(rs[:, c % 4, :], tot[:, c % 4, :]).then_inc(sumd, 1)

                def scale(i, c, j):
                    dve.wait_ge(pvd, i + 1 + AHEAD)
                    dve.wait_ge(sumd, i + 1 + 4)
                    dve.wait_ge(otd, free_at(i))
                    dve.tensor_tensor(heads(o[:, c % 2, :]), heads(psV[:]), bcast_in(rs[:, c % 4, :], C1),
                                      ALU.mult).then_inc(od, 1)

                def add(i, c, j):
                    if c % 2:
                        t = 4 * j + c // 2
                        dve.wait_ge(yd, done_at(i))
                        dve.tensor_tensor(tile_of(R.X, t), psY[:, 0:D], tile_of(R.X, t), ALU.add).then_inc(added, 1)
                        dve.wait_ge(added, t + 2)
                        dve.bn_stats(tile_of(R.stats, t), tile_of(R.X, t))
                octets(dve, 2 * NT, ((6, scale), (10, add), (3, sums), (1, soft), (-4, norm), (-1, split_cV)))


def stage_route(nc, R, name, E, two, capacity):
    N = NT * E
    with Stage(nc, name) as st:
        rev, eq, hot0, hot1, lg2 = (st.sb(n, [P, w]) for n, w in (
            ("rev", E), ("eq", N), ("hot0", N), ("hot1", N), ("lg2", N)))
        m0, m1, r, ex, w0, w1 = (st.sb(n, [P, NT]) for n in ("m0", "m1", "r", "ex", "w0", "w1"))
        ps = st.ps("ps", [P, 512])
        chain, ready, exd, revd, pos = (st.sem(n) for n in ("chain", "ready", "exd", "revd", "pos"))
        v = lambda t: t.rearrange("p (i e) -> p i e", e=E)
        with nc.Block() as block:
            @block.gpsimd
            def _(gp):
                gp.iota(rev[:].bitcast(I32), pattern=[[-1, E]], base=E, channel_multiplier=0).then_inc(revd, 1)

            @block.vector
            def _(dve):
                link = Chain(dve, chain)
                dve.wait_ge(revd, 1)
                link(dve.tensor_copy(rev[:], rev[:].bitcast(I32)))

                def first_largest(lg, m, hot):
                    link(dve.tensor_reduce(m[:], v(lg), AX_X, ALU.max))
                    link(dve.tensor_tensor(v(eq[:]), v(lg), bcast_in(m[:], E), ALU.is_equal))
                    link(dve.tensor_tensor(v(eq[:]), v(eq[:]), bcast_mid(rev[:], NT), ALU.mult))
                    link(dve.tensor_reduce(r[:], v(eq[:]), AX_X, ALU.max))
                    link(dve.tensor_tensor(v(hot), v(eq[:]), bcast_in(r[:], E), ALU.is_equal))

                first_largest(R.lg[:, 0:N], m0, hot0[:] if two else R.wt[:, 0:N])
                if two:
                    link(dve.scalar_tensor_tensor(out=lg2[:], in0=hot0[:], scalar=-3e38, in1=R.lg[:, 0:N],
                                                  op0=ALU.mult, op1=ALU.add))
                    first_largest(lg2[:], m1, hot1[:])
                    dve.tensor_tensor(m1[:], m1[:], m0[:], ALU.subtract).then_inc(ready, 1)
                    dve.wait_ge(exd, 1)
                    link(dve.tensor_scalar(w0[:], ex[:], 1.0, None, ALU.add))
                    link(dve.reciprocal(w1[:], w0[:]))
                    link(dve.tensor_tensor(w0[:], ex[:], w1[:], ALU.mult))
                    link(dve.tensor_tensor(lg2[:], hot0[:], hot1[:], ALU.add))
                    dve.sem_inc(ready, 1)
                    link(dve.tensor_tensor(v(hot0[:]), v(hot0[:]), bcast_in(w1[:], E), ALU.mult))
                    link(dve.tensor_tensor(v(hot1[:]), v(hot1[:]), bcast_in(w0[:], E), ALU.mult))
                    link(dve.tensor_tensor(R.wt[:, 0:N], hot0[:], hot1[:], ALU.add))
                    if capacity:
                        dve.wait_ge(pos, 1)
                        link(dve.tensor_scalar(eq[:], ps[:], float(capacity), None, ALU.is_lt))
                        link(dve.tensor_tensor(R.wt[:, 0:N], R.wt[:, 0:N], eq[:], ALU.mult))

            if two:
                @block.scalar
                def _(act):
                    act.wait_ge(ready, 1)
                    act.activation(ex[:], m1[:], ACT.Exp).then_inc(exd, 1)

            if capacity:
                @block.tensor
                def _(pe):
                    pe.wait_ge(ready, 2)
                    pe.matmul(ps[:], R.tri_strict[:], lg2[:], start=True, stop=True).then_inc(pos, 1)


def stage_experts1(nc, R, A):
    USED = 32
    with Stage(nc, "experts1") as st:
        we = st.sb("we", [P, E1 * D])
        xs = st.sb("xs", [P, 2, 2 * P])
        ps = [[[st.ps(f"ps{s}_{k}_{h}", [P, 512]) for h in range(2)] for k in range(2)] for s in range(2)]
        wload, xload = st.sem("wload"), [st.sem("xload0"), st.sem("xload1")]
        prod, used = st.sem("prod"), st.sem("used")
        with nc.Block() as block:
            @block.sync
            def _(sp):
                sp.dma_start(we[:].rearrange("p (e f) -> p e f", e=E1), A["f1_we"].rearrange("e d f -> d e f")
                             ).then_inc(wload, 16)

                def body(u, s, j):
                    sp.wait_ge(prod, free_at(u))
                    sp.dma_start(xs[:, s, :], R.XT[:, ds(u * 2 * P, 2 * P)]).then_inc(xload[s], 16)
                two_slots(sp, NT // 2, body)

            @block.tensor
            def _(pe):
                pe.sem_inc(prod, 2)
                pe.wait_ge(wload, 16)

                def body(u, s, j):
                    pe.wait_ge(xload[s], j * 16 + 16)
                    pe.wait_ge(used, (u - 1) * 2 * E1 + USED)
                    for k in range(2):
                        for h in range(2):
                            m = pe.matmul(ps[s][k][h][:], xs[:, s, k * P:k * P + P], we[:, h * 512:h * 512 + 512],
                                          start=True, stop=True)
                    m.then_inc(prod, 1)
                two_slots(pe, NT // 2, body)

            @block.vector
            def _(dve):
                dve.sem_inc(used, USED)

                def body(u, s, j):
                    dve.wait_ge(prod, done_at(u))
                    for e in range(E1):
                        for k in range(2):
                            i = u * 2 + k
                            x = tile_of(R.X, i)
                            dve.wait_ge(used, u * 2 * E1 + 2 * e + k - 1 + USED)
                            dve.scalar_tensor_tensor(out=x, in0=ps[s][k][e // 4][:, (e % 4) * D:(e % 4) * D + D],
                                                     scalar=R.wt[:, ds(i * E1 + e, 1)], in1=x, op0=ALU.mult,
                                                     op1=ALU.add).then_inc(used, 1)
                two_slots(dve, NT // 2, body)


def stage_project2(nc, R, A, qkv, mean, rstd, nbias):
    N = 3 * NT
    with Stage(nc, "project2") as st:
        w3 = st.sb("w3", [P, 3, D])
        cT, xh, xT = (st.sb(n, [P, 2, GW]) for n in ("cT", "xh", "xT"))
        raw = st.sb("raw", [P, N, 6])
        t0, t1 = st.sb("t0", [P, N]), st.sb("t1", [P, N])
        psX = [st.ps(f"psX{k}", [P, 512]) for k in range(2)]
        psQ = [st.ps(f"psQ{k}", [P, 512]) for k in range(4)]
        wload, cload = st.sem("wload"), [st.sem("cload0"), st.sem("cload1")]
        normed, turned, xtm, prod, copied, statd, var_ready, rooted, chain = (
            st.sem(n) for n in ("normed", "turned", "xtm", "prod", "copied", "statd", "var_ready", "rooted", "chain"))
        with nc.Block() as block:
            @block.sync
            def _(sp):
                for n, a in enumerate((A["l2_wq"], A["l2_wk"], A["l2_wv"])):
                    sp.dma_start(w3[:, n, :], a).then_inc(wload, 16)

                def body(g, s, j):
                    sp.wait_ge(prod, g * 4 + 1)
                    sp.dma_start(cT[:, s, :], A["ctxT"][:, ds(g * GW, GW)]).then_inc(cload[s], 16)
                two_slots(sp, NG, body)

            @block.tensor
            def _(pe):
                pe.sem_inc(turned, 2)
                pe.sem_inc(prod, 5)
                pe.wait_ge(wload, 48)

                def front(g, s, j):
                    pe.wait_ge(xtm, free_at(g))
                    pe.wait_ge(normed, g + 1)
                    for k in range(4):
                        t = pe.transpose(psX[s][:, k * P:(k + 1) * P], xh[:, s, k * P:k * P + P], R.ident[:])
                    t.then_inc(turned, 1)

                def back(g, s, j):
                    pe.wait_ge(xtm, done_at(g))
                    pe.wait_ge(cload[s], j * 16 + 16)
                    for k in range(4):
                        cols = slice(k * P, k * P + P)
                        pe.wait_ge(copied, g * 4 + k + 1)
                        pe.matmul(psQ[k][:, 0:D], xT[:, s, cols], w3[:, 0, :], start=True, stop=True)
                        pe.matmul(psQ[k][:, D:3 * D], cT[:, s, cols], w3[:, 1:3, :].rearrange("p a d -> p (a d)"),
                                  start=True, stop=True).then_inc(prod, 1)
                pipelined(pe, NG, ((3, back), (1, front)))

            @block.scalar
            def _(act):
                act.sem_inc(xtm, 2)
                act.sem_inc(copied, 4)

                def front(g, s, j):
                    act.wait_ge(turned, done_at(g))
                    act.wait_ge(prod, g * 4 + 1)
                    act.activation(xT[:, s, :], psX[s][:], ACT.Copy).then_inc(xtm, 1)

                def back(g, s, j):
                    for k in range(4):
                        act.wait_ge(prod, g * 4 + k + 1 + 5)
                        act.activation(tile_of(qkv, g * 4 + k), psQ[k][:, 0:3 * D], ACT.Copy).then_inc(copied, 1)
                pipelined(act, NG, ((4, back), (2, front)))
                act.wait_ge(var_ready, 1)
                act.activation(t1[:], t0[:], ACT.Sqrt).then_inc(rooted, 1)

            @block.vector
            def _(dve):

                def front(g, s, j):
                    dve.wait_ge(turned, free_at(g))
                    for k in range(4):
                        i = g * 4 + k
                        n = dve.tensor_scalar(xh[:, s, k * P:k * P + P], tile_of(R.X, i), R.mean[:, ds(i, 1)],
                                              R.rstd[:, ds(i, 1)], ALU.subtract, ALU.mult)
                    n.then_inc(normed, 1)

                def back(g, s, j):
                    for k in range(4):
                        i = g * 4 + k
                        dve.wait_ge(copied, i + 1 + 4)
                        for n in range(3):
                            m = dve.bn_stats(tile_of(raw, i * 3 + n), qkv[:, ds(i, 1), n * D:n * D + D]
                                             .rearrange("p a d -> p (a d)"))
                        m.then_inc(statd, 1)
                pipelined(dve, NG, ((5, back), (0, front)))
                dve.wait_ge(statd, NT)
                link = Chain(dve, chain)
                m0, v0, m1, v1 = (raw[:, :, c] for c in (1, 2, 4, 5))
                link(dve.tensor_tensor(mean[:], m0, m1, ALU.add))
                link(dve.tensor_tensor(t0[:], m0, m1, ALU.subtract))
                link(dve.tensor_tensor(t1[:], v0, v1, ALU.add))
                link(dve.tensor_scalar(mean[:], mean[:], 0.5, None, ALU.mult))
                link(dve.tensor_tensor(t0[:], t0[:], t0[:], ALU.mult))
                link(dve.tensor_scalar(t1[:], t1[:], 1.0 / D, 1e-6, ALU.mult, ALU.add))
                dve.scalar_tensor_tensor(out=t0[:], in0=t0[:], scalar=0.25, in1=t1[:], op0=ALU.mult,
                                         op1=ALU.add).then_inc(var_ready, 1)
                dve.wait_ge(rooted, 1)
                link(dve.reciprocal(rstd[:], t1[:]))
                dve.scalar_tensor_tensor(out=nbias[:], in0=mean[:], scalar=-1.0, in1=rstd[:], op0=ALU.mult,
                                         op1=ALU.mult)


def stage_linear2(nc, R, A, qkv, rstd, nbias):
    W = D + H2
    EK = 1e-6
    with Stage(nc, "linear2") as st:
        dw = st.sb("dw", [P, C2, D])
        db = st.sb("db", [P, D])
        gm, bt = st.sb("gm", [P, D]), st.sb("bt", [P, D])
        em = st.sb("em", [P, NT])
        mask = st.sb("mask", [P, W])
        n3 = st.sb("n3", [P, 2, 3, D])
        feat = st.sb("feat", [P, 2, 2, D])
        va = st.sb("va", [P, 2, W])
        kvm = st.sb("kvm", [P, 2, 2, W])
        qT = st.sb("qT", [P, 2, P])
        den, rd = st.sb("den", [P, 2, H2]), st.sb("rd", [P, 2, H2])
        rdm = st.sb("rdm", [P, 2, 2, H2, 4])
        spread = st.sb("spread", [P, 2, C2, 2, H2, 4])
        psK = st.ps("psK", [P, 2, 512])
        psT, psA, psO = ([st.ps(f"{n}{k}", [P, 512]) for k in range(2)] for n in ("psT", "psA", "psO"))
        names = ("wload", "ready", "n3d", "scaled", "shifted", "featd", "chain", "kvd", "kvmd", "qt", "qm", "attd",
                 "dchain", "spreadd", "outd", "outm")
        (wload, ready, n3d, scaled, shifted, featd, chain, kvd, kvmd, qt, qm, attd, dchain, spreadd, outd,
         outm) = (st.sem(n) for n in names)
        with nc.Block() as block:
            @block.sync
            def _(sp):
                sp.dma_start(dw[:], A["l2_dw"]).then_inc(wload, 16)
                sp.dma_start(db[:], A["l2_db"].partition_broadcast(P)).then_inc(wload, 16)
                sp.dma_start(gm[:], A["l2_g"].partition_broadcast(P)).then_inc(wload, 16)
                sp.dma_start(bt[:], A["l2_b"].partition_broadcast(P)).then_inc(wload, 16)
                sp.dma_start(em[:], A["l2_mask"]).then_inc(wload, 16)

            @block.scalar
            def _(act):
                act.sem_inc(qm, 2)

                def norm(i, s, j):
                    act.wait_ge(featd, free_at(i))
                    for n in range(3):
                        m = act.activation(n3[:, s, n, :], qkv[:, ds(i, 1), n * D:n * D + D].rearrange(
                            "p a d -> p (a d)"), ACT.Identity, bias=nbias[:, ds(i * 3 + n, 1)],
                            scale=rstd[:, ds(i * 3 + n, 1)])
                    m.then_inc(n3d, 1)

                def move_q(i, s, j):
                    act.wait_ge(qt, done_at(i))
                    act.wait_ge(attd, free_at(i))
                    act.activation(qT[:, s, :], psT[s][:, 0:P], ACT.Copy).then_inc(qm, 1)
                pipelined(act, NT, ((3, move_q), (0, norm)))

            @block.gpsimd
            def _(gp):
                gp.wait_ge(wload, 80)

                def affine(i, s, j):
                    gp.wait_ge(n3d, i + 1)
                    gp.tensor_tensor(n3[:, s, :, :], n3[:, s, :, :], bcast_mid(gm[:], 3), ALU.mult).then_inc(scaled, 1)
                    gp.wait_ge(scaled, i + 1)
                    gp.tensor_tensor(n3[:, s, :, :], n3[:, s, :, :], bcast_mid(bt[:], 3), ALU.add).then_inc(shifted, 1)
                two_slots(gp, NT, affine)

            @block.tensor
            def _(pe):
                for z in (kvd, qt, attd, outd):
                    pe.sem_inc(z, 2)
                pe.wait_ge(wload, 80)

                def key_values(i, s, j):
                    pe.wait_ge(featd, done_at(i))
                    pe.wait_ge(kvmd, i + 1)
                    for b in range(2):
                        r = slice(64 * b, 64 * b + 64)
                        m = pe.matmul(psK[:, b, 0:W], feat[r, s, 1, :], va[r, s, :], start=True, stop=True)
                    m.then_inc(kvd, 1)
                    pe.wait_ge(qm, free_at(i))
                    pe.transpose(psT[s][:, 0:P], feat[:, s, 0, :], R.ident[:]).then_inc(qt, 1)

                def attend(i, s, j):
                    pe.wait_ge(kvmd, i + 2)
                    pe.wait_ge(qm, done_at(i))
                    pe.wait_ge(spreadd, free_at(i))
                    for b in range(2):
                        m = pe.matmul(psA[s][64 * b:64 * b + 64, 0:W], qT[:, s, 64 * b:64 * b + 64], kvm[:, s, b, :],
                                      start=True, stop=True)
                    m.then_inc(attd, 1)

                def dense(i, s, j):
                    pe.wait_ge(spreadd, done_at(i))
                    pe.wait_ge(outm, free_at(i))
                    for e in range(C2):
                        m = pe.matmul(psO[s][:, 0:D], spread[:, s, e, :, :, :].rearrange("p b h n -> p (b h n)"),
                                      dw[:, e, :], start=(e == 0), stop=(e == C2 - 1))
                    m.then_inc(outd, 1)
                pipelined(pe, NT, ((6, dense), (4, attend), (2, key_values)))

            @block.vector
            def _(dve):
                for z in (featd, spreadd, outm):
                    dve.sem_inc(z, 2)
                dve.sem_inc(kvmd, 1)
                dve.tensor_copy(mask[:, 0:D], R.bd8[:].rearrange("p a b -> p (a b)")).then_inc(ready, 1)
                dve.tensor_copy(mask[:, D:W], R.bd8[:, :, 0]).then_inc(ready, 1)
                for s in range(2):
                    dve.memset(va[:, s, D:W], 1.0).then_inc(ready, 1)
                dve.wait_ge(ready, 4)
                dve.wait_ge(wload, 80)

                def features(i, s, j):
                    dve.wait_ge(shifted, i + 1)
                    dve.wait_ge(kvd, free_at(i))
                    dve.wait_ge(qt, free_at(i))
                    dve.tensor_scalar(feat[:, s, :, :], n3[:, s, 0:2, :], 0.0, EK, ALU.max, ALU.add).then_inc(chain, 1)
                    dve.tensor_scalar(va[:, s, 0:D], n3[:, s, 2, :], em[:, ds(i, 1)], None, ALU.mult)

                def mask_keys(i, s, j):
                    dve.wait_ge(chain, i + 1)
                    dve.tensor_scalar(feat[:, s, 1, :], feat[:, s, 1, :], em[:, ds(i, 1)], None,
                                      ALU.mult).then_inc(featd, 1)

                def heads_only(i, s, j):
                    dve.wait_ge(kvd, done_at(i))
                    dve.wait_ge(attd, free_at(i))
                    dve.tensor_tensor(kvm[:, s, :, :], psK[:, :, 0:W], bcast_mid(mask[:], 2),
                                      ALU.mult).then_inc(kvmd, 1)

                def denominator(i, s, j):
                    dve.wait_ge(attd, done_at(i))
                    dve.tensor_scalar(den[:, s, :], psA[s][:, D:W], EK, None, ALU.add).then_inc(dchain, 1)

                def inverse(i, s, j):
                    dve.wait_ge(dchain, i * 3 + 1)
                    dve.reciprocal(rd[:, s, :], den[:, s, :]).then_inc(dchain, 1)

                def inverse_spread(i, s, j):
                    dve.wait_ge(dchain, i * 3 + 2)
                    dve.tensor_tensor(rdm[:, s, :, :, :], rd[:, s, :].rearrange("p (b h n) -> p b h n", b=1, n=1)
                                      .broadcast_to([P, 2, H2, 4]),
                                      R.bd16[:].rearrange("p (b h n) -> p b h n", b=2, h=1)
                                      .broadcast_to([P, 2, H2, 4]), ALU.mult).then_inc(dchain, 1)

                def spreads(i, s, j):
                    dve.wait_ge(dchain, i * 3 + 3)
                    dve.wait_ge(outd, free_at(i))
                    for b in range(2):
                        m = dve.tensor_tensor(spread[:, s, :, b, :, :],
                                              psA[s][:, 0:D].rearrange("p (h e a) -> p e h a", h=H2, a=1)
                                              .broadcast_to([P, C2, H2, 4]),
                                              rdm[:, s, b, :, :].rearrange("p (x h) n -> p x h n", x=1)
                                              .broadcast_to([P, C2, H2, 4]), ALU.mult)
                    m.then_inc(spreadd, 1)

                def move_out(i, s, j):
                    dve.wait_ge(outd, done_at(i))
                    dve.tensor_tensor(qkv[:, ds(i, 1), 0:D].rearrange("p a d -> p (a d)"), psO[s][:, 0:D], db[:],
                                      ALU.add).then_inc(outm, 1)

                def out_stats(i, s, j):
                    dve.wait_ge(outm, done_at(i))
                    dve.bn_stats(tile_of(R.stats, i), qkv[:, ds(i, 1), 0:D].rearrange("p a d -> p (a d)"))
                pipelined(dve, NT, ((5, denominator), (3, heads_only), (5, inverse), (7, move_out),
                                     (5, inverse_spread), (1, features), (5, spreads), (7, out_stats), (1, mask_keys)))


def stage_experts2(nc, R, A):
    NC, PARTS = I2 // P, 3
    ROWS = PARTS * E2
    HID = MASKED = 5
    with Stage(nc, "experts2") as st:
        w1_high, w1_low = (st.sb(n, [P, E2, I2]) for n in ("w1_high", "w1_low"))
        x_high, x_low = st.sb("x_high", [P, 2, GW]), st.sb("x_low", [P, 2, GW])
        b1 = st.sb("b1", [ROWS, I2])
        part_bf = st.sb("part_bf", [ROWS, I2], BF16)
        rest, total = st.sb("rest", [ROWS, I2]), st.sb("total", [ROWS, I2])
        own = st.sb("own", [ROWS, PARTS])
        b1_parts = st.sb("b1_parts", [ROWS, I2], BF16)
        pick = st.sb("pick", [E2, E2, P], BF16)
        wo = st.sb("wo", [P, NC, D])
        bo = st.sb("bo", [1, D])
        hots = st.sb("hots", [P, 2, 4, PARTS, E2], BF16)
        hotT = st.sb("hotT", [ROWS, 2, GW], BF16)
        xmT = st.sb("xmT", [P, 2, 2, E2, GW])
        hT = st.sb("hT", [P, 2, NC, GW])
        w1 = hT[:, 0, :, :]
        psM, psH, psY = ([st.ps(f"{n}{k}", [P, 512]) for k in range(2)] for n in ("psM", "psH", "psY"))
        psB = st.ps("psB", [P, 512])
        (high, x_split, wload, chain, picked, normed, hotd, hotm, spread, masked, hid, act_d, yd, added) = (
            st.sem(n) for n in ("high", "x_split", "wload", "chain", "picked", "normed", "hotd", "hotm", "spread", "masked", "hid",
                                "act_d", "yd", "added"))
        with nc.Block() as block:
            @block.sync
            def _(sp):
                for n in range(PARTS):
                    sp.dma_start(b1[n * E2:n * E2 + E2, :], A["f2_b1"]).then_inc(wload, 16)
                sp.dma_start(w1, A["f2_w1"].rearrange("e d i -> d e i")).then_inc(wload, 16)
                sp.dma_start(wo[:], A["f2_wo"].rearrange("(c p) d -> p c d", p=P)).then_inc(wload, 16)
                sp.dma_start(bo[:], A["f2_bo"]).then_inc(wload, 16)

            @block.vector
            def _(dve):
                link = Chain(dve, chain)
                dve.tensor_copy(pick[:], bcast_in(R.ident_bf[0:E2, 0:E2], P)).then_inc(picked, 1)
                for n in range(PARTS):
                    link(dve.tensor_reduce(own[:, n:n + 1], R.ident[0:ROWS, n * E2:n * E2 + E2], AX_X, ALU.add))
                dve.wait_ge(wload, 96)
                for n in range(PARTS):
                    left = b1 if n == 0 else rest
                    link(dve.tensor_copy(part_bf[:], left[:]))
                    if n < PARTS - 1:
                        link(dve.tensor_tensor(rest[:], left[:], part_bf[:], ALU.subtract))
                    if n == 0:
                        link(dve.tensor_scalar(total[:], part_bf[:], own[:, 0:1], None, ALU.mult))
                    else:
                        link(dve.scalar_tensor_tensor(out=total[:], in0=part_bf[:], scalar=own[:, n:n + 1],
                                                      in1=total[:], op0=ALU.mult, op1=ALU.add))
                dve.tensor_copy(b1_parts[:], total[:]).then_inc(picked, 1)
                for e in range(E2):
                    link(take_high(dve, w1_high[:, e, :], w1[:, e, :]))
                    m = take_low(dve, w1_low[:, e, :], w1[:, e, :], w1_high[:, e, :])
                m.then_inc(picked, 1)
                dve.sem_inc(masked, MASKED)
                dve.sem_inc(added, 2)

                def normalise(g, s, j):
                    for k in range(4):
                        i = g * 4 + k
                        dve.tensor_scalar(tile_of(R.Y, i), tile_of(R.X, i), R.mean[:, ds(i, 1)],
                                          R.rstd[:, ds(i, 1)], ALU.subtract, ALU.mult)
                    dve.wait_ge(hotd, free_at(g))
                    dve.tensor_copy(hots[:, s, :, :, :], R.wt[:, ds(g * 4 * E2, 4 * E2)].rearrange(
                        "p (k a e) -> p k a e", k=4, a=1).broadcast_to([P, 4, PARTS, E2])).then_inc(normed, 1)

                def split(g, s, j):
                    cols = ds(g * GW, GW)
                    dve.wait_ge(masked, g * E2 - E2 + MASKED)
                    take_high(dve, x_high[:, s, :], R.XT[:, cols]).then_inc(high, 1)
                    dve.wait_ge(high, g + 1)
                    take_low(dve, x_low[:, s, :], R.XT[:, cols], x_high[:, s, :]).then_inc(x_split, 1)

                def mask(e):
                    def step(g, s, j):
                        dve.wait_ge(spread, g * E2 + e + 1)
                        if e == 0:
                            dve.wait_ge(hid, g * NC - NC + HID)
                            dve.wait_ge(x_split, g + 1)
                        dve.tensor_tensor(xmT[:, s, 0, e, :].bitcast(F32R), psM[e % 2][:], x_high[:, s, :], ALU.mult)
                        dve.tensor_tensor(xmT[:, s, 1, e, :].bitcast(F32R), psM[e % 2][:], x_low[:, s, :],
                                          ALU.mult).then_inc(masked, 1)
                    return step

                def add(g, s, j):
                    dve.wait_ge(yd, done_at(g))
                    dve.wait_ge(normed, g + 1)
                    y = tiles_of(R.Y, g * 4, 4)
                    dve.tensor_tensor(y, psY[s][:].rearrange("p (k d) -> p k d", k=4), y, ALU.add).then_inc(added, 1)
                    dve.wait_ge(added, done_at(g))
                    for k in range(4):
                        dve.bn_stats(tile_of(R.stats, g * 4 + k), tile_of(R.Y, g * 4 + k))
                pipelined(dve, NG, ((1, split), *((2, mask(e)) for e in range(E2)), (5, add), (0, normalise)))

            @block.tensor
            def _(pe):
                for q in (hotd, yd):
                    pe.sem_inc(q, 2)
                pe.sem_inc(hid, HID)
                pe.wait_ge(wload, 96)
                pe.wait_ge(picked, 3)

                def turn_hot(g, s, j):
                    pe.wait_ge(normed, g + 1)
                    pe.wait_ge(hotm, g + 2)
                    for k in range(4):
                        m = pe.matmul(psB[0:ROWS, k * P:k * P + P], hots[:, s, k, :, :].rearrange("p a e -> p (a e)"),
                                      R.ident_bf[:], start=True, stop=True)
                    m.then_inc(hotd, 1)

                def spread_hot(e):
                    def step(g, s, j):
                        if e == 0:
                            pe.wait_ge(hotm, done_at(g))
                        pe.wait_ge(masked, g * E2 + e - 1 + MASKED)
                        pe.matmul(psM[e % 2][:], pick[:, e, :], hotT[0:E2, s, :], start=True,
                                  stop=True).then_inc(spread, 1)
                    return step

                def hidden(c):
                    def step(g, s, j):
                        if c == 0:
                            pe.wait_ge(masked, g * E2 + E2 + MASKED)
                        pe.wait_ge(act_d, free_at(g * NC + c))
                        cols = slice(c * P, c * P + P)
                        for e in range(E2):
                            matmul_split(pe, psH[c % 2][:], [w[:, e, cols] for w in (w1_high, w1_low)],
                                         [xmT[:, s, k, e, :] for k in range(2)], start=(e == 0), stop=False)
                        pe.matmul(psH[c % 2][:], b1_parts[:, cols], hotT[:, s, :], start=False,
                                  stop=True).then_inc(hid, 1)
                    return step

                def output(g, s, j):
                    pe.wait_ge(act_d, done_at(g * NC + NC - 1))
                    pe.wait_ge(added, free_at(g))
                    for k in range(4):
                        y = psY[s][:, k * P:k * P + P]
                        for c in range(NC):
                            pe.matmul(y, hT[:, s, c, k * P:k * P + P], wo[:, c, :], start=(c == 0), stop=False)
                        m = pe.matmul(y, R.ones[0:1, 0:P], bo[:], start=False, stop=True)
                    m.then_inc(yd, 1)
                pipelined(pe, NG, ((3, hidden(0)), (2, spread_hot(0)), (2, spread_hot(1)), (3, hidden(1)),
                                   (2, spread_hot(2)), (2, spread_hot(3)), (3, hidden(2)), (1, turn_hot),
                                   (3, hidden(3)), (4, output)))

            @block.scalar
            def _(act):
                for q in (hotm, act_d):
                    act.sem_inc(q, 2)

                def move_hot(g, s, j):
                    act.wait_ge(hotd, done_at(g))
                    act.wait_ge(hid, g * NC - NC + HID)
                    act.activation(hotT[:, s, :], psB[0:ROWS, :], ACT.Copy).then_inc(hotm, 1)

                def gelu(g, s, j):
                    act.wait_ge(yd, free_at(g))
                    for c in range(NC):
                        act.wait_ge(hid, g * NC + c + 1 + HID)
                        act.activation(hT[:, s, c, :], psH[c % 2][:], ACT.Gelu).then_inc(act_d, 1)
                pipelined(act, NG, ((3, gelu), (1, move_hot)))


def stage_norm_add(nc, R, name, gamma, beta, Y):
    with Stage(nc, name) as st:
        gm, bt = st.sb("gm", [P, D]), st.sb("bt", [P, D])
        loaded, shifted, scaled = st.sem("loaded"), st.sem("shifted"), st.sem("scaled")
        with nc.Block() as block:
            @block.sync
            def _(sp):
                sp.dma_start(gm[:], gamma.partition_broadcast(P)).then_inc(loaded, 16)
                sp.dma_start(bt[:], beta.partition_broadcast(P)).then_inc(loaded, 16)

            @block.gpsimd
            def _(gp):
                gp.wait_ge(loaded, 32)
                with gp.Fori(0, NG) as g:
                    x = tiles_of(R.X, g * 4, 4)
                    gp.tensor_tensor(x, x, bcast_mid(bt[:], 4), ALU.add).then_inc(shifted, 1)

            @block.vector
            def _(dve):
                dve.wait_ge(loaded, 32)
                with dve.Fori(0, NG) as g:
                    for k in range(4):
                        i = g * 4 + k
                        y = tile_of(Y, i)
                        dve.scalar_tensor_tensor(out=y, in0=y, scalar=R.mean[:, ds(i, 1)], in1=gm[:],
                                                 op0=ALU.subtract, op1=ALU.mult).then_inc(scaled, 1)
                    dve.wait_ge(shifted, g + 1)
                    for k in range(4):
                        i = g * 4 + k
                        dve.wait_ge(scaled, i + 1)
                        dve.scalar_tensor_tensor(out=tile_of(R.X, i), in0=tile_of(Y, i), scalar=R.rstd[:, ds(i, 1)],
                                                 in1=tile_of(R.X, i), op0=ALU.mult, op1=ALU.add)


def stage_bilinear3(nc, R, A):
    with Stage(nc, "bilinear3") as st:
        wq = st.sb("wq", [P, D])
        qT = st.sb("qT", [P, 2, GW])
        gg = st.sb("gg", [P, 2, 8, D])
        psQ, psY = ([st.ps(f"{n}{k}", [P, 512]) for k in range(2)] for n in ("psQ", "psY"))
        wload, gload = st.sem("wload"), [st.sem("gload0"), st.sem("gload1")]
        qd, qm, yd, added = (st.sem(n) for n in ("qd", "qm", "yd", "added"))
        with nc.Block() as block:
            @block.sync
            def _(sp):
                sp.dma_start(wq[:], A["l3_wqT"]).then_inc(wload, 16)

                def body(g, s, j):
                    sp.wait_ge(yd, free_at(g))
                    sp.dma_start(gg[:, s, :, :], R.G3[ds(g * 8 + 2, 8), :, :].rearrange("b p d -> p b d")
                                 ).then_inc(gload[s], 16)
                two_slots(sp, NG, body)

            @block.tensor
            def _(pe):
                for z in (qd, yd):
                    pe.sem_inc(z, 2)
                pe.wait_ge(wload, 16)

                def queries(g, s, j):
                    pe.wait_ge(qm, free_at(g))
                    pe.matmul(psQ[s][:], wq[:], R.XT[:, ds(g * GW, GW)], start=True, stop=True).then_inc(qd, 1)

                def outputs(g, s, j):
                    pe.wait_ge(gload[s], j * 16 + 16)
                    pe.wait_ge(added, free_at(g))
                    pe.wait_ge(qm, done_at(g))
                    for n in range(8):
                        k, b = n // 2, n % 2
                        m = pe.matmul(psY[s][64 * b:64 * b + 64, k * P:k * P + P], qT[:, s, n * S:n * S + S],
                                      gg[:, s, n, :], start=True, stop=True)
                    m.then_inc(yd, 1)
                pipelined(pe, NG, ((2, outputs), (0, queries)))

            @block.scalar
            def _(act):
                act.sem_inc(qm, 2)

                def move(g, s, j):
                    act.wait_ge(qd, done_at(g))
                    act.wait_ge(yd, free_at(g))
                    act.activation(qT[:, s, :], psQ[s][:], ACT.Copy).then_inc(qm, 1)
                pipelined(act, NG, ((1, move),))

            @block.vector
            def _(dve):
                dve.sem_inc(added, 2)

                def add(g, s, j):
                    dve.wait_ge(yd, done_at(g))
                    x = tiles_of(R.X, g * 4, 4)
                    dve.tensor_tensor(x, psY[s][:].rearrange("p (k d) -> p k d", k=4), x, ALU.add).then_inc(added, 1)
                    dve.wait_ge(added, done_at(g))
                    for k in range(4):
                        dve.bn_stats(tile_of(R.stats, g * 4 + k), tile_of(R.X, g * 4 + k))
                pipelined(dve, NG, ((3, add),))


def stage_experts3(nc, R, A):
    NC = I3 // P
    HID = 33
    with Stage(nc, "experts3") as st:
        fc, fc_high, fc_low = (st.sb(n, [P, E3, I3]) for n in ("fc", "fc_high", "fc_low"))
        x_high, x_low = st.sb("x_high", [P, 2, GW]), st.sb("x_low", [P, 2, GW])
        proj = st.sb("proj", [P, E3, NC, D])
        hT = st.sb("hT", [P, 2, NC, GW])
        psH = [st.ps(f"psH{k}", [P, 512]) for k in range(4)]
        psY = [st.ps(f"psY{k}", [P, 512]) for k in range(2)]
        wload, hid, gelud, yd, used, high, w_split, x_split = (
            st.sem(n) for n in ("wload", "hid", "gelud", "yd", "used", "high", "w_split", "x_split"))
        with nc.Block() as block:
            @block.sync
            def _(sp):
                sp.dma_start(fc[:], A["f3_fc"].rearrange("e d i -> d e i")).then_inc(wload, 16)
                sp.dma_start(proj[:], A["f3_proj"].rearrange("e (c p) d -> p e c d", p=P)).then_inc(wload, 16)

            @block.tensor
            def _(pe):
                pe.sem_inc(yd, 2)
                pe.sem_inc(hid, HID)
                pe.wait_ge(wload, 32)
                pe.wait_ge(w_split, E3)

                def hidden(g, s, e):
                    pe.wait_ge(x_split, g + 1)
                    for c in range(NC):
                        pe.wait_ge(gelud, (g * E3 + e) * NC + c + 1)
                        matmul_split(pe, psH[c][:], [w[:, e, c * P:c * P + P] for w in (fc_high, fc_low)],
                                     [x[:, s, :] for x in (x_high, x_low)]).then_inc(hid, 1)

                def project(g, e):
                    pe.wait_ge(gelud, (g * E3 + e) * NC + NC + 4)
                    pe.wait_ge(used, (g * E3 + e) * 4 + 4)
                    for k in range(4):
                        for c in range(NC):
                            m = pe.matmul(psY[e % 2][:, k * P:k * P + P], hT[:, e % 2, c, k * P:k * P + P],
                                          proj[:, e, c, :], start=(c == 0), stop=(c == NC - 1))
                    m.then_inc(yd, 1)

                def group(g, s, last=False):
                    for e in range(E3):
                        if e < E3 - 1:
                            hidden(g, s, e + 1)
                        elif not last:
                            hidden(g + 1, 1 - s, 0)
                        project(g, e)
                hidden(0, 0, 0)
                with pe.Fori(0, NG // 2 - 1) as j:
                    group(2 * j, 0)
                    group(2 * j + 1, 1)
                group(NG - 2, 0)
                group(NG - 1, 1, last=True)

            @block.scalar
            def _(act):
                act.sem_inc(gelud, 4)
                with act.Fori(0, NG) as g:
                    for e in range(E3):
                        act.wait_ge(yd, g * E3 + e + 1)
                        for c in range(NC):
                            act.wait_ge(hid, (g * E3 + e) * NC + c + 1 + HID)
                            act.activation(hT[:, e % 2, c, :], psH[c][:], ACT.Gelu).then_inc(gelud, 1)

            @block.vector
            def _(dve):
                dve.sem_inc(used, 8)
                dve.wait_ge(wload, 32)
                for e in range(E3):
                    take_high(dve, fc_high[:, e, :], fc[:, e, :]).then_inc(high, 1)
                for e in range(E3):
                    dve.wait_ge(high, e + 1)
                    take_low(dve, fc_low[:, e, :], fc[:, e, :], fc_high[:, e, :]).then_inc(w_split, 1)

                def split_x(g, s, j):
                    x = R.XT[:, ds(g * GW, GW)]
                    dve.wait_ge(hid, (g - 1) * E3 * NC + HID)
                    take_high(dve, x_high[:, s, :], x).then_inc(high, 1)
                    dve.wait_ge(high, g + 1 + E3)
                    take_low(dve, x_low[:, s, :], x, x_high[:, s, :]).then_inc(x_split, 1)

                def combine(g, s, j):
                    for e in range(E3):
                        dve.wait_ge(yd, g * E3 + e + 1 + 2)
                        for k in range(4):
                            i = g * 4 + k
                            dve.wait_ge(used, (g * E3 + e) * 4 + k + 1 + 4)
                            x = tile_of(R.X, i)
                            dve.scalar_tensor_tensor(out=x, in0=psY[e % 2][:, k * P:k * P + P],
                                                     scalar=R.wt[:, ds(i * E3 + e, 1)], in1=x, op0=ALU.mult,
                                                     op1=ALU.add).then_inc(used, 1)
                skewed(dve, NG, split_x, combine)


def program(nc, A, out):
    ctx = ExitStack()
    with ctx:
        def sb(name, shape, dt=F32):
            return ctx.enter_context(nc.sbuf_tensor(name, shape, dt))

        R = Resident()
        R.X = sb("X", [P, NT, D])
        R.ident, R.same2, R.tri_incl, R.tri_strict = (
            sb(n, [P, P]) for n in ("ident", "same2", "tri_incl", "tri_strict"))
        R.ident_bf, R.causal = sb("ident_bf", [P, P], BF16), sb("causal", [P, 512], BF16)
        R.delta, R.ones = sb("delta", [P, S]), sb("ones", [P, 512])
        R.bd16, R.bd16q = sb("bd16", [P, H0]), sb("bd16q", [P, H0])
        R.bd8 = sb("bd8", [P, H2, C2])
        R.vmask = sb("vmask", [P, 4, 2, C0])
        R.vmask128 = R.vmask[:].rearrange("p a b c -> p (a b c)")
        R.stats, R.t0, R.t1 = sb("stats", [P, NT, 6]), sb("t0", [P, NT]), sb("t1", [P, NT])
        R.mean, R.rstd = sb("mean", [P, NT]), sb("rstd", [P, NT])
        R.cs, R.g = sb("cs", [P, NT * H0]), sb("g", [P, NT, H0])
        R.rowmax, R.rowsum = sb("rowmax", [P, NT, H0]), sb("rowsum", [P, NT, H0])
        R.G3 = nc.dram_tensor("G3", (B + 2, P, D), F32, kind="Internal").ap()
        R.khop = nc.dram_tensor("khop", (B, S, H0 * S), F32, kind="Internal").ap()

        def finish():
            with Stage(nc, "store") as st:
                stored = st.sem("stored")
                with nc.Block() as block:
                    @block.sync
                    def _(sp):
                        sp.dma_start(out.rearrange("(i p) d -> p i d", p=P), R.X[:]).then_inc(stored, 16)
                        sp.wait_ge(stored, 16)

        stage_setup(nc, R, A)
        with nc.sbuf_tensor("XT", [P, TOK], F32) as R.XT:
            stage_stats(nc, R, "stats0", collected=True)
            with nc.sbuf_tensor("rpe_rows", [P, S // 2, D], F32) as rows:
                with nc.sbuf_tensor("G", [P, NT * 2 * H0], F32) as R.G:
                    w = [A["gate_wT"][n * P:(n + 1) * P, :] for n in range(3)]
                    stage_norm_T(nc, R, "norm0", w[0], 2 * H0, R.G, A["ctxT"], w[1:], A["gate_b"],
                                 gather=(A["rpe"], A["hopsT"], rows))
                    stage_gates(nc, R, A)
                stage_hop(nc, R, rows)
            with nc.sbuf_tensor("Y", [P, NT, D], F32) as R.Y:
                stage_mlstm(nc, R, A)
                stage_headnorm(nc, R, A)
            stage_stats(nc, R, "stats1")
            stage_norm_T(nc, R, "norm1")
            stage_scan(nc, R, A)
        R.lg, R.wt = sb("lg", [P, 512]), sb("wt", [P, 512])
        stage_stats(nc, R, "stats2", collected=True)
        stage_attend(nc, R, A)
        with nc.sbuf_tensor("XT3", [P, TOK], F32) as R.XT:
            stage_stats(nc, R, "stats3", collected=True)
            stage_norm_T(nc, R, "norm3", A["f1_wrT"], E1, R.lg)
            stage_route(nc, R, "route3", E1, True, CAP)
            stage_experts1(nc, R, A)
        stage_stats(nc, R, "stats4")
        with (nc.sbuf_tensor("qkv", [P, NT, 3 * D], F32) as qkv, nc.sbuf_tensor("mean3", [P, 3 * NT], F32) as mean3,
              nc.sbuf_tensor("rstd3", [P, 3 * NT], F32) as rstd3, nc.sbuf_tensor("nbias3", [P, 3 * NT], F32) as nbias3):
            stage_project2(nc, R, A, qkv, mean3, rstd3, nbias3)
            stage_linear2(nc, R, A, qkv, rstd3, nbias3)
            y = qkv[:, :, 0:D]
            stage_stats(nc, R, "stats4y", eps=1e-6, collected=True)
            stage_norm_add(nc, R, "add4", A["l2_g"], A["l2_b"], y)
        R.XT = sb("XT5", [P, TOK])
        stage_stats(nc, R, "stats5")
        stage_norm_T(nc, R, "norm5", A["f2_wr"], E2, R.lg)
        stage_route(nc, R, "route5", E2, False, 0)
        with nc.sbuf_tensor("Y2", [P, NT, D], F32) as R.Y:
            stage_experts2(nc, R, A)
            stage_stats(nc, R, "stats5y", eps=1e-12, collected=True)
            stage_norm_add(nc, R, "add5", A["f2_g"], A["f2_b"], R.Y)
        stage_stats(nc, R, "stats6")
        stage_norm_T(nc, R, "norm6")
        stage_bilinear3(nc, R, A)
        stage_stats(nc, R, "stats7", collected=True)
        stage_norm_T(nc, R, "norm7", A["f3_gate"], E3, R.lg)
        stage_route(nc, R, "route7", E3, True, 0)
        stage_experts3(nc, R, A)
        finish()


def laid_out(a):
    import numpy as np

    f = lambda n: np.asarray(a[n])
    c = np.ascontiguousarray
    ctx = f("ctx_1024").reshape(TOK, D)
    return {
        "x": f("x").reshape(TOK, D), "ctx": ctx, "ctxT": c(ctx.T),
        "hopsT": c(f("itok_SxS2_0_2016").reshape(S // 2, 2 * S).T), "rpe": f("L0_xattn_rpe"),
        "gate_wT": c(np.concatenate([f("L0_xattn_igate_w"), f("L0_xattn_fgate_w")]).T),
        "gate_b": np.concatenate([f("L0_xattn_igate_b"), f("L0_xattn_fgate_b")]),
        "ln_w": f("L0_xattn_ln_w"), "ln_b": f("L0_xattn_ln_b"),
        "lstm_wT": c(np.stack([f(f"L0_ffn_w{g}").T for g in "fico"])),
        "lstm_uT": c(np.stack([f(f"L0_ffn_u{g}").T for g in "fico"])),
        "lstm_bT": c(np.stack([f(f"L0_ffn_b{g}") for g in "fico"]).T),
        "in_c": f("L0_ffn_in_c"),
        "a1_wq": f("L1_xattn_Wq").reshape(D, H1 * C1), "a1_wk": f("L1_xattn_Wk").reshape(D, H1 * C1),
        "a1_wv": f("L1_xattn_Wv").reshape(D, H1 * C1),
        "a1_wo": c(f("L1_xattn_Wo").reshape(HP1, 2 * C1, D).transpose(1, 0, 2)),
        "a1_bqT": c(f("L1_xattn_bq").reshape(HP1, 2 * C1).T), "a1_bkT": c(f("L1_xattn_bk").reshape(HP1, 2 * C1).T),
        "a1_bvT": c(f("L1_xattn_bv").reshape(HP1, 2 * C1).T), "a1_bo": f("L1_xattn_bo")[None],
        "f1_wrT": c(f("L1_ffn_Wr").T), "f1_we": f("L1_ffn_We"),
        "l2_wq": f("L2_xattn_wq"), "l2_wk": f("L2_xattn_wk"), "l2_wv": f("L2_xattn_wv"),
        "l2_g": f("L2_xattn_ln_gamma"), "l2_b": f("L2_xattn_ln_beta"), "l2_dw": np.tile(f("L2_xattn_dense_w").reshape(H2, C2, D), (P // H2, 1, 1)),
        "f2_wr": f("L2_ffn_W_router"), "f2_w1": f("L2_ffn_W1"), "f2_b1": f("L2_ffn_b1"), "f2_wo": f("L2_ffn_Wo"),
        "f2_bo": f("L2_ffn_bo")[None], "f2_g": f("L2_ffn_ln_gamma"), "f2_b": f("L2_ffn_ln_beta"),
        "l3_wqT": c(f("L3_xattn_Wq").T), "l3_wkT": c(f("L3_xattn_Wk").T), "l3_wvT": c(f("L3_xattn_Wv").T),
        "l3_woT": c(f("L3_xattn_Wo").T), "f3_gate": f("L3_ffn_gate_w"), "f3_fc": f("L3_ffn_fc_w"),
        "f3_proj": f("L3_ffn_proj_w"),
        "l2_db": f("L2_xattn_dense_b"), "l2_mask": c(f("mask_BxS2_ff1").reshape(NT, P).T),
    }


def build(nc, arrays):
    A = {
        name: nc.dram_tensor(f"in_{name}", a.shape, mybir.dt.from_np(a.dtype), kind="ExternalInput").ap()
        for name, a in arrays.items()}
    out = nc.dram_tensor("out", (TOK, D), F32, kind="ExternalOutput").ap()
    program(nc, A, out)


def kernel(**inputs):
    import concourse.bacc as bacc
    from concourse.bass_utils import run_bass_kernel_spmd

    arrays = laid_out(inputs)
    nc = bacc.Bacc("TRN2", target_bir_lowering=False, num_devices=1)
    build(nc, arrays)
    got = run_bass_kernel_spmd(nc, [{f"in_{n}": a for n, a in arrays.items()}], core_ids=[0])
    return got.results[0]["out"].reshape(B, S, D)
```
